# Optimizing a Trainium2 kernel written in Bass

```python
import numpy as np
import jax
import jax.numpy as jnp

def _softmax(x, axis=-1):
    return jax.nn.softmax(x, axis=axis)

def _gelu(x):
    return jax.nn.gelu(x, approximate=True)

def _silu(x):
    return jax.nn.silu(x)

def _sigmoid(x):
    return jax.nn.sigmoid(x)

def _layernorm(x, axis=-1, eps=1e-05):
    m = jnp.mean(x, axis=axis, keepdims=True)
    v = jnp.var(x, axis=axis, keepdims=True)
    return (x - m) / jnp.sqrt(v + eps)

def _scatter_add(tgt, idx, src, axis=0):
    return tgt.at[idx].add(src)

def _segment_sum(src, seg, n):
    return jax.ops.segment_sum(src, seg, n)
kernel_name = 'mk_decoder_postln_d2_seqx_r8_ea5e25'

def setup_inputs(seed: int=0):
    np.random.seed(seed)
    _w = jnp.asarray

    def _rec_inputs():
        import jax
        import jax.numpy as jnp
        _rk = jax.random.key(seed)
        x = -0.0002928 + 1 * jax.random.normal(jax.random.fold_in(_rk, 1), (32, 56, 128), jnp.float32)
        _lenS = 56 - jax.random.randint(jax.random.fold_in(_rk, 7), (32,), 0, max(1, 56 // 4) + 1, jnp.int32)
        _lenS2 = 1500 - jax.random.randint(jax.random.fold_in(_rk, 8), (32,), 0, max(1, 1500 // 4) + 1, jnp.int32)
        _ctx_1024P = jax.random.normal(jax.random.fold_in(_rk, 11), (32, 16, 128), jnp.float32)
        _ctx_1024c = jax.random.dirichlet(jax.random.fold_in(_rk, 511), 0.3 * jnp.ones((16,), jnp.float32), (32, 1500))
        _ctx_1024t = jnp.einsum('bsk,bkd->bsd', _ctx_1024c, _ctx_1024P)
        _ctx_1024t = _ctx_1024t * jax.lax.rsqrt(jnp.mean(jnp.square(_ctx_1024t)) + 1e-12) * 0.953939
        ctx_1024 = -1.39393e-06 + 0.999914 * (_ctx_1024t + 0.3 * jax.random.normal(jax.random.fold_in(_rk, 611), (32, 1500, 128), jnp.float32))
        _validS = jnp.arange(56)[None, :] < _lenS[:, None]
        _validS2 = jnp.arange(1500)[None, :] < _lenS2[:, None]
        _causal = jnp.tril(jnp.ones((56, 56), dtype=bool))
        mask_BxSxS2_bk1 = jnp.broadcast_to(_validS2[:, None, :], (32, 56, 1500))
        return (x, ctx_1024, mask_BxSxS2_bk1)
    x, ctx_1024, mask_BxSxS2_bk1 = _rec_inputs()

    def _L0_attn_setup():
        import jax, jax.numpy as jnp
        import numpy as np
        D_MODEL = 128
        NUM_HEADS = 16
        D_K = D_MODEL // NUM_HEADS
        THETA = 10000.0
        NEG_INF = -1000000000.0

        def _rope(x, positions):
            half = D_K // 2
            inv_freq = 1.0 / THETA ** (jnp.arange(0, D_K, 2, dtype=jnp.float32) / D_K)
            angles = positions.astype(jnp.float32)[:, None] * inv_freq
            cos, sin = (jnp.cos(angles), jnp.sin(angles))
            xe = x[..., 0::2]
            xo = x[..., 1::2]
            re = xe * cos - xo * sin
            ro = xe * sin + xo * cos
            return jnp.stack([re, ro], axis=-1).reshape(x.shape).astype(x.dtype)
        key = jax.random.key(seed)
        ks = jax.random.split(key, 5)
        sigma = np.sqrt(2.0 / (D_MODEL + D_MODEL))
        x = jax.random.normal(ks[0], (2, 256, D_MODEL), dtype=jnp.float32)
        mk = lambda k: (sigma * jax.random.normal(k, (D_MODEL, D_MODEL))).astype(jnp.float32)
        return {'x': x, 'Wq': mk(ks[1]), 'bq': jnp.zeros((D_MODEL,), jnp.float32), 'Wk': mk(ks[2]), 'bk': jnp.zeros((D_MODEL,), jnp.float32), 'Wv': mk(ks[3]), 'bv': jnp.zeros((D_MODEL,), jnp.float32), 'Wo': mk(ks[4]), 'bo': jnp.zeros((D_MODEL,), jnp.float32), 'token_positions': jnp.arange(256, dtype=jnp.int64) if jax.config.jax_enable_x64 else jnp.arange(256, dtype=jnp.int32)}
    _L0_attn_all = _L0_attn_setup()
    _L0_attn_in = {k: v for k, v in _L0_attn_all.items() if k in ('Wq', 'bq', 'Wk', 'bk', 'Wv', 'bv', 'Wo', 'bo', 'token_positions')}
    del _L0_attn_all

    def _L0_xattn_setup():
        import jax, jax.numpy as jnp
        import numpy as np
        D_MODEL = 128
        H = 16
        D_K = D_MODEL // H
        B, S = (2, 256)
        key = jax.random.key(seed)
        ks = jax.random.split(key, 8)
        scale = 1.0 / np.sqrt(D_MODEL)
        return {'q': jax.random.normal(ks[0], (B, S, D_MODEL), dtype=jnp.float32), 'k': jax.random.normal(ks[1], (B, S, D_MODEL), dtype=jnp.float32), 'v': jax.random.normal(ks[2], (B, S, D_MODEL), dtype=jnp.float32), 'W_q': jax.random.normal(ks[3], (H, D_MODEL, D_K), dtype=jnp.float32) * scale, 'W_k': jax.random.normal(ks[4], (H, D_MODEL, D_K), dtype=jnp.float32) * scale, 'W_v': jax.random.normal(ks[5], (H, D_MODEL, D_K), dtype=jnp.float32) * scale, 'W_o': jax.random.normal(ks[6], (D_MODEL, H * D_K), dtype=jnp.float32) * scale, 'b_o': jnp.zeros((D_MODEL,), dtype=jnp.float32)}
    _L0_xattn_all = _L0_xattn_setup()
    _L0_xattn_in = {k: v for k, v in _L0_xattn_all.items() if k in ('W_q', 'W_k', 'W_v', 'W_o', 'b_o')}
    del _L0_xattn_all

    def _L0_ffn_setup():
        import math
        import jax, jax.numpy as jnp
        import numpy as np
        B, T, H = (4, 256, 128)
        E, K, F = (8, 2, 256)
        CAP_FACTOR = 1.25

        def _moe_forward(x, Wg, W_in, W_out):
            b, t, h = x.shape
            xf = x.reshape(-1, h)
            S = xf.shape[0]
            C = int(math.ceil(K * S / E * CAP_FACTOR))
            logits = xf @ Wg
            probs = jax.nn.softmax(logits, axis=-1)
            top_vals, top_idx = jax.lax.top_k(probs, K)
            flat_idx = top_idx.T.reshape(-1)
            onehot = jax.nn.one_hot(flat_idx, E, dtype=jnp.int32)
            cum = jnp.cumsum(onehot, axis=0) - 1
            loc = jnp.take_along_axis(cum, flat_idx[:, None], axis=1)[:, 0]
            loc = loc.reshape(K, S).T
            keep = loc < C
            gates = top_vals * keep.astype(top_vals.dtype)
            denom = jnp.maximum(gates.sum(-1, keepdims=True), 1e-09)
            gates = gates / denom
            loc_c = jnp.where(keep, loc, C)
            e_flat = top_idx.reshape(-1)
            l_flat = loc_c.reshape(-1)
            xk = jnp.broadcast_to(xf[:, None, :], (S, K, h)).reshape(-1, h)
            xk = jnp.where(keep.reshape(-1, 1), xk, 0.0)
            buf = jnp.zeros((E, C + 1, h), x.dtype).at[e_flat, l_flat].set(xk)
            inp = buf[:, :C]
            hid = jnp.einsum('ech,ehf->ecf', inp, W_in)
            a, g = jnp.split(hid, 2, axis=-1)
            hid = jax.nn.gelu(a, approximate=False) * g
            out_e = jnp.einsum('ecf,efh->ech', hid, W_out)
            out_pad = jnp.concatenate([out_e, jnp.zeros((E, 1, h), out_e.dtype)], axis=1)
            gathered = out_pad[e_flat, l_flat].reshape(S, K, h)
            y = (gathered * gates[..., None]).sum(axis=1)
            return y.reshape(b, t, h)
        key = jax.random.key(seed)
        k1, k2, k3, k4 = jax.random.split(key, 4)
        x = jax.random.normal(k1, (B, T, H), dtype=jnp.float32)
        Wg = jax.random.normal(k2, (H, E), dtype=jnp.float32) * 0.02
        W_in = jax.random.normal(k3, (E, H, 2 * F), dtype=jnp.float32) * (1.0 / math.sqrt(H))
        W_out = jax.random.normal(k4, (E, F, H), dtype=jnp.float32) * (1.0 / math.sqrt(F))
        return {'x': x, 'Wg': Wg, 'W_in': W_in, 'W_out': W_out}
    _L0_ffn_all = _L0_ffn_setup()
    _L0_ffn_in = {k: v for k, v in _L0_ffn_all.items() if k in ('Wg', 'W_in', 'W_out')}
    del _L0_ffn_all

    def _L1_attn_setup():
        import jax, jax.numpy as jnp
        import numpy as np
        HEADS = 16
        PHI = (1.0 + np.sqrt(5.0)) / 2.0

        def phi_bias(L):
            pos = jnp.arange(L, dtype=jnp.float32) * PHI % 1.0
            dist = jnp.abs(pos[:, None] - pos[None, :])
            return jnp.log(jnp.exp(-dist) + 1e-08)
        key = jax.random.key(seed)
        k1, k2, k3, k4 = jax.random.split(key, 4)
        B, L, D = (2, 256, 128)
        x = jax.random.normal(k1, (B, L, D), dtype=jnp.float32)
        w_qkv = jax.random.normal(k2, (D, 3 * D), dtype=jnp.float32) * D ** (-0.5)
        w_proj = jax.random.normal(k3, (D, D), dtype=jnp.float32) * D ** (-0.5)
        b_proj = jax.random.normal(k4, (D,), dtype=jnp.float32) * 0.01
        return {'x': x, 'w_qkv': w_qkv, 'w_proj': w_proj, 'b_proj': b_proj}
    _L1_attn_all = _L1_attn_setup()
    _L1_attn_in = {k: v for k, v in _L1_attn_all.items() if k in ('w_qkv', 'w_proj', 'b_proj')}
    del _L1_attn_all

    def _L1_xattn_setup():
        import jax, jax.numpy as jnp
        import numpy as np
        import math
        N, K, M = (4, 256, 128)
        DQ, DV = (128, 128)

        def _xavier_uniform(k, shape, fan_in, fan_out):
            bound = math.sqrt(6.0 / (fan_in + fan_out))
            return jax.random.uniform(k, shape, jnp.float32, -bound, bound)
        key = jax.random.key(seed)
        ks = jax.random.split(key, 9)
        query = jax.random.normal(ks[0], (N, K, M), jnp.float32)
        key_t = jax.random.normal(ks[1], (N, K, M), jnp.float32)
        value = jax.random.normal(ks[2], (N, K, M), jnp.float32)
        mask = jnp.broadcast_to(jnp.triu(jnp.ones((K, K), bool), k=1), (N, K, K))
        Wq = _xavier_uniform(ks[3], (DQ, M), M, DQ)
        bq = jax.random.uniform(ks[4], (DQ,), jnp.float32, -1 / math.sqrt(M), 1 / math.sqrt(M))
        Wk = _xavier_uniform(ks[5], (DQ, M), M, DQ)
        bk = jax.random.uniform(ks[6], (DQ,), jnp.float32, -1 / math.sqrt(M), 1 / math.sqrt(M))
        Wv = _xavier_uniform(ks[7], (DV, M), M, DV)
        bv = jax.random.uniform(ks[8], (DV,), jnp.float32, -1 / math.sqrt(M), 1 / math.sqrt(M))
        return {'query': query, 'key': key_t, 'value': value, 'mask': mask, 'Wq': Wq, 'bq': bq, 'Wk': Wk, 'bk': bk, 'Wv': Wv, 'bv': bv}
    _L1_xattn_all = _L1_xattn_setup()
    _L1_xattn_in = {k: v for k, v in _L1_xattn_all.items() if k in ('Wq', 'bq', 'Wk', 'bk', 'Wv', 'bv')}
    del _L1_xattn_all

    def _L1_ffn_setup():
        import jax, jax.numpy as jnp
        import numpy as np
        CAPACITY_FACTOR = 1.0
        key = jax.random.key(seed)
        ks = jax.random.split(key, 5)
        B, S, D, E, F = (2, 256, 128, 8, 512)
        x = jax.random.normal(ks[0], (B, S, D), dtype=jnp.float32)
        Ws = jax.random.normal(ks[1], (D, E), dtype=jnp.float32) * (1.0 / np.sqrt(D))
        bs = jnp.zeros((E,), dtype=jnp.float32)
        W1 = jax.random.normal(ks[2], (E, D, F), dtype=jnp.float32) * (1.0 / np.sqrt(D))
        b1 = jnp.zeros((E, F), dtype=jnp.float32)
        W2 = jax.random.normal(ks[3], (E, F, D), dtype=jnp.float32) * (1.0 / np.sqrt(F))
        b2 = jnp.zeros((E, D), dtype=jnp.float32)
        return {'x': x, 'Ws': Ws, 'bs': bs, 'W1': W1, 'b1': b1, 'W2': W2, 'b2': b2}
    _L1_ffn_all = _L1_ffn_setup()
    _L1_ffn_in = {k: v for k, v in _L1_ffn_all.items() if k in ('Ws', 'bs', 'W1', 'b1', 'W2', 'b2')}
    del _L1_ffn_all
    return {'x': x, 'ctx_1024': ctx_1024, 'mask_BxSxS2_bk1': mask_BxSxS2_bk1, 'L0_attn_Wq': _L0_attn_in['Wq'], 'L0_attn_bq': _L0_attn_in['bq'], 'L0_attn_Wk': _L0_attn_in['Wk'], 'L0_attn_bk': _L0_attn_in['bk'], 'L0_attn_Wv': _L0_attn_in['Wv'], 'L0_attn_bv': _L0_attn_in['bv'], 'L0_attn_Wo': _L0_attn_in['Wo'], 'L0_attn_bo': _L0_attn_in['bo'], 'L0_attn_token_positions': _L0_attn_in['token_positions'], 'L0_xattn_W_q': _L0_xattn_in['W_q'], 'L0_xattn_W_k': _L0_xattn_in['W_k'], 'L0_xattn_W_v': _L0_xattn_in['W_v'], 'L0_xattn_W_o': _L0_xattn_in['W_o'], 'L0_xattn_b_o': _L0_xattn_in['b_o'], 'L0_ffn_Wg': _L0_ffn_in['Wg'], 'L0_ffn_W_in': _L0_ffn_in['W_in'], 'L0_ffn_W_out': _L0_ffn_in['W_out'], 'L1_attn_w_qkv': _L1_attn_in['w_qkv'], 'L1_attn_w_proj': _L1_attn_in['w_proj'], 'L1_attn_b_proj': _L1_attn_in['b_proj'], 'L1_xattn_Wq': _L1_xattn_in['Wq'], 'L1_xattn_bq': _L1_xattn_in['bq'], 'L1_xattn_Wk': _L1_xattn_in['Wk'], 'L1_xattn_bk': _L1_xattn_in['bk'], 'L1_xattn_Wv': _L1_xattn_in['Wv'], 'L1_xattn_bv': _L1_xattn_in['bv'], 'L1_ffn_Ws': _L1_ffn_in['Ws'], 'L1_ffn_bs': _L1_ffn_in['bs'], 'L1_ffn_W1': _L1_ffn_in['W1'], 'L1_ffn_b1': _L1_ffn_in['b1'], 'L1_ffn_W2': _L1_ffn_in['W2'], 'L1_ffn_b2': _L1_ffn_in['b2']}

def reference(x, ctx_1024, mask_BxSxS2_bk1, L0_attn_Wq, L0_attn_bq, L0_attn_Wk, L0_attn_bk, L0_attn_Wv, L0_attn_bv, L0_attn_Wo, L0_attn_bo, L0_attn_token_positions, L0_xattn_W_q, L0_xattn_W_k, L0_xattn_W_v, L0_xattn_W_o, L0_xattn_b_o, L0_ffn_Wg, L0_ffn_W_in, L0_ffn_W_out, L1_attn_w_qkv, L1_attn_w_proj, L1_attn_b_proj, L1_xattn_Wq, L1_xattn_bq, L1_xattn_Wk, L1_xattn_bk, L1_xattn_Wv, L1_xattn_bv, L1_ffn_Ws, L1_ffn_bs, L1_ffn_W1, L1_ffn_b1, L1_ffn_W2, L1_ffn_b2):
    import jax
    import jax.numpy as jnp

    def _L0_attn_ref(x, Wq, bq, Wk, bk, Wv, bv, Wo, bo, token_positions):
        import jax, jax.numpy as jnp
        import numpy as np
        D_MODEL = 128
        NUM_HEADS = 16
        D_K = D_MODEL // NUM_HEADS
        THETA = 10000.0
        NEG_INF = -1000000000.0

        def _rope(x, positions):
            half = D_K // 2
            inv_freq = 1.0 / THETA ** (jnp.arange(0, D_K, 2, dtype=jnp.float32) / D_K)
            angles = positions.astype(jnp.float32)[:, None] * inv_freq
            cos, sin = (jnp.cos(angles), jnp.sin(angles))
            xe = x[..., 0::2]
            xo = x[..., 1::2]
            re = xe * cos - xo * sin
            ro = xe * sin + xo * cos
            return jnp.stack([re, ro], axis=-1).reshape(x.shape).astype(x.dtype)
        B, S, D = x.shape
        Q = x @ Wq.T + bq
        K = x @ Wk.T + bk
        V = x @ Wv.T + bv

        def split_heads(t):
            return t.reshape(B, S, NUM_HEADS, D_K).transpose(0, 2, 1, 3)
        Q, K, V = (split_heads(Q), split_heads(K), split_heads(V))
        pos = jnp.arange(S)
        Q = _rope(Q, pos)
        K = _rope(K, pos)
        scale = 1.0 / jnp.sqrt(jnp.float32(D_K))
        scores = jnp.einsum('bhqd,bhkd->bhqk', Q, K) * scale
        causal = jnp.tril(jnp.ones((S, S), dtype=bool))
        scores = jnp.where(causal, scores, NEG_INF)
        weights = jax.nn.softmax(scores, axis=-1)
        attn = jnp.einsum('bhqk,bhkd->bhqd', weights, V)
        concat = attn.transpose(0, 2, 1, 3).reshape(B, S, D)
        return concat @ Wo.T + bo

    def _L0_xattn_ref(q, k, v, W_q, W_k, W_v, W_o, b_o):
        import jax, jax.numpy as jnp
        import numpy as np
        D_MODEL = 128
        H = 16
        D_K = D_MODEL // H
        B, S = (2, 256)
        b, s, _ = q.shape
        h, _, d_k = W_q.shape
        inv_sqrt_dk = jnp.asarray(1.0 / np.sqrt(d_k), q.dtype)
        qh = jnp.einsum('bsd,hdk->bhsk', q, W_q)
        kh = jnp.einsum('bsd,hdk->bhsk', k, W_k)
        vh = jnp.einsum('bsd,hdk->bhsk', v, W_v)
        scores = jnp.einsum('bhqk,bhsk->bhqs', qh, kh) * inv_sqrt_dk
        attn = jax.nn.softmax(scores, axis=-1)
        ctx = jnp.einsum('bhqs,bhsk->bhqk', attn, vh)
        ctx = ctx.transpose(0, 2, 1, 3).reshape(b, s, h * d_k)
        return ctx @ W_o.T + b_o

    def _L0_ffn_ref(x, Wg, W_in, W_out):
        import math
        import jax, jax.numpy as jnp
        import numpy as np
        B, T, H = (4, 256, 128)
        E, K, F = (8, 2, 256)
        CAP_FACTOR = 1.25

        def _moe_forward(x, Wg, W_in, W_out):
            b, t, h = x.shape
            xf = x.reshape(-1, h)
            S = xf.shape[0]
            C = int(math.ceil(K * S / E * CAP_FACTOR))
            logits = xf @ Wg
            probs = jax.nn.softmax(logits, axis=-1)
            top_vals, top_idx = jax.lax.top_k(probs, K)
            flat_idx = top_idx.T.reshape(-1)
            onehot = jax.nn.one_hot(flat_idx, E, dtype=jnp.int32)
            cum = jnp.cumsum(onehot, axis=0) - 1
            loc = jnp.take_along_axis(cum, flat_idx[:, None], axis=1)[:, 0]
            loc = loc.reshape(K, S).T
            keep = loc < C
            gates = top_vals * keep.astype(top_vals.dtype)
            denom = jnp.maximum(gates.sum(-1, keepdims=True), 1e-09)
            gates = gates / denom
            loc_c = jnp.where(keep, loc, C)
            e_flat = top_idx.reshape(-1)
            l_flat = loc_c.reshape(-1)
            xk = jnp.broadcast_to(xf[:, None, :], (S, K, h)).reshape(-1, h)
            xk = jnp.where(keep.reshape(-1, 1), xk, 0.0)
            buf = jnp.zeros((E, C + 1, h), x.dtype).at[e_flat, l_flat].set(xk)
            inp = buf[:, :C]
            hid = jnp.einsum('ech,ehf->ecf', inp, W_in)
            a, g = jnp.split(hid, 2, axis=-1)
            hid = jax.nn.gelu(a, approximate=False) * g
            out_e = jnp.einsum('ecf,efh->ech', hid, W_out)
            out_pad = jnp.concatenate([out_e, jnp.zeros((E, 1, h), out_e.dtype)], axis=1)
            gathered = out_pad[e_flat, l_flat].reshape(S, K, h)
            y = (gathered * gates[..., None]).sum(axis=1)
            return y.reshape(b, t, h)
        return _moe_forward(x, Wg, W_in, W_out)

    def _L1_attn_ref(x, w_qkv, w_proj, b_proj):
        import jax, jax.numpy as jnp
        import numpy as np
        HEADS = 16
        PHI = (1.0 + np.sqrt(5.0)) / 2.0

        def phi_bias(L):
            pos = jnp.arange(L, dtype=jnp.float32) * PHI % 1.0
            dist = jnp.abs(pos[:, None] - pos[None, :])
            return jnp.log(jnp.exp(-dist) + 1e-08)
        B, L, D = x.shape
        H = HEADS
        Dh = D // H
        scale = Dh ** (-0.5)
        qkv = (x @ w_qkv).reshape(B, L, 3, H, Dh)
        q = jnp.transpose(qkv[:, :, 0], (0, 2, 1, 3))
        k = jnp.transpose(qkv[:, :, 1], (0, 2, 1, 3))
        v = jnp.transpose(qkv[:, :, 2], (0, 2, 1, 3))
        attn = jnp.einsum('bhid,bhjd->bhij', q, k) * scale
        attn = attn + phi_bias(L)[None, None]
        attn = jax.nn.softmax(attn, axis=-1)
        out = jnp.einsum('bhij,bhjd->bhid', attn, v)
        out = jnp.transpose(out, (0, 2, 1, 3)).reshape(B, L, D)
        return out @ w_proj + b_proj

    def _L1_xattn_ref(query, key, value, mask, Wq, bq, Wk, bk, Wv, bv):
        import jax, jax.numpy as jnp
        import numpy as np
        import math
        N, K, M = (4, 256, 128)
        DQ, DV = (128, 128)

        def _xavier_uniform(k, shape, fan_in, fan_out):
            bound = math.sqrt(6.0 / (fan_in + fan_out))
            return jax.random.uniform(k, shape, jnp.float32, -bound, bound)
        Q = jnp.einsum('nkm,dm->nkd', query, Wq) + bq
        Kp = jnp.einsum('nkm,dm->nkd', key, Wk) + bk
        V = jnp.einsum('nkm,dm->nkd', value, Wv) + bv
        scores = jnp.einsum('nqd,nkd->nqk', Q, Kp) / jnp.sqrt(jnp.float32(DQ))
        scores = jnp.where(mask, jnp.float32(-1000000000.0), scores)
        w = jax.nn.softmax(scores, axis=2)
        y = jnp.einsum('nqk,nkd->nqd', w, V)
        return y

    def _L1_ffn_ref(x, Ws, bs, W1, b1, W2, b2):
        import jax, jax.numpy as jnp
        import numpy as np
        CAPACITY_FACTOR = 1.0
        B, S, D = x.shape
        E = Ws.shape[1]
        N = B * S
        k = int(CAPACITY_FACTOR * N / E)
        xf = x.reshape(N, D)
        route_prob = jax.nn.softmax(xf @ Ws + bs, axis=-1).T
        route_vals, routes = jax.lax.top_k(route_prob, k)
        xin = xf[routes]
        h = jax.nn.gelu(jnp.einsum('ekd,edf->ekf', xin, W1) + b1[:, None, :])
        out = jnp.einsum('ekf,efd->ekd', h, W2) + b2[:, None, :]
        out = out * route_vals[..., None]
        final = jnp.zeros((N, D), dtype=x.dtype).at[routes.reshape(-1)].add(out.reshape(-1, D))
        return final.reshape(B, S, D)
    x = _layernorm(x + _L0_attn_ref(x, L0_attn_Wq, L0_attn_bq, L0_attn_Wk, L0_attn_bk, L0_attn_Wv, L0_attn_bv, L0_attn_Wo, L0_attn_bo, L0_attn_token_positions), axis=-1)
    x = _layernorm(x + _L0_xattn_ref(x, ctx_1024, ctx_1024, L0_xattn_W_q, L0_xattn_W_k, L0_xattn_W_v, L0_xattn_W_o, L0_xattn_b_o), axis=-1)
    x = _layernorm(x + _L0_ffn_ref(x, L0_ffn_Wg, L0_ffn_W_in, L0_ffn_W_out), axis=-1)
    x = _layernorm(x + _L1_attn_ref(x, L1_attn_w_qkv, L1_attn_w_proj, L1_attn_b_proj), axis=-1)
    x = _layernorm(x + _L1_xattn_ref(x, ctx_1024, ctx_1024, mask_BxSxS2_bk1, L1_xattn_Wq, L1_xattn_bq, L1_xattn_Wk, L1_xattn_bk, L1_xattn_Wv, L1_xattn_bv), axis=-1)
    x = _layernorm(x + _L1_ffn_ref(x, L1_ffn_Ws, L1_ffn_bs, L1_ffn_W1, L1_ffn_b1, L1_ffn_W2, L1_ffn_b2), axis=-1)
    return x

_drawn_inputs = setup_inputs


def setup_inputs(seed=0):
    import zlib

    import numpy as np

    out = dict(_drawn_inputs(seed))
    spreads = {'L0_attn_bq': (0.0, 0.1),
     'L0_attn_bk': (0.0, 0.1),
     'L0_attn_bv': (0.0, 0.1),
     'L0_attn_bo': (0.0, 0.1),
     'L0_xattn_b_o': (0.0, 0.1),
     'L1_ffn_bs': (0.0, 0.1),
     'L1_ffn_b1': (0.0, 0.321),
     'L1_ffn_b2': (0.0, 0.1)}
    factors = {'L1_attn_b_proj': 3.626, 'L1_xattn_bq': 2.975, 'L1_xattn_bk': 8.0}
    for name, (base, spread) in spreads.items():
        noise = np.random.default_rng([zlib.crc32(name.encode()), seed]).standard_normal(out[name].shape)
        drawn = base * np.exp(spread * noise) if base else spread * noise
        out[name] = jnp.asarray(drawn.astype(out[name].dtype))
    for name, factor in factors.items():
        out[name] = (out[name] * factor).astype(out[name].dtype)
    return out
```

```python
from contextlib import ExitStack

import numpy as np

import concourse.bass as bass
from concourse import mybir

F32 = mybir.dt.float32
F16 = mybir.dt.float16
I32 = mybir.dt.int32
U8 = mybir.dt.uint8
ALU = mybir.AluOpType
ACT = mybir.ActivationFunctionType
AX = mybir.AxisListType

B, S, D = 32, 56, 128
SK = 1500
H, DK = 16, 8
PAIRS = B // 2
PT = 2 * S
TOK = B * S
QP = 64
CHUNK = 125
CHUNKS = SK // CHUNK
GROUPS, HG = 4, 4
GC = HG * S
THIRD = SK // 3
HEAD_SCALE = float(DK) ** -0.5
LN_EPS = 1e-5
NEG = -1e9
BLK = 448
NBLK = TOK // BLK


def wait_pos(eng, sem, value):
    if isinstance(value, int) and value <= 0:
        return
    eng.wait_ge(sem, value)


def in_steps(eng, first, last, loop_from, loop_to, body):
    for s in range(first, loop_from):
        body(s, s % 2, s // 2)
    with eng.Fori(loop_from // 2, loop_to // 2) as i:
        for u in range(2):
            body(2 * i + u, u, i)
    for s in range(loop_to, last):
        body(s, s % 2, s // 2)


def in_blocks(eng, count, body):
    body(0)
    with eng.Fori(1, count) as n:
        body(n)


def has(s, low, high):
    return not isinstance(s, int) or low <= s < high


class Core:

    def __init__(self, nc, dram):
        self.nc, self.dram = nc, dram


def tools(nc, ctx):
    stage_sems = []

    @ctx.callback
    def _():
        nc.clear_and_free_semaphores(stage_sems)
        nc.all_engine_barrier()

    def sb(name, shape, dt=F32):
        return ctx.enter_context(nc.sbuf_tensor(name, shape, dt))

    def ps(name, shape, dt=F32):
        return ctx.enter_context(nc.psum_tensor(name, shape, dt))

    def sem(name):
        stage_sems.append(nc.alloc_semaphore(name))
        return stage_sems[-1]

    return sb, ps, sem


def load_inputs(core):
    nc, dram = core.nc, core.dram
    with ExitStack() as ctx:
        sb, ps, sem = tools(nc, ctx)
        loaded = sem("in_loaded")
        block = ctx.enter_context(nc.Block())

        @block.sync
        def _(sp):
            sp.dma_start(core.xT[:], dram["xT"]).then_inc(loaded, 16)
            sp.dma_start(core.x[:], dram["x"].rearrange("(t p) d -> p t d", p=PT)).then_inc(loaded, 16)
            sp.dma_start(core.ident[:], dram["ident"]).then_inc(loaded, 16)
            sp.dma_start(core.first_row[:], dram["first_row"]).then_inc(loaded, 16)
            sp.wait_ge(loaded, 64)


def layer_norm(core, tag, out=None):
    nc, x, xT = core.nc, core.x, core.xT
    with ExitStack() as ctx:
        sb, ps, sem = tools(nc, ctx)
        stats = sb(f"{tag}_stats", [PT, PAIRS, 6])
        mv = sb(f"{tag}_mv", [PT, PAIRS, 2])
        std = sb(f"{tag}_std", [PT, PAIRS])
        rstd = sb(f"{tag}_rstd", [PT, PAIRS])
        turned = [ps(f"{tag}_turned{k}", [128, 512]) for k in range(4)]
        stats_made, var_made, std_made, rstd_made = (sem(f"{tag}_{n}") for n in ("stats_s", "var_s", "std_s", "rstd_s"))
        normed, transposed, stored = (sem(f"{tag}_{n}") for n in ("normed", "transposed", "stored"))
        block = ctx.enter_context(nc.Block())

        @block.vector
        def _(dve):
            for t in range(PAIRS):
                nc.vector.bn_stats(stats[:, t, :], x[:, t, :]).then_inc(stats_made, 1)
            for t in range(PAIRS):
                dve.wait_ge(stats_made, t + 1)
                nc.vector.bn_aggr(mv[:, t, :], stats[:, t, :]).then_inc(stats_made, 1)
            dve.wait_ge(stats_made, 2 * PAIRS)
            nc.vector.tensor_scalar(std[:], mv[:, :, 1], LN_EPS, None, ALU.add).then_inc(var_made, 1)
            dve.wait_ge(std_made, 1)
            nc.vector.reciprocal(rstd[:], std[:]).then_inc(rstd_made, 1)
            dve.wait_ge(rstd_made, 1)
            for t in range(PAIRS):
                nc.vector.tensor_scalar(x[:, t, :], x[:, t, :], mv[:, t, 0:1], rstd[:, t:t + 1],
                                        ALU.subtract, ALU.mult).then_inc(normed, 1)

        @block.scalar
        def _(act):
            act.wait_ge(var_made, 1)
            nc.scalar.activation(std[:], std[:], ACT.Sqrt).then_inc(std_made, 1)
            if out is None:
                for k in range(4):
                    act.wait_ge(transposed, k + 1)
                    nc.scalar.copy(xT[:, k * BLK:(k + 1) * BLK], turned[k][:, 0:BLK])

        @block.tensor
        def _(pe):
            if out is None:
                for k in range(4):
                    pe.wait_ge(normed, 4 * k + 4)
                    for t in range(4):
                        mm = nc.tensor.transpose(turned[k][:, t * PT:(t + 1) * PT], x[:, 4 * k + t, :],
                                                 core.ident[0:PT, 0:PT])
                    mm.then_inc(transposed, 1)

        @block.sync
        def _(sp):
            if out is not None:
                for k in range(4):
                    sp.wait_ge(normed, 4 * k + 4)
                    sp.dma_start(out[4 * k * PT:4 * (k + 1) * PT, :].rearrange("(t p) d -> p t d", p=PT),
                                 x[:, 4 * k:4 * k + 4, :]).then_inc(stored, 16)
                sp.wait_ge(stored, 64)


def self_attention(core, layer):
    nc, dram, x, xT = core.nc, core.dram, core.x, core.xT
    rope = layer == 0
    L = f"s{layer}_"
    names = ["wq", "wqs", "wk", "wks", "wv", "wo", "bo"] if rope else ["wq", "wk", "wv", "wo", "bo"]
    with ExitStack() as ctx:
        sb, ps, sem = tools(nc, ctx)
        W = {n: sb(L + n, [128, 128]) for n in names}
        bias = sb(L + "bias", [128, S])
        head_of_row = sb(L + "head_of_row", [128, H])
        vmask = sb(L + "vmask", [PT, 128])
        if rope:
            cos, sin = sb(L + "cos", [128, S]), sb(L + "sin", [128, S])
            cols = sb(L + "cols", [128, 5])
            part_a, part_b = sb(L + "part_a", [128, BLK]), sb(L + "part_b", [128, BLK])
        Q = sb(L + "Q", [128, B, QP])
        K = sb(L + "K", [128, B, S])
        q_pair = sb(L + "q_pair", [128, 2, 2, QP])
        x_twice = sb(L + "x_twice", [128, 2, 2, 2, S])
        Kbd = sb(L + "Kbd", [128, 2, 2, H * S])
        Vbd = sb(L + "Vbd", [PT, 2, 2, H, DK + 1])
        P = sb(L + "P", [128, 2, H * S])
        PTr = sb(L + "PTr", [PT, H // 2, 128])
        top = sb(L + "top", [128, 2, H])
        rden = sb(L + "rden", [128, 2, H])
        O = sb(L + "O", [128, 2, 128])
        OT = sb(L + "OT", [128, 2, PT])

        psS = ps(L + "psS", [128, 2, 512])
        psT = ps(L + "psT", [128, 2, 512])
        psV = ps(L + "psV", [128, 512])
        psO = ps(L + "psO", [128, 512])
        psOT = ps(L + "psOT", [128, 512])
        psY = ps(L + "psY", [128, 512])

        loaded, padded = sem(L + "loaded"), sem(L + "padded")
        proj_ready, proj_used, rope_parts = (sem(L + n) for n in ("proj_ready", "proj_used", "rope_parts"))
        xs_ready, kbd_ready, v_ready, vbd_ready, s_ready, top_ready, s_used, p_ready = (sem(L + n) for n in (
            "xs_ready", "kbd_ready", "v_ready", "vbd_ready", "s_ready", "top_ready", "s_used", "p_ready"))
        t_ready, t_moved, o_ready, rden_ready, o_moved, ot_ready, ot_moved, y_ready, y_used = (sem(L + n) for n in (
            "t_ready", "t_moved", "o_ready", "rden_ready", "o_moved", "ot_ready", "ot_moved", "y_ready", "y_used"))
        block = ctx.enter_context(nc.Block())
        n_loads = len(names) + (8 if rope else 5)
        projections = [("wq", "wqs", 0, Q), ("wk", "wks", 2, K)]
        banks = [psS[:, 0, :], psS[:, 1, :], psT[:, 0, :], psT[:, 1, :]]

        @block.sync
        def _(sp):
            for n in names:
                sp.dma_start(W[n][:], dram[L + n]).then_inc(loaded, 16)
            sp.dma_start(bias[:], dram[L + "bias"]).then_inc(loaded, 16)
            sp.dma_start(head_of_row[:], dram["head_of_row"]).then_inc(loaded, 16)
            sp.dma_start(vmask[:], dram["vmask"]).then_inc(loaded, 16)
            for u in range(2):
                sp.dma_start(Vbd[:, u, :, :, :], dram["vbd_ones"]).then_inc(loaded, 16)
            if rope:
                sp.dma_start(cos[:], dram["rope_cos"]).then_inc(loaded, 16)
                sp.dma_start(sin[:], dram["rope_sin"]).then_inc(loaded, 16)
                sp.dma_start(cols[:], dram["s0_cols"]).then_inc(loaded, 16)

        @block.gpsimd
        def _(pool):
            nc.gpsimd.memset(Q[:, :, S:QP], 0.0).then_inc(padded, 1)
            pool.wait_ge(loaded, 16 * n_loads)
            pool.wait_ge(proj_used, 2 * NBLK)

            def step(t, u, i):
                if has(t, 0, PAIRS):
                    wait_pos(pool, s_ready, t - 1)
                    for b in range(2):
                        nc.gpsimd.tensor_tensor(
                            Kbd[:, u, b, :].rearrange("p (h k) -> p h k", h=H),
                            K[:, 2 * t + b, :].unsqueeze(1).to_broadcast([128, H, S]),
                            head_of_row[:].unsqueeze(2).to_broadcast([128, H, S]), ALU.mult).then_inc(kbd_ready, 1)

            in_steps(pool, 0, PAIRS, 2, PAIRS, step)

        @block.tensor
        def _(pe):
            pe.wait_ge(loaded, 16 * n_loads)
            for n, (w, ws, _, _) in enumerate(projections):
                for k in range(NBLK):
                    m = n * NBLK + k
                    wait_pos(pe, proj_used, m - (1 if rope else 3))
                    if rope:
                        nc.tensor.matmul(banks[2 * (m % 2)][:, 0:BLK], W[w][:], xT[:, k * BLK:(k + 1) * BLK],
                                         start=True, stop=True)
                        nc.tensor.matmul(banks[2 * (m % 2) + 1][:, 0:BLK], W[ws][:], xT[:, k * BLK:(k + 1) * BLK],
                                         start=True, stop=True).then_inc(proj_ready, 1)
                    else:
                        nc.tensor.matmul(banks[m % 4][:, 0:BLK], W[w][:], xT[:, k * BLK:(k + 1) * BLK],
                                         start=True, stop=True).then_inc(proj_ready, 1)
            pe.wait_ge(proj_used, 2 * NBLK)

            def step(t, u, i):
                v = 1 - u
                if has(t, 0, PAIRS):
                    pe.wait_ge(xs_ready, t + 1)
                    wait_pos(pe, vbd_ready, t)
                    for b in range(2):
                        mm = nc.tensor.matmul(psV[0:PT, b * 128:(b + 1) * 128], x_twice[:, u, b, :, :], W["wv"][:],
                                              start=True, stop=True)
                    mm.then_inc(v_ready, 1)
                if has(t, 1, PAIRS + 1):
                    pe.wait_ge(p_ready, t)
                    wait_pos(pe, t_moved, t - 1)
                    for hp in range(H // 2):
                        mm = nc.tensor.transpose(psT[0:PT, hp // 4, (hp % 4) * 128:(hp % 4 + 1) * 128],
                                                 P[:, v, hp * PT:(hp + 1) * PT], core.ident[:])
                    mm.then_inc(t_ready, 1)
                if has(t, 2, PAIRS + 2):
                    pe.wait_ge(o_moved, t - 1)
                    wait_pos(pe, ot_moved, t - 2)
                    nc.tensor.transpose(psOT[:, 0:128], O[:, u, :], core.ident[:]).then_inc(ot_ready, 1)
                if has(t, 0, PAIRS):
                    pe.wait_ge(kbd_ready, 2 * t + 2)
                    wait_pos(pe, s_used, t)
                    for half in range(2):
                        nc.tensor.matmul(psS[:, half, 0:BLK], core.ident[:],
                                         bias[:].unsqueeze(1).to_broadcast([128, H // 2, S]),
                                         start=True, stop=False, skip_group_check=True)
                        for b in range(2):
                            mm = nc.tensor.matmul(psS[QP * b:QP * (b + 1), half, 0:BLK], q_pair[:, u, b, :],
                                                  Kbd[:, u, b, half * BLK:(half + 1) * BLK],
                                                  start=False, stop=True, skip_group_check=True)
                    mm.then_inc(s_ready, 1)
                if has(t, 1, PAIRS + 1):
                    pe.wait_ge(t_moved, t)
                    pe.wait_ge(vbd_ready, t)
                    wait_pos(pe, o_moved, t - 1)
                    for b in range(2):
                        for hp in range(H // 2):
                            mm = nc.tensor.matmul(
                                psO[QP * b:QP * (b + 1), hp * 18:(hp + 1) * 18], PTr[:, hp, QP * b:QP * (b + 1)],
                                Vbd[:, v, b, 2 * hp:2 * hp + 2, :], start=True, stop=True)
                    mm.then_inc(o_ready, 1)
                if has(t, 2, PAIRS + 2):
                    pe.wait_ge(ot_moved, t - 1)
                    wait_pos(pe, y_used, t - 2)
                    nc.tensor.matmul(psY[0:PT, 0:128], OT[:, u, :], W["wo"][:], start=True, stop=False)
                    nc.tensor.matmul(psY[0:PT, 0:128], core.first_row[:, 0:PT], W["bo"][:],
                                     start=False, stop=True).then_inc(y_ready, 1)

            in_steps(pe, 0, PAIRS + 2, 4, PAIRS, step)

        @block.vector
        def _(dve):
            dve.wait_ge(loaded, 16 * n_loads)
            for n, (_, _, col, dest) in enumerate(projections):
                for k in range(NBLK):
                    m = n * NBLK + k
                    dve.wait_ge(proj_ready, m + 1)
                    if not rope:
                        nc.vector.tensor_copy(dest[:, 8 * k:8 * k + 8, 0:S],
                                              banks[m % 4][:, 0:BLK].rearrange("p (b s) -> p b s", b=8)).then_inc(proj_used, 1)
                        continue
                    wait_pos(dve, proj_used, m)
                    for w, part, table in ((0, part_a, cos), (1, part_b, sin)):
                        nc.vector.scalar_tensor_tensor(
                            part[:].rearrange("p (b s) -> p b s", b=8),
                            banks[2 * (m % 2) + w][:, 0:BLK].rearrange("p (b s) -> p b s", b=8),
                            cols[:, col + w:col + w + 1], table[:].unsqueeze(1).to_broadcast([128, 8, S]),
                            ALU.add, ALU.mult).then_inc(rope_parts, 1)
                    dve.wait_ge(rope_parts, 2 * m + 2)
                    nc.vector.tensor_tensor(dest[:, 8 * k:8 * k + 8, 0:S], part_a[:].rearrange("p (b s) -> p b s", b=8),
                                            part_b[:].rearrange("p (b s) -> p b s", b=8), ALU.add).then_inc(proj_used, 1)

            def step(t, u, i):
                v = 1 - u
                if has(t, 0, PAIRS):
                    dve.wait_ge(v_ready, t + 1)
                    wait_pos(dve, o_ready, t - 1)
                    for b in range(2):
                        vbd = nc.vector.tensor_tensor(Vbd[:, u, b, :, 0:DK],
                                                     psV[0:PT, b * 128:(b + 1) * 128].rearrange("p (h d) -> p h d", h=H),
                                                     vmask[:].rearrange("p (h d) -> p h d", h=H), ALU.mult)
                    vbd.then_inc(vbd_ready, 1)
                    dve.wait_ge(s_ready, t + 1)
                    scores = psS[:, :, 0:BLK].rearrange("p a (h k) -> p a h k", k=S)
                    nc.vector.tensor_reduce(top[:, u, :].rearrange("p (a h) -> p a h", a=2), scores, AX.X,
                                            ALU.max).then_inc(top_ready, 1)
                    dve.wait_ge(top_ready, t + 1)
                    nc.vector.tensor_tensor(
                        P[:, u, :].rearrange("p (a h k) -> p a h k", a=2, k=S), scores,
                        top[:, u, :].rearrange("p (a h) -> p a h", a=2).unsqueeze(3).to_broadcast([128, 2, H // 2, S]),
                        ALU.subtract).then_inc(s_used, 1)
                if has(t, 1, PAIRS + 1):
                    dve.wait_ge(o_ready, t)
                    sums = psO[:, 0:144].rearrange("p (h d) -> p h d", h=H)
                    nc.vector.reciprocal(rden[:, v, :], sums[:, :, DK]).then_inc(rden_ready, 1)
                    dve.wait_ge(rden_ready, t)
                    wait_pos(dve, ot_ready, t - 2)
                    nc.vector.tensor_tensor(O[:, v, :].rearrange("p (h d) -> p h d", h=H), sums[:, :, 0:DK],
                                            rden[:, v, :].unsqueeze(2).to_broadcast([128, H, DK]),
                                            ALU.mult).then_inc(o_moved, 1)
                if has(t, 2, PAIRS + 2):
                    dve.wait_ge(y_ready, t - 1)
                    nc.vector.tensor_tensor(x[:, t - 2, :], psY[0:PT, 0:128], x[:, t - 2, :],
                                            ALU.add).then_inc(y_used, 1)

            in_steps(dve, 0, PAIRS + 2, 4, PAIRS, step)

        @block.scalar
        def _(act):
            act.wait_ge(padded, 1)
            act.wait_ge(proj_used, 2 * NBLK)

            def step(t, u, i):
                v = 1 - u
                if has(t, 0, PAIRS):
                    wait_pos(act, s_ready, t - 1)
                    wait_pos(act, v_ready, t - 1)
                    nc.scalar.copy(q_pair[:, u, :, :], Q[:, bass.ds(2 * t, 2), :])
                    nc.scalar.copy(x_twice[:, u, :, :, :],
                                   xT[:, bass.ds(PT * t, PT)].rearrange("p (b s) -> p b s", b=2).unsqueeze(2)
                                   .to_broadcast([128, 2, 2, S])).then_inc(xs_ready, 1)
                if has(t, 1, PAIRS + 1):
                    act.wait_ge(t_ready, t)
                    wait_pos(act, o_ready, t - 1)
                    nc.scalar.copy(PTr[:], psT[0:PT, :, :].rearrange("p a (h c) -> p (a h) c", c=128)).then_inc(t_moved, 1)
                if has(t, 2, PAIRS + 2):
                    act.wait_ge(ot_ready, t - 1)
                    wait_pos(act, y_ready, t - 2)
                    dst = OT[:, u, :].rearrange("p (b s) -> p b s", b=2)
                    src = psOT[:, 0:128].rearrange("p (b s) -> p b s", b=2)[:, :, 0:S]
                    if rope:
                        nc.scalar.activation(dst, src, ACT.Identity, bias=cols[:, 4:5]).then_inc(ot_moved, 1)
                    else:
                        nc.scalar.copy(dst, src).then_inc(ot_moved, 1)
                if has(t, 0, PAIRS):
                    act.wait_ge(s_used, t + 1)
                    nc.scalar.activation(P[:, u, :], P[:, u, :], ACT.Exp, scale=HEAD_SCALE).then_inc(p_ready, 1)

            in_steps(act, 0, PAIRS + 2, 4, PAIRS, step)


class Units:

    RING = 3
    PER_STEP = {"V": 3, "K": 3, "max": 24, "shift": 2, "den": 1, "y": 1}
    ORDER = [[("V", k) for k in range(3)] + [("K", k) for k in range(3)] + ([("den", 0)] if u == 0 else [])
             + [("max", k) for k in range(5)] + ([("y", 0)] if u == 0 else [])
             + [("max", k) for k in range(5, 24)] + [("shift", k) for k in range(2)] for u in range(2)]
    PAIR = ORDER[0] + ORDER[1]
    assert len(PAIR) % RING == 0

    def __init__(self, ready, read):
        self.ready, self.read = ready, read

    @staticmethod
    def has(kind, s):
        low, high = {"V": (-1, B - 1), "K": (-2, B - 2), "max": (-1, B - 1), "shift": (-1, B - 1),
                     "den": (2, B + 1), "y": (2, B + 1)}[kind]
        return has(s, low, high)

    def bank(self, u, unit):
        return (u * len(self.ORDER[0]) + self.ORDER[u].index(unit)) % self.RING

    def count(self, kind, k, s, i):
        turn = {"V": s + 1, "K": s + 2, "max": s + 1, "shift": s + 1, "den": i - 1, "y": i - 1}[kind]
        return self.PER_STEP[kind] * turn + k + 1

    def wait_free(self, eng, s, u, i, unit):
        at = u * len(self.ORDER[0]) + self.ORDER[u].index(unit)
        back = 0
        while True:
            at -= self.RING
            if at < 0:
                at += len(self.PAIR)
                back += 1
                if isinstance(s, int) and i - back < -1:
                    return
            kind, k = self.PAIR[at]
            v = int(at >= len(self.ORDER[0]))
            before = s - u - 2 * back + v
            if self.has(kind, before):
                return wait_pos(eng, self.read[kind], self.count(kind, k, before, i - back))

    def wait_ready(self, eng, s, i, unit):
        eng.wait_ge(self.ready[unit[0]], self.count(*unit, s, i))

    def wait_read(self, eng, s, i, unit):
        eng.wait_ge(self.read[unit[0]], self.count(*unit, s, i))


def context_attention(core):
    nc, dram, x, xT = core.nc, core.dram, core.x, core.xT
    R = 32
    with ExitStack() as ctx:
        sb, ps, sem = tools(nc, ctx)
        wq, wk, wv, bo = (sb(f"c0_{n}", [128, 128]) for n in ("wq", "wk", "wv", "bo"))
        wo = sb("c0_wo", [128, HG, 128])
        sum_row = sb("c0_sum_row", [128, 128])
        head_in_group = sb("c0_head_in_group", [128, HG])
        q_hi, q_lo = sb("c0_q_hi", [128, B, HG, S], F16), sb("c0_q_lo", [128, B, HG, S], F16)
        ctxT = sb("c0_ctxT", [128, 2, SK])
        k_hi, k_lo = sb("c0_k_hi", [128, 2, SK], F16), sb("c0_k_lo", [128, 2, SK], F16)
        Kst = [sb(f"c0_Kst{v}", [97, GROUPS, SK], F16) for v in range(2)]
        Qst = [sb(f"c0_Qst{v}", [97, GROUPS, HG, S], F16) for v in range(2)]
        V3 = sb("c0_V3", [CHUNK, 2, CHUNKS, GROUPS, R])
        V1 = sb("c0_V1", [CHUNK, 2, CHUNKS, GROUPS, R])
        P = sb("c0_P", [CHUNK, 3, GROUPS, GC])
        thirds = sb("c0_thirds", [PT, 8, 3])
        top = sb("c0_top", [PT, 8])
        sums = sb("c0_sums", [128, HG, 2, S])
        rden = sb("c0_rden", [128, HG, 2, S])
        heads = sb("c0_heads", [128, HG, 2, S])

        psE = ps("c0_psE", [128, 2, 2, 512])
        psO = ps("c0_psO", [128, HG, S + 8])
        ring = [ps(f"c0_ring{k}", [128, 512]) for k in range(Units.RING)]

        loaded, filled = sem("c0_loaded"), sem("c0_filled")
        q_ready, q_hi_made, q_lo_made = sem("c0_q_ready"), sem("c0_q_hi_made"), sem("c0_q_lo_made")
        ctx_loaded = [sem(f"c0_ctx_loaded{v}") for v in range(2)]
        stacked = [sem(f"c0_stacked{g}") for g in range(GROUPS)]
        k_hi_made, thirds_made, top_made = sem("c0_k_hi_made"), sem("c0_thirds_made"), sem("c0_top_made")
        e_ready, p_ready, av_done, o_moved, heads_made = (sem(f"c0_{n}") for n in (
            "e_ready", "p_ready", "av_done", "o_moved", "heads_made"))
        ready = {k: sem(f"c0_{k}_ready") for k in Units.PER_STEP}
        read = {k: sem(f"c0_{k}_read") for k in Units.PER_STEP}
        units = Units(ready, read)
        block = ctx.enter_context(nc.Block())
        N_LOADS = 7
        first, last, loop_from, loop_to = -2, B + 1, 4, B - 4

        @block.sync
        def _(sp):
            for dst, name in ((wq, "c0_wq"), (wk, "c0_wk"), (wv, "c0_wv"), (bo, "c0_bo"), (wo, "c0_wo"),
                              (sum_row, "c0_sum_row"), (head_in_group, "head_in_group")):
                sp.dma_start(dst[:], dram[name]).then_inc(loaded, 16)
            for v in range(2):
                sp.dma_start(ctxT[:, v, :], dram["ctxT"][v]).then_inc(ctx_loaded[v], 16)
            sp.wait_ge(q_lo_made, NBLK * HG)

            def step(s, u, i):
                v = 1 - u
                if has(s, -1, B - 1):
                    if isinstance(s, int):
                        sp.wait_ge(read["K"], 3 * (s + 2))
                        wait_pos(sp, top_made, s + 1)
                    wait_pos(sp, e_ready, CHUNKS * s)
                    for g in range(GROUPS):
                        rows = slice(R * g, R * g + R)
                        for part, (khalf, qhalf) in enumerate(((k_hi, q_hi), (k_hi, q_lo), (k_lo, q_hi))):
                            at = slice(R * part, R * part + R)
                            sp.dma_start(Kst[v][at, g, :], khalf[rows, v, :]).then_inc(stacked[g], 16)
                            sp.dma_start(Qst[v][at, g, :, :], qhalf[rows, s + 1, :, :]).then_inc(stacked[g], 16)
                if has(s, -1, B - 3):
                    sp.wait_ge(ready["V"], 3 * (s + 2))
                    sp.wait_ge(loaded, 16 * N_LOADS)
                    sp.dma_start(ctxT[:, v, :], dram["ctxT"][s + 3]).then_inc(ctx_loaded[v], 16)

            in_steps(sp, first, last, loop_from, loop_to, step)

        @block.gpsimd
        def _(pool):
            fills = ((Kst[0][96:97, :, :], 1.0), (Kst[1][96:97, :, :], 1.0), (V3[:, :, :, :, 24:R], 0.0),
                     (V1[:, :, :, :, 8:R], 0.0), (V3[:, :, :, :, 24:25], 1.0), (V1[:, :, :, :, 24:25], 1.0))
            for n, (where, value) in enumerate(fills):
                wait_pos(pool, filled, n)
                nc.gpsimd.memset(where, value).then_inc(filled, 1)

        @block.tensor
        def _(pe):
            pe.wait_ge(loaded, 16 * N_LOADS)
            for k in range(NBLK):
                wait_pos(pe, q_lo_made, HG * (k - 1))
                nc.tensor.matmul(psE[:, 0, k % 2, 0:BLK], wq[:], xT[:, k * BLK:(k + 1) * BLK],
                                 start=True, stop=True).then_inc(q_ready, 1)
            pe.wait_ge(q_lo_made, NBLK * HG)
            pe.wait_ge(filled, 6)

            def values(s, u, i, k):
                v, unit = 1 - u, ("V", k)
                if k == 0:
                    pe.wait_ge(ctx_loaded[v], 8 * (s + 1 - v) + 16)
                units.wait_free(pe, s, u, i, unit)
                for c in range(4):
                    at = CHUNK * (4 * k + c)
                    mm = nc.tensor.matmul(ring[units.bank(u, unit)][0:CHUNK, 128 * c:128 * c + 128],
                                          ctxT[:, v, at:at + CHUNK], wv[:], start=True, stop=True)
                mm.then_inc(ready["V"], 1)

            def keys(s, u, i, k):
                unit = ("K", k)
                if k == 0:
                    pe.wait_ge(ctx_loaded[u], 8 * (s + 2 - u) + 16)
                units.wait_free(pe, s, u, i, unit)
                nc.tensor.matmul(ring[units.bank(u, unit)][:, 0:THIRD], wk[:], ctxT[:, u, THIRD * k:THIRD * (k + 1)],
                                 start=True, stop=True).then_inc(ready["K"], 1)

            def maxima(s, u, i, k):
                v, unit = 1 - u, ("max", k)
                tile, third = k // 3, k % 3
                g, half = tile // 2, tile % 2
                if k % 6 == 0:
                    pe.wait_ge(stacked[g], 96 * (s + 2))
                units.wait_free(pe, s, u, i, unit)
                nc.tensor.matmul(ring[units.bank(u, unit)][0:PT, 0:THIRD], Qst[v][0:96, g, 2 * half:2 * half + 2, :],
                                 Kst[v][0:96, g, THIRD * third:THIRD * (third + 1)],
                                 start=True, stop=True).then_inc(ready["max"], 1)

            def shift(s, u, i, k):
                unit = ("shift", k)
                if k == 0:
                    pe.wait_ge(top_made, s + 2)
                units.wait_free(pe, s, u, i, unit)
                for t in range(4):
                    mm = nc.tensor.matmul(ring[units.bank(u, unit)][96:128, PT * t:PT * (t + 1)],
                                          top[:, 4 * k + t:4 * k + t + 1].to_broadcast([PT, 32]),
                                          core.ident[0:PT, 0:PT], start=True, stop=True)
                mm.then_inc(ready["shift"], 1)

            def denominators(s, u, i):
                units.wait_free(pe, s, u, i, ("den", 0))
                pe.wait_ge(o_moved, s)
                nc.tensor.matmul(ring[units.bank(u, ("den", 0))][:, 0:BLK], sum_row[:], sums[:],
                                 start=True, stop=True).then_inc(ready["den"], 1)

            def output(s, u, i):
                units.wait_free(pe, s, u, i, ("y", 0))
                pe.wait_ge(heads_made, i)
                bank = ring[units.bank(u, ("y", 0))]
                for j in range(HG):
                    nc.tensor.matmul(bank[0:PT, 0:128], heads[:, j, :, :], wo[:, j, :], start=(j == 0), stop=False)
                nc.tensor.matmul(bank[0:PT, 0:128], core.first_row[:, 0:PT], bo[:],
                                 start=False, stop=True).then_inc(ready["y"], 1)

            def scores(s, u, i, c):
                n = CHUNKS * s + c
                if c == 0:
                    for k in range(2):
                        units.wait_read(pe, s - 1, i - (u == 0), ("shift", k))
                wait_pos(pe, p_ready, n - 1)
                for g in range(GROUPS):
                    mm = nc.tensor.matmul(psE[0:CHUNK, c % 2, g // 2, (g % 2) * GC:(g % 2 + 1) * GC],
                                          Kst[u][:, g, CHUNK * c:CHUNK * (c + 1)], Qst[u][:, g, :, :],
                                          start=True, stop=True)
                mm.then_inc(e_ready, 1)

            def weighted_values(s, u, i, c):
                n = CHUNKS * s + c
                if c == 0:
                    for k in range(3):
                        units.wait_read(pe, s - 1, i - (u == 0), ("V", k))
                    wait_pos(pe, o_moved, s)
                pe.wait_ge(p_ready, n + 1)
                for g in range(GROUPS):
                    nc.tensor.matmul(psO[R * g:R * g + R, 0:3, 0:S], V3[:, u, c, g, :], P[:, c % 3, g, 0:3 * S],
                                     start=(c == 0), stop=(c == CHUNKS - 1), skip_group_check=True)
                for g in range(GROUPS):
                    mm = nc.tensor.matmul(psO[R * g:R * g + R, 3, 0:S], V1[:, u, c, g, :], P[:, c % 3, g, 3 * S:4 * S],
                                          start=False, stop=(c == CHUNKS - 1), skip_group_check=True)
                mm.then_inc(av_done, 1)

            def step(s, u, i):
                main = has(s, 0, B)
                maxes = 0
                for c in range(CHUNKS):
                    if main:
                        scores(s, u, i, c)
                        if c > 0:
                            weighted_values(s, u, i, c - 1)
                    if c == 0 and units.has("V", s):
                        for k in range(3):
                            values(s, u, i, k)
                    if c == 1 and units.has("K", s):
                        for k in range(3):
                            keys(s, u, i, k)
                    if c == 1 and u == 0 and units.has("den", s):
                        denominators(s, u, i)
                    if 2 <= c <= 10 and units.has("max", s):
                        for _ in range(3 if c < 8 else 2):
                            if maxes == 5 and u == 0 and units.has("y", s):
                                output(s, u, i)
                            maxima(s, u, i, maxes)
                            maxes += 1
                    if c == 4 and u == 0 and units.has("y", s) and not units.has("max", s):
                        output(s, u, i)
                if units.has("shift", s):
                    for k in range(2):
                        shift(s, u, i, k)
                if main:
                    weighted_values(s, u, i, CHUNKS - 1)

            in_steps(pe, first, last, loop_from, loop_to, step)

        @block.vector
        def _(dve):
            dve.wait_ge(loaded, 16 * N_LOADS)
            for k in range(NBLK):
                src = psE[:, 0, k % 2, 0:BLK].rearrange("p (b q) -> p b q", q=S)
                for j in range(HG):
                    n = k * HG + j
                    if j == 0:
                        dve.wait_ge(q_ready, k + 1)
                    nc.vector.tensor_scalar(q_hi[:, 8 * k:8 * k + 8, j, :], src, head_in_group[:, j:j + 1], None,
                                            ALU.mult).then_inc(q_hi_made, 1)
                    dve.wait_ge(q_hi_made, n + 1)
                    nc.vector.scalar_tensor_tensor(q_lo[:, 8 * k:8 * k + 8, j, :], src, head_in_group[:, j:j + 1],
                                                   q_hi[:, 8 * k:8 * k + 8, j, :], ALU.mult,
                                                   ALU.subtract).then_inc(q_lo_made, 1)

            def step(s, u, i):
                v = 1 - u
                if has(s, 1, B + 1):
                    dve.wait_ge(av_done, CHUNKS * s)
                    nc.vector.tensor_copy(sums[:, :, v, :], psO[:, :, 0:S]).then_inc(o_moved, 1)
                for kind, k in Units.ORDER[u]:
                    if not units.has(kind, s):
                        continue
                    unit = (kind, k)
                    bank = ring[units.bank(u, unit)]
                    if kind == "K":
                        dve.wait_ge(k_hi_made, units.count("K", k, s, i))
                        at = slice(THIRD * k, THIRD * (k + 1))
                        nc.vector.tensor_tensor(k_lo[:, u, at], bank[:, 0:THIRD], k_hi[:, u, at],
                                                ALU.subtract).then_inc(read["K"], 1)
                    elif kind == "max":
                        units.wait_ready(dve, s, i, unit)
                        if k == 0:
                            wait_pos(dve, top_made, s + 1)
                        nc.vector.tensor_reduce(thirds[:, k // 3, k % 3:k % 3 + 1], bank[0:PT, 0:THIRD], AX.X,
                                                ALU.max).then_inc(read["max"], 1)
                    elif kind == "den":
                        units.wait_ready(dve, s, i, unit)
                        wait_pos(dve, heads_made, i - 1)
                        nc.vector.reciprocal(rden[:].rearrange("p a b c -> p (a b c)"), bank[:, 0:BLK]).then_inc(read["den"], 1)
                        units.wait_read(dve, s, i, unit)
                        dve.wait_ge(o_moved, s)
                        wait_pos(dve, ready["y"], i - 1)
                        nc.vector.tensor_tensor(heads[:], sums[:], rden[:], ALU.mult).then_inc(heads_made, 1)
                    elif kind == "y":
                        units.wait_ready(dve, s, i, unit)
                        nc.vector.tensor_tensor(x[:, i - 1, :], bank[0:PT, 0:128], x[:, i - 1, :],
                                                ALU.add).then_inc(read["y"], 1)
                if units.has("max", s):
                    units.wait_read(dve, s, i, ("max", 23))
                    wait_pos(dve, ready["shift"], 2 * (s + 1))
                    nc.vector.tensor_reduce(top[:], thirds[:], AX.X, ALU.max).then_inc(top_made, 1)

            in_steps(dve, first, last, loop_from, loop_to, step)

        @block.scalar
        def _(act):
            act.wait_ge(filled, 6)

            def step(s, u, i):
                v = 1 - u

                def move_values(k):
                    unit = ("V", k)
                    units.wait_ready(act, s, i, unit)
                    wait_pos(act, av_done, CHUNKS * s)
                    src = ring[units.bank(u, unit)][0:CHUNK, :].rearrange("p (c g r) -> p c g r", c=4, g=GROUPS)
                    nc.scalar.copy(V3[:, v, 4 * k:4 * k + 4, :, 0:24], src[:, :, :, 0:24])
                    nc.scalar.copy(V1[:, v, 4 * k:4 * k + 4, :, 0:8], src[:, :, :, 24:32]).then_inc(read["V"], 1)

                def move_keys(k):
                    unit = ("K", k)
                    units.wait_ready(act, s, i, unit)
                    if has(s, 0, B):
                        for g in range(GROUPS):
                            act.wait_ge(stacked[g], 96 * (s + 1))
                    nc.scalar.copy(k_hi[:, u, THIRD * k:THIRD * (k + 1)],
                                   ring[units.bank(u, unit)][:, 0:THIRD]).then_inc(k_hi_made, 1)

                for c in range(CHUNKS):
                    if has(s, 0, B):
                        n = CHUNKS * s + c
                        act.wait_ge(e_ready, n + 1)
                        wait_pos(act, av_done, n - 2)
                        nc.scalar.activation(P[:, c % 3, :, :].rearrange("p (a g) n -> p a (g n)", a=2),
                                             psE[0:CHUNK, c % 2, :, 0:2 * GC], ACT.Exp,
                                             scale=HEAD_SCALE).then_inc(p_ready, 1)
                    for k in range(3):
                        if c == 0 and units.has("V", s):
                            move_values(k)
                        if c == 1 and units.has("K", s):
                            move_keys(k)
                if units.has("shift", s):
                    for k in range(2):
                        unit = ("shift", k)
                        units.wait_ready(act, s, i, unit)
                        wait_pos(act, e_ready, CHUNKS * s)
                        nc.scalar.activation(Qst[v][96:97, 2 * k:2 * k + 2, :, :].rearrange("p a b c -> p (a b c)"),
                                             ring[units.bank(u, unit)][96:97, 0:BLK], ACT.Copy,
                                             scale=-1.0).then_inc(read["shift"], 1)

            in_steps(act, first, last, loop_from, loop_to, step)


E = 8
TOP2_CAPACITY = -(-2 * TOK * 5 // (E * 4))
CHOICE = TOK // E


def chain(nc, sem):
    made = [0]

    def link(instruction):
        made[0] += 1
        instruction.then_inc(sem, 1)

    def wait():
        nc.vector.wait_ge(sem, made[0])

    return link, wait


def router_logits(core, pe, w, bank, bias_row, ready):
    nc = core.nc
    for t in range(PAIRS):
        mm = nc.tensor.matmul(bank[0:PT, E * t:E * t + E], core.xT[:, PT * t:PT * (t + 1)], w[:],
                              start=True, stop=bias_row is None)
        if bias_row is not None:
            mm = nc.tensor.matmul(bank[0:PT, E * t:E * t + E], core.first_row[:, 0:PT], bias_row[:],
                                  start=False, stop=True)
    mm.then_inc(ready, 1)


def over_experts(tile):
    return tile[:].unsqueeze(2).to_broadcast([PT, PAIRS, E])


def top2_experts(core):
    nc, dram, x, xT = core.nc, core.dram, core.x, core.xT
    F = 256
    with ExitStack() as ctx:
        sb, ps, sem = tools(nc, ctx)
        wg = sb("m0_wg", [128, E])
        w_in = sb("m0_w_in", [128, E, 2 * F])
        w_out = sb("m0_w_out", [128, E, 2, D])
        tri = sb("m0_tri", [128, 128])
        rank = sb("m0_rank", [PT, E])
        ones = sb("m0_ones", [PT, PT])
        small = [PT, PAIRS, E]
        prob, work, first, second, kept = (sb(f"m0_{n}", small) for n in ("prob", "work", "first", "second", "kept"))
        gates = sb("m0_gates", small)
        col = sb("m0_col", [PT, PAIRS])
        first_count = sb("m0_first_count", [PT, E])
        act_out = sb("m0_act_out", [128, 2, BLK])
        hidden = sb("m0_hidden", [128, 2, 2, BLK])

        psR = ps("m0_psR", [128, 512])
        psC = ps("m0_psC", [128, 512])
        psH = [ps(f"m0_psH{k}", [128, 2, 512]) for k in range(2)]
        psY = [ps(f"m0_psY{k}", [128, 512]) for k in range(2)]

        loaded, logits_ready, chained, shifted, exp_made, first_made, second_made, counted = (sem(f"m0_{n}") for n in (
            "loaded", "logits_ready", "chained", "shifted", "exp_made", "first_made", "second_made", "counted"))
        h_ready, gelu_made, hidden_made, y_ready, y_added, gates_made = (sem(f"m0_{n}") for n in (
            "h_ready", "gelu_made", "hidden_made", "y_ready", "y_added", "gates_made"))
        block = ctx.enter_context(nc.Block())
        N_LOADS = 6

        @block.sync
        def _(sp):
            for dst, name in ((wg, "m0_wg"), (tri, "tri"), (rank, "rank"), (ones, "ones"), (w_in, "m0_w_in"),
                              (w_out, "m0_w_out")):
                sp.dma_start(dst[:], dram[name]).then_inc(loaded, 16)

        def outputs(pe, n, e):
            pe.wait_ge(hidden_made, 16 * n + 2 * e + 2)
            if e >= 2:
                pe.wait_ge(y_added, 8 * n + e - 1)
            else:
                wait_pos(pe, y_added, 8 * n)
            for t in range(4):
                for c in range(2):
                    mm = nc.tensor.matmul(psY[e % 2][0:PT, 128 * t:128 * t + 128],
                                          hidden[:, e % 2, c, PT * t:PT * (t + 1)], w_out[:, e, c, :],
                                          start=(c == 0), stop=(c == 1))
            mm.then_inc(y_ready, 1)

        @block.tensor
        def _(pe):
            pe.wait_ge(loaded, 16 * N_LOADS)
            router_logits(core, pe, wg, psR, None, logits_ready)
            for n, (chosen, made) in enumerate(((first, first_made), (second, second_made))):
                pe.wait_ge(made, 1)
                if n == 1:
                    pe.wait_ge(first_made, 3)
                nc.tensor.matmul(psC[0:PT, 0:128], tri[0:PT, 0:PT], chosen[:], start=True, stop=False,
                                 skip_group_check=True)
                for t in range(PAIRS - 1):
                    mm = nc.tensor.matmul(psC[0:PT, E * (t + 1):128], ones[:],
                                          chosen[:, t, :].unsqueeze(1).to_broadcast([PT, PAIRS - 1 - t, E]),
                                          start=False, stop=t == PAIRS - 2, skip_group_check=True)
                if n == 1:
                    mm = nc.tensor.matmul(psC[0:PT, 0:128], ones[:],
                                          first_count[:].unsqueeze(1).to_broadcast([PT, PAIRS, E]),
                                          start=False, stop=True, skip_group_check=True)
                mm.then_inc(counted, 1)

            def block_of_tokens(n):
                for e in range(E):
                    for c in range(2):
                        at = 2 * e + c
                        if at >= 2:
                            pe.wait_ge(hidden_made, 16 * n + at - 1)
                        else:
                            wait_pos(pe, hidden_made, 16 * n)
                        for g in range(2):
                            mm = nc.tensor.matmul(psH[c][:, g, 0:BLK],
                                                  w_in[:, e, F * g + 128 * c:F * g + 128 * (c + 1)],
                                                  xT[:, bass.ds(BLK * n, BLK)], start=True, stop=True)
                        mm.then_inc(h_ready, 1)
                        if c == 1 and e >= 1:
                            outputs(pe, n, e - 1)
                outputs(pe, n, E - 1)

            in_blocks(pe, NBLK, block_of_tokens)

        @block.scalar
        def _(act):
            act.wait_ge(shifted, 1)
            nc.scalar.activation(prob[:], prob[:], ACT.Exp).then_inc(exp_made, 1)
            def block_of_tokens(n):
                for e in range(E):
                    for c in range(2):
                        at = 2 * e + c
                        act.wait_ge(h_ready, 16 * n + at + 1)
                        if at >= 2:
                            act.wait_ge(hidden_made, 16 * n + at - 1)
                        else:
                            wait_pos(act, hidden_made, 16 * n)
                        nc.scalar.activation(act_out[:, c, :], psH[c][:, 0, 0:BLK], ACT.Gelu).then_inc(gelu_made, 1)

            in_blocks(act, NBLK, block_of_tokens)

        @block.vector
        def _(dve):
            link, wait = chain(nc, chained)
            vec = nc.vector
            logits = psR[0:PT, 0:128].rearrange("p (t e) -> p t e", e=E)
            counts = psC[0:PT, 0:128].rearrange("p (t e) -> p t e", e=E)
            ranks = rank[:].unsqueeze(1).to_broadcast([PT, PAIRS, E])
            dve.wait_ge(logits_ready, 1)
            link(vec.tensor_reduce(col[:], logits, AX.X, ALU.max))
            wait()
            vec.tensor_tensor(prob[:], logits, over_experts(col), ALU.subtract).then_inc(shifted, 1)
            dve.wait_ge(exp_made, 1)
            link(vec.tensor_reduce(col[:], prob[:], AX.X, ALU.add))
            wait()
            link(vec.reciprocal(col[:], col[:]))
            wait()
            link(vec.tensor_tensor(prob[:], prob[:], over_experts(col), ALU.mult))
            wait()
            for n, (chosen, made) in enumerate(((first, first_made), (second, second_made))):
                source = prob if n == 0 else work
                link(vec.tensor_reduce(col[:], source[:], AX.X, ALU.max))
                wait()
                link(vec.tensor_tensor(kept[:], source[:], over_experts(col), ALU.is_equal))
                wait()
                link(vec.tensor_tensor(kept[:], kept[:], ranks, ALU.mult))
                wait()
                link(vec.tensor_reduce(col[:], kept[:], AX.X, ALU.max))
                wait()
                vec.tensor_tensor(chosen[:], kept[:], over_experts(col), ALU.is_equal).then_inc(made, 1)
                dve.wait_ge(made, 1)
                if n == 0:
                    link(vec.scalar_tensor_tensor(work[:].rearrange("p t e -> p (t e)"),
                                                  first[:].rearrange("p t e -> p (t e)"), -2.0,
                                                  prob[:].rearrange("p t e -> p (t e)"), ALU.mult, ALU.add))
                    wait()
            vec.tensor_reduce(first_count[:], first[:].rearrange("p t e -> p e t"), AX.X, ALU.add).then_inc(first_made, 1)
            dve.wait_ge(counted, 1)
            link(vec.scalar_tensor_tensor(work[:], counts, float(TOP2_CAPACITY), first[:], ALU.is_le, ALU.mult))
            wait()
            dve.wait_ge(first_made, 2)
            vec.tensor_copy(kept[:], work[:]).then_inc(first_made, 1)
            dve.wait_ge(counted, 2)
            link(vec.scalar_tensor_tensor(work[:], counts, float(TOP2_CAPACITY), second[:], ALU.is_le, ALU.mult))
            wait()
            dve.wait_ge(first_made, 3)
            link(vec.tensor_tensor(kept[:], kept[:], work[:], ALU.add))
            wait()
            link(vec.tensor_tensor(gates[:], prob[:], kept[:], ALU.mult))
            wait()
            link(vec.tensor_reduce(col[:], gates[:], AX.X, ALU.add))
            wait()
            link(vec.tensor_scalar(col[:], col[:], 1e-9, None, ALU.max))
            wait()
            link(vec.reciprocal(col[:], col[:]))
            wait()
            vec.tensor_tensor(gates[:], gates[:], over_experts(col), ALU.mult).then_inc(gates_made, 1)
            dve.wait_ge(gates_made, 1)

            def add_outputs(n, e):
                dve.wait_ge(y_ready, 8 * n + e + 1)
                if e >= 1:
                    dve.wait_ge(y_added, 8 * n + e)
                for t in range(4):
                    add = vec.scalar_tensor_tensor(x[:, 4 * n + t, :], psY[e % 2][0:PT, 128 * t:128 * t + 128],
                                                   gates[:, 4 * n + t, e:e + 1], x[:, 4 * n + t, :],
                                                   ALU.mult, ALU.add)
                add.then_inc(y_added, 1)

            def block_of_tokens(n):
                for e in range(E):
                    for c in range(2):
                        dve.wait_ge(gelu_made, 16 * n + 2 * e + c + 1)
                        if e >= 2:
                            dve.wait_ge(y_ready, 8 * n + e - 1)
                        else:
                            wait_pos(dve, y_ready, 8 * n)
                        vec.tensor_tensor(hidden[:, e % 2, c, :], act_out[:, c, :], psH[c][:, 1, 0:BLK],
                                          ALU.mult).then_inc(hidden_made, 1)
                    if e >= 1:
                        add_outputs(n, e - 1)
                add_outputs(n, E - 1)

            in_blocks(dve, NBLK, block_of_tokens)

def masked_attention(core):
    nc, dram, x, xT = core.nc, core.dram, core.x, core.xT
    scale = float(D) ** -0.5
    with ExitStack() as ctx:
        sb, ps, sem = tools(nc, ctx)
        wq, wk, wv, bv = (sb(f"c1_{n}", [128, 128]) for n in ("wq", "wk", "wv", "bv"))
        cols = sb("c1_cols", [128, 2])
        Q = sb("c1_Q", [128, B, QP])
        QK = sb("c1_QK", [128, B, QP])
        q_bk = sb("c1_q_bk", [128, PAIRS])
        qk_pair = sb("c1_qk_pair", [128, 2, 2, QP])
        ctxT = sb("c1_ctxT", [128, 2, 2, SK])
        rows = sb("c1_rows", [CHUNK, 2, 2, CHUNKS, D])
        mask_words = sb("c1_mask", [128, 2, SK // 4], I32)
        mask = mask_words[:].rearrange("p u w -> p (u w)").bitcast(U8).rearrange("p (u n) -> p u n", u=2)
        masked = sb("c1_masked", [128, SK])
        P = sb("c1_P", [128, 2, SK])
        PTr = sb("c1_PTr", [CHUNK, CHUNKS, 128])
        top, down, total, rden = (sb(f"c1_{n}", [128, 2]) for n in ("top", "down", "total", "rden"))
        OT = sb("c1_OT", [128, 2, S])

        psS = ps("c1_psS", [128, 3, 512])
        psT = ps("c1_psT", [128, 3, 512])
        psO = ps("c1_psO", [128, 512])
        psY = ps("c1_psY", [128, 512])

        loaded, filled, q_ready, q_made, qk_ready, qk_made, b_ready, b_made = (sem(f"c1_{n}") for n in (
            "loaded", "filled", "q_ready", "q_made", "qk_ready", "qk_made", "b_ready", "b_made"))
        ctx_loaded, rows_loaded, mask_loaded = ([sem(f"c1_{n}_loaded{v}") for v in range(2)]
                                                for n in ("ctx", "rows", "mask"))
        pair_ready, down_cleared, s_ready, s_moved, s_masked, top_made, down_made, p_made, rden_made, p_ready = (sem(f"c1_{n}") for n in (
            "pair_ready", "down_cleared", "s_ready", "s_moved", "s_masked", "top_made", "down_made", "p_made", "rden_made", "p_ready"))
        t_ready, t_moved, o_ready, o_moved, y_ready, y_added = (sem(f"c1_{n}") for n in (
            "t_ready", "t_moved", "o_ready", "o_moved", "y_ready", "y_added"))
        block = ctx.enter_context(nc.Block())
        N_LOADS = 5

        @block.sync
        def _(sp):
            for dst, name in ((wq, "c1_wq"), (wk, "c1_wk"), (wv, "c1_wv"), (bv, "c1_bv"), (cols, "c1_cols")):
                sp.dma_start(dst[:], dram[name]).then_inc(loaded, 16)
            sp.wait_ge(filled, 2)

            def step(t, u, i):
                if not has(t, 0, PAIRS):
                    return
                wait_pos(sp, s_ready, t - 1)
                for b in range(2):
                    sp.dma_start(ctxT[:, u, b, :], dram["ctxT"][2 * t + b]).then_inc(ctx_loaded[u], 16)
                wait_pos(sp, s_masked, t - 1)
                for b in range(2):
                    sp.dma_start(mask_words[QP * b:QP * b + S, u, :], dram["mask"][2 * t + b]).then_inc(mask_loaded[u], 16)
                wait_pos(sp, o_ready, t - 1)
                for b in range(2):
                    sp.dma_start(rows[:, u, b, :, :],
                                 dram["ctx"][2 * t + b].rearrange("(p c) d -> p c d", c=CHUNKS)).then_inc(rows_loaded[u], 16)

            in_steps(sp, 0, PAIRS, 4, PAIRS, step)

        @block.gpsimd
        def _(pool):
            nc.gpsimd.memset(mask_words[:], 0).then_inc(filled, 1)
            pool.wait_ge(filled, 1)
            nc.gpsimd.memset(Q[:, :, S:QP], 0.0).then_inc(filled, 1)
            pool.wait_ge(filled, 2)
            nc.gpsimd.memset(masked[:], NEG / scale).then_inc(filled, 1)

        @block.tensor
        def _(pe):
            pe.wait_ge(loaded, 16 * N_LOADS)
            pe.wait_ge(filled, 3)
            for k in range(NBLK):
                nc.tensor.matmul(psS[:, k, 0:BLK] if k < 3 else psO[:, 0:BLK], wq[:], xT[:, k * BLK:(k + 1) * BLK],
                                 start=True, stop=True).then_inc(q_ready, 1)
            for k in range(NBLK):
                pe.wait_ge(q_made, k + 1)
                nc.tensor.matmul(psT[:, k, :] if k < 3 else psY[:, :], wk[:], Q[:, 8 * k:8 * k + 8, :],
                                 start=True, stop=True).then_inc(qk_ready, 1)
            for t in range(PAIRS):
                mm = nc.tensor.matmul(psO[:, t:t + 1], Q[:, 2 * t:2 * t + 2, :], cols[:, 1:2], start=True, stop=True)
            mm.then_inc(b_ready, 1)
            pe.wait_ge(qk_made, NBLK)
            pe.wait_ge(b_made, 1)

            def step(t, u, i):
                v = 1 - u
                if has(t, 0, PAIRS):
                    pe.wait_ge(ctx_loaded[u], 32 * i + 32)
                    pe.wait_ge(pair_ready, t + 1)
                    wait_pos(pe, s_moved, t)
                    for b in range(2):
                        for k in range(3):
                            mm = nc.tensor.matmul(psS[QP * b:QP * (b + 1), k, 0:THIRD], qk_pair[:, u, b, :],
                                                  ctxT[:, u, b, THIRD * k:THIRD * (k + 1)], start=True, stop=True)
                    mm.then_inc(s_ready, 1)
                if has(t, 1, PAIRS + 1):
                    pe.wait_ge(p_ready, t)
                    for k in range(3):
                        wait_pos(pe, t_moved, 3 * (t - 2) + k + 1)
                        for c in range(4 * k, 4 * k + 4):
                            mm = nc.tensor.transpose(psT[0:CHUNK, k, (c % 4) * 128:(c % 4 + 1) * 128],
                                                     P[:, v, c:SK:CHUNKS], core.ident[:])
                        mm.then_inc(t_ready, 1)
                if has(t, 2, PAIRS + 2):
                    pe.wait_ge(o_moved, t - 1)
                    wait_pos(pe, y_added, t - 2)
                    nc.tensor.matmul(psY[0:PT, 0:128], OT[:], wv[:], start=True, stop=False)
                    nc.tensor.matmul(psY[0:PT, 0:128], core.first_row[:, 0:PT], bv[:],
                                     start=False, stop=True).then_inc(y_ready, 1)
                if has(t, 1, PAIRS + 1):
                    pe.wait_ge(rows_loaded[v], 32 * (i - (u == 0)) + 32)
                    wait_pos(pe, o_moved, t - 1)
                    for c in range(CHUNKS):
                        if c % 4 == 0:
                            pe.wait_ge(t_moved, 3 * (t - 1) + c // 4 + 1)
                        for b in range(2):
                            mm = nc.tensor.matmul(psO[:, S * b:S * (b + 1)], rows[:, v, b, c, :],
                                                  PTr[:, c, QP * b:QP * b + S], start=(c == 0 and b == 0),
                                                  stop=(c == CHUNKS - 1), skip_group_check=True)
                    mm.then_inc(o_ready, 1)

            in_steps(pe, 0, PAIRS + 2, 4, PAIRS, step)

        @block.vector
        def _(dve):
            dve.wait_ge(filled, 2)
            dve.wait_ge(loaded, 16 * N_LOADS)
            for k in range(NBLK):
                dve.wait_ge(q_ready, k + 1)
                src = psS[:, k, 0:BLK] if k < 3 else psO[:, 0:BLK]
                nc.vector.tensor_scalar(Q[:, 8 * k:8 * k + 8, 0:S], src.rearrange("p (b s) -> p b s", s=S),
                                        cols[:, 0:1], None, ALU.add).then_inc(q_made, 1)
            for k in range(NBLK):
                dve.wait_ge(qk_ready, k + 1)
                nc.vector.tensor_copy(QK[:, 8 * k:8 * k + 8, :].rearrange("p b s -> p (b s)"),
                                      psT[:, k, :] if k < 3 else psY[:, :]).then_inc(qk_made, 1)
            dve.wait_ge(b_ready, 1)
            nc.vector.tensor_copy(q_bk[:], psO[:, 0:PAIRS]).then_inc(b_made, 1)
            dve.wait_ge(filled, 3)

            def step(t, u, i):
                v = 1 - u
                if has(t, 1, PAIRS + 1):
                    dve.wait_ge(p_made, t)
                    nc.vector.reciprocal(rden[:, v:v + 1], total[:, v:v + 1]).then_inc(rden_made, 1)
                    dve.wait_ge(rden_made, t)
                    nc.vector.tensor_scalar(P[:, v, :], P[:, v, :], rden[:, v:v + 1], None, ALU.mult).then_inc(p_ready, 1)
                if has(t, 0, PAIRS):
                    dve.wait_ge(mask_loaded[u], 32 * i + 32)
                    dve.wait_ge(s_moved, t + 1)
                    wait_pos(dve, p_made, t - 1)
                    nc.vector.memset(down[:, u:u + 1], 0.0).then_inc(down_cleared, 1)
                    nc.vector.copy_predicated(P[:, u, :], mask[:, u, :], masked[:]).then_inc(s_masked, 1)
                    dve.wait_ge(s_masked, t + 1)
                    wait_pos(dve, down_made, t - 1)
                    nc.vector.tensor_reduce(top[:, u:u + 1], P[:, u, :], AX.X, ALU.max).then_inc(top_made, 1)
                    dve.wait_ge(top_made, t + 1)
                    dve.wait_ge(down_cleared, t + 1)
                    nc.vector.tensor_scalar(down[:, u:u + 1], top[:, u:u + 1], -scale, None, ALU.mult).then_inc(down_made, 1)
                if has(t, 2, PAIRS + 2):
                    dve.wait_ge(y_ready, t - 1)
                    nc.vector.tensor_tensor(x[:, t - 2, :], psY[0:PT, 0:128], x[:, t - 2, :], ALU.add).then_inc(y_added, 1)

            in_steps(dve, 0, PAIRS + 2, 4, PAIRS, step)

        @block.scalar
        def _(act):
            act.wait_ge(qk_made, NBLK)
            act.wait_ge(b_made, 1)

            def step(t, u, i):
                v = 1 - u
                if has(t, 0, PAIRS):
                    wait_pos(act, s_ready, t - 1)
                    nc.scalar.copy(qk_pair[:, u, :, :], QK[:, bass.ds(2 * t, 2), :]).then_inc(pair_ready, 1)
                    act.wait_ge(s_ready, t + 1)
                    wait_pos(act, t_ready, t - 1)
                    nc.scalar.activation(P[:, u, :].rearrange("p (a n) -> p a n", a=3), psS[:, :, 0:THIRD], ACT.Identity,
                                         bias=q_bk[:, bass.ds(t, 1)]).then_inc(s_moved, 1)
                if has(t, 1, PAIRS + 1):
                    wait_pos(act, o_ready, t - 1)
                    for k in range(3):
                        act.wait_ge(t_ready, 3 * (t - 1) + k + 1)
                        nc.scalar.copy(PTr[:, 4 * k:4 * k + 4, :].rearrange("p c q -> p (c q)"),
                                       psT[0:CHUNK, k, :]).then_inc(t_moved, 1)
                if has(t, 0, PAIRS):
                    act.wait_ge(down_made, t + 1)
                    wait_pos(act, rden_made, t - 1)
                    nc.scalar.activation(P[:, u, :], P[:, u, :], ACT.Exp, bias=down[:, u:u + 1], scale=scale,
                                         accum_out=total[:, u:u + 1]).then_inc(p_made, 1)
                if has(t, 1, PAIRS + 1):
                    act.wait_ge(o_ready, t)
                    wait_pos(act, y_ready, t - 1)
                    nc.scalar.copy(OT[:].rearrange("p b s -> p (b s)"), psO[:, 0:PT]).then_inc(o_moved, 1)

            in_steps(act, 0, PAIRS + 1, 4, PAIRS, step)


def choosing_experts(core):
    nc, dram, x, xT = core.nc, core.dram, core.x, core.xT
    FC = 4
    BITS = 30
    with ExitStack() as ctx:
        sb, ps, sem = tools(nc, ctx)
        ws = sb("m1_ws", [128, E])
        bs = sb("m1_bs", [128, E])
        b1 = sb("m1_b1", [128, E, FC])
        w1 = sb("m1_w1", [128, E, FC, 128])
        w2 = sb("m1_w2", [128, E, FC, D])
        b2 = sb("m1_b2", [128, PAIRS, D])
        same = sb("m1_same", [128, 128])
        before = sb("m1_before", [128, 128])
        prob = sb("m1_prob", [PT, PAIRS, E])
        col = sb("m1_col", [PT, PAIRS])
        pT = sb("m1_pT", [128, PT])
        marks = sb("m1_marks", [128, PT])
        equal = sb("m1_equal", [128, PT])
        order = sb("m1_order", [128, PT])
        count = sb("m1_count", [128, 1])
        equals = sb("m1_equals", [128, 1])
        room = sb("m1_room", [128, 1])
        earlier = sb("m1_earlier", [128, 1])
        prefix, bit, tried, taken = (sb(f"m1_{n}", [128, 1], I32) for n in ("prefix", "bit", "tried", "taken"))
        gatesT = sb("m1_gatesT", [128, PT])
        gates = sb("m1_gates", [PT, PAIRS, E])
        hidden = sb("m1_hidden", [128, 2, FC, BLK])

        psR = ps("m1_psR", [128, 512])
        psH = [ps(f"m1_psH{k}", [128, 512]) for k in range(4)]
        psY = [ps(f"m1_psY{k}", [128, 512]) for k in range(2)]

        loaded, logits_ready, chained, shifted, exp_made, prob_made, pT_ready, pT_made = (sem(f"m1_{n}") for n in (
            "loaded", "logits_ready", "chained", "shifted", "exp_made", "prob_made", "pT_ready", "pT_made"))
        bits_set, tried_made, counted, count_ready, taken_made, prefix_made, bit_halved = (sem(f"m1_{n}") for n in (
            "bits_set", "tried_made", "counted", "count_ready", "taken_made", "prefix_made", "bit_halved"))
        asked, answered, gatesT_made, gates_ready, gates_made, b2_ready, b2_added = (sem(f"m1_{n}") for n in (
            "asked", "answered", "gatesT_made", "gates_ready", "gates_made", "b2_ready", "b2_added"))
        h_ready, gelu_made, y_ready, y_added = (sem(f"m1_{n}") for n in ("h_ready", "gelu_made", "y_ready", "y_added"))
        block = ctx.enter_context(nc.Block())
        loads = ((ws, "m1_ws"), (bs, "m1_bs"), (b1, "m1_b1"), (same, "same"), (before, "before"),
                 (w1, "m1_w1"), (w2, "m1_w2"), (b2, "m1_b2"))

        @block.sync
        def _(sp):
            for dst, name in loads:
                sp.dma_start(dst[:], dram[name]).then_inc(loaded, 16)

        def outputs(pe, n, e):
            pe.wait_ge(gelu_made, 32 * n + FC * (e + 1))
            if e >= 2:
                pe.wait_ge(y_added, 8 * n + e - 1)
            else:
                wait_pos(pe, y_added, 8 * n)
            for t in range(4):
                for c in range(FC):
                    mm = nc.tensor.matmul(psY[e % 2][0:PT, 128 * t:128 * t + 128],
                                          hidden[:, e % 2, c, PT * t:PT * (t + 1)], w2[:, e, c, :],
                                          start=(c == 0), stop=(c == FC - 1))
            mm.then_inc(y_ready, 1)

        @block.tensor
        def _(pe):
            pe.wait_ge(loaded, 16 * len(loads))
            router_logits(core, pe, ws, psR, bs, logits_ready)
            pe.wait_ge(prob_made, 1)
            nc.tensor.transpose(psR[:, 128:128 + PT], prob[:].rearrange("p t e -> p (t e)"),
                                core.ident[0:PT, 0:PT]).then_inc(pT_ready, 1)
            with pe.Fori(0, BITS) as n:
                pe.wait_ge(counted, n + 1)
                nc.tensor.matmul(psR[:, 256:257], same[:], count[:], start=True, stop=True).then_inc(count_ready, 1)
            pe.wait_ge(asked, 1)
            nc.tensor.matmul(psR[:, 257:258], same[:], count[:], start=True, stop=True)
            nc.tensor.matmul(psR[:, 258:259], before[:], equals[:], start=True, stop=True).then_inc(answered, 1)
            pe.wait_ge(gatesT_made, 1)
            nc.tensor.transpose(psR[0:PT, 384:512], gatesT[:], core.ident[:]).then_inc(gates_ready, 1)
            for k in range(4):
                for t in range(4):
                    mm = nc.tensor.matmul(psH[k][0:PT, 128 * t:128 * t + 128], gatesT[:], b2[:, 4 * k + t, :],
                                          start=True, stop=True)
                mm.then_inc(b2_ready, 1)
            pe.wait_ge(b2_added, 4)

            def block_of_tokens(n):
                for e in range(E):
                    for c in range(FC):
                        at = FC * e + c
                        if at >= 4:
                            pe.wait_ge(gelu_made, 32 * n + at - 3)
                        else:
                            wait_pos(pe, gelu_made, 32 * n)
                        nc.tensor.matmul(psH[c][:, 0:BLK], w1[:, e, c, :], xT[:, bass.ds(BLK * n, BLK)],
                                         start=True, stop=True).then_inc(h_ready, 1)
                    if e >= 1:
                        outputs(pe, n, e - 1)
                outputs(pe, n, E - 1)

            in_blocks(pe, NBLK, block_of_tokens)

        @block.scalar
        def _(act):
            act.wait_ge(shifted, 1)
            nc.scalar.activation(prob[:], prob[:], ACT.Exp).then_inc(exp_made, 1)
            def block_of_tokens(n):
                for e in range(E):
                    for c in range(FC):
                        act.wait_ge(h_ready, 32 * n + FC * e + c + 1)
                        if e >= 2:
                            act.wait_ge(y_ready, 8 * n + e - 1)
                        else:
                            wait_pos(act, y_ready, 8 * n)
                        nc.scalar.activation(hidden[:, e % 2, c, :], psH[c][:, 0:BLK], ACT.Gelu_apprx_tanh,
                                             bias=b1[:, e, c:c + 1]).then_inc(gelu_made, 1)

            in_blocks(act, NBLK, block_of_tokens)

        @block.vector
        def _(dve):
            link, wait = chain(nc, chained)
            vec = nc.vector
            logits = psR[0:PT, 0:128].rearrange("p (t e) -> p t e", e=E)
            dve.wait_ge(logits_ready, 1)
            link(vec.tensor_reduce(col[:], logits, AX.X, ALU.max))
            wait()
            vec.tensor_tensor(prob[:], logits, over_experts(col), ALU.subtract).then_inc(shifted, 1)
            link(vec.memset(prefix[:], 0))
            link(vec.memset(bit[:], 1 << (BITS - 1)))
            dve.wait_ge(exp_made, 1)
            link(vec.tensor_reduce(col[:], prob[:], AX.X, ALU.add))
            wait()
            link(vec.reciprocal(col[:], col[:]))
            wait()
            vec.tensor_tensor(prob[:], prob[:], over_experts(col), ALU.mult).then_inc(prob_made, 1)
            dve.wait_ge(pT_ready, 1)
            link(vec.tensor_copy(pT[:], psR[:, 128:128 + PT]))
            wait()
            def test_bit(n):
                wait_pos(dve, prefix_made, n)
                wait_pos(dve, bit_halved, n)
                vec.tensor_tensor(tried[:], prefix[:], bit[:], ALU.bitwise_or).then_inc(tried_made, 1)
                dve.wait_ge(tried_made, n + 1)
                vec.tensor_scalar(marks[:], pT[:], tried[:].bitcast(F32), 0.0, ALU.is_ge, ALU.add,
                                  accum_out=count[:]).then_inc(counted, 1)
                dve.wait_ge(count_ready, n + 1)
                vec.tensor_scalar(taken[:], psR[:, 256:257], float(CHOICE), bit[:], ALU.is_ge,
                                  ALU.mult).then_inc(taken_made, 1)
                dve.wait_ge(taken_made, n + 1)
                vec.tensor_tensor(prefix[:], prefix[:], taken[:], ALU.bitwise_or).then_inc(prefix_made, 1)
                vec.tensor_scalar(bit[:], bit[:], 1, None, ALU.logical_shift_right).then_inc(bit_halved, 1)

            in_blocks(dve, BITS, test_bit)
            dve.wait_ge(prefix_made, BITS)
            dve.wait_ge(bit_halved, BITS)
            threshold = prefix[:].bitcast(F32)
            link(vec.tensor_scalar(marks[:], pT[:], threshold, 0.0, ALU.is_gt, ALU.add, accum_out=count[:]))
            wait()
            vec.tensor_scalar(equal[:], pT[:], threshold, 0.0, ALU.is_equal, ALU.add,
                              accum_out=equals[:]).then_inc(asked, 1)
            dve.wait_ge(asked, 1)
            link(vec.tensor_tensor_scan(order[:], equal[:], equal[:], 0.0, ALU.add, ALU.max))
            dve.wait_ge(answered, 1)
            link(vec.tensor_scalar(room[:], psR[:, 257:258], -1.0, float(CHOICE), ALU.mult, ALU.add))
            wait()
            link(vec.tensor_scalar(order[:], order[:], psR[:, 258:259], None, ALU.add))
            wait()
            link(vec.scalar_tensor_tensor(order[:], order[:], room[:], equal[:], ALU.is_le, ALU.mult))
            wait()
            link(vec.tensor_tensor(marks[:], marks[:], order[:], ALU.add))
            wait()
            vec.tensor_tensor(gatesT[:], marks[:], pT[:], ALU.mult).then_inc(gatesT_made, 1)
            dve.wait_ge(gates_ready, 1)
            vec.tensor_copy(gates[:].rearrange("p t e -> p (t e)"), psR[0:PT, 384:512]).then_inc(gates_made, 1)
            for k in range(4):
                dve.wait_ge(b2_ready, k + 1)
                vec.tensor_tensor(x[:, 4 * k:4 * k + 4, :].rearrange("p t d -> p (t d)"), psH[k][0:PT, :],
                                  x[:, 4 * k:4 * k + 4, :].rearrange("p t d -> p (t d)"), ALU.add).then_inc(b2_added, 1)
            dve.wait_ge(b2_added, 4)
            dve.wait_ge(gates_made, 1)

            def block_of_tokens(n):
                for e in range(E):
                    dve.wait_ge(y_ready, 8 * n + e + 1)
                    if e >= 1:
                        dve.wait_ge(y_added, 8 * n + e)
                    for t in range(4):
                        add = vec.scalar_tensor_tensor(x[:, 4 * n + t, :], psY[e % 2][0:PT, 128 * t:128 * t + 128],
                                                       gates[:, 4 * n + t, e:e + 1], x[:, 4 * n + t, :],
                                                       ALU.mult, ALU.add)
                    add.then_inc(y_added, 1)

            in_blocks(dve, NBLK, block_of_tokens)

def program(nc, dram, out, stages=6):
    with ExitStack() as ctx:
        sb, ps, sem = tools(nc, ctx)
        core = Core(nc, dram)
        core.x = sb("x", [PT, PAIRS, D])
        core.xT = sb("xT", [128, TOK])
        core.ident = sb("ident", [128, 128])
        core.first_row = sb("first_row", [128, 128])
        load_inputs(core)
        self_attention(core, 0)
        layer_norm(core, "n0")
        context_attention(core)
        layer_norm(core, "n1")
        top2_experts(core)
        layer_norm(core, "n2")
        self_attention(core, 1)
        layer_norm(core, "n3")
        masked_attention(core)
        layer_norm(core, "n4")
        choosing_experts(core)
        layer_norm(core, "n5", out)




def shape_tables():
    f = np.float32
    p = np.arange(128)
    t = {"ident": np.eye(128, dtype=f), "first_row": np.zeros((128, 128), f)}
    t["first_row"][0] = 1.0
    t["head_of_row"] = (p[:, None] // DK == np.arange(H)[None]).astype(f)
    two = np.arange(PT)[:, None] // S
    t["vmask"] = ((p[None] // DK) % 2 == two).astype(f)
    ones = np.zeros((PT, 2, H, DK + 1), f)
    ones[:, :, :, DK] = (np.arange(H)[None, None] % 2 == two[:, :, None])
    t["vbd_ones"] = ones
    inv = (f(1.0) / f(10000.0) ** (np.arange(0, DK, 2, dtype=f) / f(DK))).astype(f)
    ang = np.arange(S, dtype=f)[:, None] * inv
    at = (p % DK) // 2
    t["rope_cos"] = np.cos(ang).astype(f).T[at]
    t["rope_sin"] = np.sin(ang).astype(f).T[at] * np.where(p % 2 == 0, -1, 1).astype(f)[:, None]
    causal = np.where(np.tril(np.ones((S, S), bool)), f(0), f(NEG))
    phi = (1.0 + np.sqrt(5.0)) / 2.0
    pos = (np.arange(S, dtype=f) * f(phi)) % f(1.0)
    dist = np.abs(pos[:, None] - pos[None, :])
    table = np.log(np.exp(-dist) + f(1e-8)) / f(HEAD_SCALE)
    for n, a in (("s0_bias", causal), ("s1_bias", table)):
        padded = np.zeros((2, QP, S), f)
        padded[:, :S] = a
        t[n] = padded.reshape(128, S)
    t["head_in_group"] = ((p[:, None] // DK) % HG == np.arange(HG)[None]).astype(f)
    t["tri"] = np.triu(np.ones((128, 128), f))
    t["ones"] = np.ones((PT, PT), f)
    t["rank"] = np.broadcast_to(E - np.arange(E, dtype=f), (PT, E))
    expert, pair = p % E, p // E
    t["same"] = (expert[:, None] == expert[None]).astype(f)
    t["before"] = t["same"] * (pair[:, None] < pair[None])
    t["c0_sum_row"] = (p[:, None] == (p // 32 * 32 + 24)[None]).astype(f)
    return t


def laid_out(i):
    f = np.float32
    swap = np.arange(128) ^ 1

    def row(v):
        out = np.zeros((128, 128), f)
        out[0] = v
        return out

    a = {"x": i["x"].reshape(TOK, D), "xT": i["x"].reshape(TOK, D).T}
    a["s0_wq"], a["s0_wk"], a["s0_wv"], a["s0_wo"] = (i[f"L0_attn_W{n}"].T for n in "qkvo")
    a["s0_wqs"], a["s0_wks"] = a["s0_wq"][:, swap], a["s0_wk"][:, swap]
    a["s0_bo"] = row(i["L0_attn_bo"])
    a["s0_cols"] = np.stack([i["L0_attn_bq"], i["L0_attn_bq"][swap], i["L0_attn_bk"], i["L0_attn_bk"][swap],
                             i["L0_attn_bv"]], axis=1)
    a["ctxT"] = i["ctx_1024"].transpose(0, 2, 1)
    a["c0_wq"], a["c0_wk"], a["c0_wv"] = (i[f"L0_xattn_W_{n}"].transpose(1, 0, 2).reshape(128, 128) for n in "qkv")
    wo = i["L0_xattn_W_o"].T.reshape(GROUPS, HG, DK, 128)
    padded = np.zeros((GROUPS, 32, HG, 128), f)
    for j in range(HG):
        at = DK * j if j < 3 else 0
        padded[:, at:at + DK, j, :] = wo[:, j]
    a["c0_wo"] = padded.reshape(128, HG, 128)
    a["c0_bo"] = row(i["L0_xattn_b_o"])
    a["m0_wg"] = i["L0_ffn_Wg"]
    a["m0_w_in"] = i["L0_ffn_W_in"].transpose(1, 0, 2)
    a["m0_w_out"] = i["L0_ffn_W_out"].reshape(E, 2, 128, D).transpose(2, 0, 1, 3)
    a["s1_wq"], a["s1_wk"], a["s1_wv"] = (i["L1_attn_w_qkv"][:, 128 * n:128 * n + 128] for n in range(3))
    a["s1_wo"], a["s1_bo"] = i["L1_attn_w_proj"], row(i["L1_attn_b_proj"])
    a["ctx"] = i["ctx_1024"]
    a["mask"] = i["mask_BxSxS2_bk1"].view(np.int32)
    a["c1_wq"], a["c1_wk"], a["c1_wv"] = i["L1_xattn_Wq"].T, i["L1_xattn_Wk"], i["L1_xattn_Wv"].T
    a["c1_bv"] = row(i["L1_xattn_bv"])
    a["c1_cols"] = np.stack([i["L1_xattn_bq"], i["L1_xattn_bk"]], axis=1)
    a["m1_ws"] = i["L1_ffn_Ws"]
    a["m1_bs"] = row8 = np.zeros((128, E), f)
    row8[0] = i["L1_ffn_bs"]
    a["m1_b1"] = i["L1_ffn_b1"].reshape(E, 4, 128).transpose(2, 0, 1)
    a["m1_w1"] = i["L1_ffn_W1"].reshape(E, D, 4, 128).transpose(1, 0, 2, 3)
    a["m1_w2"] = i["L1_ffn_W2"].reshape(E, 4, 128, D).transpose(2, 0, 1, 3)
    b2 = np.zeros((PAIRS, E, PAIRS, D), f)
    for t in range(PAIRS):
        b2[t, :, t] = i["L1_ffn_b2"]
    a["m1_b2"] = b2.reshape(128, PAIRS, D)
    return a


def kernel(**inputs):
    import concourse.bacc as bacc
    from concourse.bass_utils import run_bass_kernel_spmd

    inputs = {k: np.asarray(v) for k, v in inputs.items()}
    arrays = {f"in_{k}": np.ascontiguousarray(v) for k, v in {**laid_out(inputs), **shape_tables()}.items()}
    nc = bacc.Bacc("TRN2", target_bir_lowering=False, num_devices=1)
    dram = {k[3:]: nc.dram_tensor(k, v.shape, mybir.dt.from_np(v.dtype), kind="ExternalInput").ap()
            for k, v in arrays.items()}
    out = nc.dram_tensor("out", (TOK, D), F32, kind="ExternalOutput").ap()
    program(nc, dram, out)
    result = run_bass_kernel_spmd(nc, [arrays], core_ids=[0])
    return result.results[0]["out"].reshape(B, S, D)
```

```python
from contextlib import ExitStack

import numpy as np

import concourse.bass as bass
from concourse import mybir

F32 = mybir.dt.float32
F16 = mybir.dt.float16
BF16 = mybir.dt.bfloat16
I32 = mybir.dt.int32
U8 = mybir.dt.uint8
ALU = mybir.AluOpType
ACT = mybir.ActivationFunctionType
AX = mybir.AxisListType

B, S, D = 32, 56, 128
SK = 1500
H, DK = 16, 8
PAIRS = B // 2
PT = 2 * S
TOK = B * S
QP = 64
CHUNK = 125
CHUNKS = SK // CHUNK
GROUPS, HG = 4, 4
GC = HG * S
THIRD = SK // 3
HEAD_SCALE = float(DK) ** -0.5
LN_EPS = 1e-5
NEG = -1e9
BLK = 448
NBLK = TOK // BLK


def wait_pos(eng, sem, value):
    if isinstance(value, int) and value <= 0:
        return
    eng.wait_ge(sem, value)


def in_steps(eng, first, last, loop_from, loop_to, period, body):
    for s in range(first, loop_from):
        body(s, s % period, s // 2)
    with eng.Fori(loop_from // period, loop_to // period) as n:
        for u in range(period):
            body(period * n + u, u, period // 2 * n + u // 2)
    for s in range(loop_to, last):
        body(s, s % period, s // 2)


def in_blocks(eng, count, body):
    body(0)
    with eng.Fori(1, count) as n:
        body(n)


def has(s, low, high):
    return not isinstance(s, int) or low <= s < high


class Core:

    def __init__(self, nc, dram):
        self.nc, self.dram = nc, dram


def tools(nc, ctx):
    stage_sems = []

    @ctx.callback
    def _():
        nc.clear_and_free_semaphores(stage_sems)
        nc.all_engine_barrier()

    def sb(name, shape, dt=F32):
        return ctx.enter_context(nc.sbuf_tensor(name, shape, dt))

    def ps(name, shape, dt=F32):
        return ctx.enter_context(nc.psum_tensor(name, shape, dt))

    def sem(name):
        stage_sems.append(nc.alloc_semaphore(name))
        return stage_sems[-1]

    return sb, ps, sem


def load_inputs(core):
    nc, dram = core.nc, core.dram
    with ExitStack() as ctx:
        sb, ps, sem = tools(nc, ctx)
        loaded = sem("in_loaded")
        block = ctx.enter_context(nc.Block())

        @block.sync
        def _(sp):
            sp.dma_start(core.xT[:], dram["xT"]).then_inc(loaded, 16)
            sp.dma_start(core.x[:], dram["x"].rearrange("(t p) d -> p t d", p=PT)).then_inc(loaded, 16)
            sp.dma_start(core.ident[:], dram["ident"]).then_inc(loaded, 16)
            sp.dma_start(core.first_row[:], dram["first_row"]).then_inc(loaded, 16)
            sp.wait_ge(loaded, 64)


def layer_norm(core, tag, out=None):
    nc, x, xT = core.nc, core.x, core.xT
    with ExitStack() as ctx:
        sb, ps, sem = tools(nc, ctx)
        stats = sb(f"{tag}_stats", [PT, PAIRS, 6])
        mv = sb(f"{tag}_mv", [PT, PAIRS, 2])
        std = sb(f"{tag}_std", [PT, PAIRS])
        rstd = sb(f"{tag}_rstd", [PT, PAIRS])
        turned = [ps(f"{tag}_turned{k}", [128, 512]) for k in range(4)]
        stats_made, var_made, std_made, rstd_made = (sem(f"{tag}_{n}") for n in ("stats_s", "var_s", "std_s", "rstd_s"))
        normed, transposed, stored = (sem(f"{tag}_{n}") for n in ("normed", "transposed", "stored"))
        block = ctx.enter_context(nc.Block())

        @block.vector
        def _(dve):
            for t in range(PAIRS):
                nc.vector.bn_stats(stats[:, t, :], x[:, t, :]).then_inc(stats_made, 1)
            for t in range(PAIRS):
                dve.wait_ge(stats_made, t + 1)
                nc.vector.bn_aggr(mv[:, t, :], stats[:, t, :]).then_inc(stats_made, 1)
            dve.wait_ge(stats_made, 2 * PAIRS)
            nc.vector.tensor_scalar(std[:], mv[:, :, 1], LN_EPS, None, ALU.add).then_inc(var_made, 1)
            dve.wait_ge(std_made, 1)
            nc.vector.reciprocal(rstd[:], std[:]).then_inc(rstd_made, 1)
            dve.wait_ge(rstd_made, 1)
            for t in range(PAIRS):
                nc.vector.tensor_scalar(x[:, t, :], x[:, t, :], mv[:, t, 0:1], rstd[:, t:t + 1],
                                        ALU.subtract, ALU.mult).then_inc(normed, 1)

        @block.scalar
        def _(act):
            act.wait_ge(var_made, 1)
            nc.scalar.activation(std[:], std[:], ACT.Sqrt).then_inc(std_made, 1)
            if out is None:
                for k in range(4):
                    act.wait_ge(transposed, k + 1)
                    nc.scalar.copy(xT[:, k * BLK:(k + 1) * BLK], turned[k][:, 0:BLK])

        @block.tensor
        def _(pe):
            if out is None:
                for k in range(4):
                    pe.wait_ge(normed, 4 * k + 4)
                    for t in range(4):
                        mm = nc.tensor.transpose(turned[k][:, t * PT:(t + 1) * PT], x[:, 4 * k + t, :],
                                                 core.ident[0:PT, 0:PT])
                    mm.then_inc(transposed, 1)

        @block.sync
        def _(sp):
            if out is not None:
                for k in range(4):
                    sp.wait_ge(normed, 4 * k + 4)
                    sp.dma_start(out[4 * k * PT:4 * (k + 1) * PT, :].rearrange("(t p) d -> p t d", p=PT),
                                 x[:, 4 * k:4 * k + 4, :]).then_inc(stored, 16)
                sp.wait_ge(stored, 64)


def self_attention(core, layer):
    nc, dram, x, xT = core.nc, core.dram, core.x, core.xT
    rope = layer == 0
    L = f"s{layer}_"
    names = ["wq", "wqs", "wk", "wks", "wv", "wo", "bo"] if rope else ["wq", "wk", "wv", "wo", "bo"]
    with ExitStack() as ctx:
        sb, ps, sem = tools(nc, ctx)
        W = {n: sb(L + n, [128, 128]) for n in names}
        PARTS = 1 if rope else 3
        bias = sb(L + "bias", [128, PARTS, S])
        bias_parts = sb(L + "bias_parts", [128, PARTS, S], BF16)
        ident_bf16 = sb(L + "ident_bf16", [128, 128], BF16)
        head_of_row = sb(L + "head_of_row", [128, H])
        vmask = sb(L + "vmask", [PT, 128])
        if rope:
            cos, sin = sb(L + "cos", [128, S]), sb(L + "sin", [128, S])
            cols = sb(L + "cols", [128, 5])
            part_a, part_b = sb(L + "part_a", [128, BLK]), sb(L + "part_b", [128, BLK])
        Q = sb(L + "Q", [128, B, QP])
        K = sb(L + "K", [128, B, S])
        q_pair = sb(L + "q_pair", [128, 2, 2, QP])
        x_twice = sb(L + "x_twice", [128, 2, 2, 2, S])
        Kbd = sb(L + "Kbd", [128, 2, 2, H * S])
        Vbd = sb(L + "Vbd", [PT, 2, 2, H, DK + 1])
        P = sb(L + "P", [128, 2, H * S])
        PTr = sb(L + "PTr", [PT, H // 2, 128])
        top = sb(L + "top", [128, 2, H])
        rden = sb(L + "rden", [128, 2, H])
        O = sb(L + "O", [128, 2, 128])
        OT = sb(L + "OT", [128, 2, PT])

        psS = ps(L + "psS", [128, 2, 512])
        psT = ps(L + "psT", [128, 2, 512])
        psV = ps(L + "psV", [128, 512])
        psO = ps(L + "psO", [128, 512])
        psOT = ps(L + "psOT", [128, 512])
        psY = ps(L + "psY", [128, 512])

        first_loaded, loaded, padded, parts_made = (sem(L + n) for n in ("first_loaded", "loaded", "padded", "parts_made"))
        proj_ready, proj_used, rope_parts = (sem(L + n) for n in ("proj_ready", "proj_used", "rope_parts"))
        xs_ready, kbd_ready, v_ready, vbd_ready, s_ready, top_ready, s_used, p_ready = (sem(L + n) for n in (
            "xs_ready", "kbd_ready", "v_ready", "vbd_ready", "s_ready", "top_ready", "s_used", "p_ready"))
        t_ready, t_moved, o_ready, rden_ready, o_moved, ot_ready, ot_moved, y_ready, y_used = (sem(L + n) for n in (
            "t_ready", "t_moved", "o_ready", "rden_ready", "o_moved", "ot_ready", "ot_moved", "y_ready", "y_used"))
        block = ctx.enter_context(nc.Block())
        first = {n: W[n] for n in ("wq", "wqs", "wk", "wks") if n in W}
        later = {"wv": W["wv"], "wo": W["wo"], "bo": W["bo"], "bias": bias}
        FIRST_LOADS, LOADS = len(first) + (3 if rope else 0), len(later) + 4
        steps = (-1, PAIRS + 2, 4, PAIRS - 2, 2)
        projections = [("wq", "wqs", 0, Q), ("wk", "wks", 2, K)]
        banks = [psS[:, 0, :], psS[:, 1, :], psT[:, 0, :], psT[:, 1, :]]

        @block.sync
        def _(sp):
            for n, dst in first.items():
                sp.dma_start(dst[:], dram[L + n]).then_inc(first_loaded, 16)
            if rope:
                sp.dma_start(cos[:], dram["rope_cos"]).then_inc(first_loaded, 16)
                sp.dma_start(sin[:], dram["rope_sin"]).then_inc(first_loaded, 16)
                sp.dma_start(cols[:], dram["s0_cols"]).then_inc(first_loaded, 16)
            sp.dma_start(head_of_row[:], dram["head_of_row"]).then_inc(loaded, 16)
            sp.dma_start(vmask[:], dram["vmask"]).then_inc(loaded, 16)
            for n, dst in later.items():
                sp.dma_start(dst[:], dram[L + n]).then_inc(loaded, 16)
            for u in range(2):
                sp.dma_start(Vbd[:, u, :, :, :], dram["vbd_ones"]).then_inc(loaded, 16)

        @block.gpsimd
        def _(pool):
            nc.gpsimd.memset(Q[:, :, S:QP], 0.0).then_inc(padded, 1)
            pool.wait_ge(loaded, 16 * LOADS)
            pool.wait_ge(proj_used, 2 * NBLK)

            def step(t, u, i):
                if has(t, 0, PAIRS):
                    wait_pos(pool, s_ready, 2 * (t - 1))
                    for b in range(2):
                        nc.gpsimd.tensor_tensor(
                            Kbd[:, u, b, :].rearrange("p (h k) -> p h k", h=H),
                            K[:, 2 * t + b, :].unsqueeze(1).to_broadcast([128, H, S]),
                            head_of_row[:].unsqueeze(2).to_broadcast([128, H, S]), ALU.mult).then_inc(kbd_ready, 1)

            in_steps(pool, 0, PAIRS, 2, PAIRS, 2, step)

        @block.tensor
        def _(pe):
            pe.wait_ge(first_loaded, 16 * FIRST_LOADS)
            for n, (w, ws, _, _) in enumerate(projections):
                for k in range(NBLK):
                    m = n * NBLK + k
                    wait_pos(pe, proj_used, m - (1 if rope else 3))
                    if rope:
                        nc.tensor.matmul(banks[2 * (m % 2)][:, 0:BLK], W[w][:], xT[:, k * BLK:(k + 1) * BLK],
                                         start=True, stop=True)
                        nc.tensor.matmul(banks[2 * (m % 2) + 1][:, 0:BLK], W[ws][:], xT[:, k * BLK:(k + 1) * BLK],
                                         start=True, stop=True).then_inc(proj_ready, 1)
                    else:
                        nc.tensor.matmul(banks[m % 4][:, 0:BLK], W[w][:], xT[:, k * BLK:(k + 1) * BLK],
                                         start=True, stop=True).then_inc(proj_ready, 1)
            pe.wait_ge(proj_used, 2 * NBLK)
            pe.wait_ge(loaded, 16 * LOADS)
            pe.wait_ge(parts_made, 2)

            def step(t, u, i):
                v = 1 - u
                if has(t, 2, PAIRS + 2):
                    pe.wait_ge(o_moved, t - 1)
                    wait_pos(pe, ot_moved, t - 2)
                    nc.tensor.transpose(psOT[:, 0:128], O[:, u, :], core.ident[:]).then_inc(ot_ready, 1)
                if has(t, 1, PAIRS + 1):
                    for half in range(2):
                        pe.wait_ge(p_ready, 2 * t - 1 + half)
                        wait_pos(pe, t_moved, 2 * t - 3 + half)
                        for hp in range(4):
                            at = half * BLK + hp * PT
                            mm = nc.tensor.transpose(psT[0:PT, half, hp * 128:(hp + 1) * 128], P[:, v, at:at + PT],
                                                     core.ident[:])
                        mm.then_inc(t_ready, 1)
                if has(t, 0, PAIRS):
                    pe.wait_ge(xs_ready, t + 1)
                    pe.wait_ge(kbd_ready, 2 * t + 2)
                    for half in range(2):
                        wait_pos(pe, s_used, 2 * t - 1 + half)
                        for part in range(PARTS):
                            nc.tensor.matmul(psS[:, half, 0:BLK], ident_bf16[:],
                                             bias_parts[:, part, :].unsqueeze(1).to_broadcast([128, H // 2, S]),
                                             start=(part == 0), stop=False, skip_group_check=True)
                        for b in range(2):
                            mm = nc.tensor.matmul(psS[QP * b:QP * (b + 1), half, 0:BLK], q_pair[:, u, b, :],
                                                  Kbd[:, u, b, half * BLK:(half + 1) * BLK],
                                                  start=False, stop=True, skip_group_check=True)
                        mm.then_inc(s_ready, 1)
                if has(t, 2, PAIRS + 2):
                    pe.wait_ge(ot_moved, t - 1)
                    wait_pos(pe, y_used, t - 2)
                    nc.tensor.matmul(psY[0:PT, 0:128], OT[:, u, :], W["wo"][:], start=True, stop=False)
                    nc.tensor.matmul(psY[0:PT, 0:128], core.first_row[:, 0:PT], W["bo"][:],
                                     start=False, stop=True).then_inc(y_ready, 1)
                if has(t, 1, PAIRS + 1):
                    pe.wait_ge(t_moved, 2 * t)
                    pe.wait_ge(vbd_ready, t)
                    wait_pos(pe, o_moved, t - 1)
                    for b in range(2):
                        for hp in range(H // 2):
                            mm = nc.tensor.matmul(
                                psO[QP * b:QP * (b + 1), hp * 18:(hp + 1) * 18], PTr[:, hp, QP * b:QP * (b + 1)],
                                Vbd[:, v, b, 2 * hp:2 * hp + 2, :], start=True, stop=True)
                    mm.then_inc(o_ready, 1)
                if has(t, -1, PAIRS - 1):
                    pe.wait_ge(xs_ready, t + 2)
                    wait_pos(pe, vbd_ready, t + 1)
                    for b in range(2):
                        mm = nc.tensor.matmul(psV[0:PT, b * 128:(b + 1) * 128], x_twice[:, v, b, :, :], W["wv"][:],
                                              start=True, stop=True)
                    mm.then_inc(v_ready, 1)

            in_steps(pe, *steps, step)

        @block.vector
        def _(dve):
            dve.wait_ge(first_loaded, 16 * FIRST_LOADS)
            for n, (_, _, col, dest) in enumerate(projections):
                for k in range(NBLK):
                    m = n * NBLK + k
                    dve.wait_ge(proj_ready, m + 1)
                    if not rope:
                        nc.vector.tensor_copy(dest[:, 8 * k:8 * k + 8, 0:S],
                                              banks[m % 4][:, 0:BLK].rearrange("p (b s) -> p b s", b=8)).then_inc(proj_used, 1)
                        continue
                    wait_pos(dve, proj_used, m)
                    for w, part, table in ((0, part_a, cos), (1, part_b, sin)):
                        nc.vector.scalar_tensor_tensor(
                            part[:].rearrange("p (b s) -> p b s", b=8),
                            banks[2 * (m % 2) + w][:, 0:BLK].rearrange("p (b s) -> p b s", b=8),
                            cols[:, col + w:col + w + 1], table[:].unsqueeze(1).to_broadcast([128, 8, S]),
                            ALU.add, ALU.mult).then_inc(rope_parts, 1)
                    dve.wait_ge(rope_parts, 2 * m + 2)
                    nc.vector.tensor_tensor(dest[:, 8 * k:8 * k + 8, 0:S], part_a[:].rearrange("p (b s) -> p b s", b=8),
                                            part_b[:].rearrange("p (b s) -> p b s", b=8), ALU.add).then_inc(proj_used, 1)

            def step(t, u, i):
                v = 1 - u
                if has(t, 0, PAIRS):
                    for half in range(2):
                        dve.wait_ge(s_ready, 2 * t + half + 1)
                        scores = psS[:, half, 0:BLK].rearrange("p (h k) -> p h k", k=S)
                        heads = top[:, u, H // 2 * half:H // 2 * (half + 1)]
                        nc.vector.tensor_reduce(heads, scores, AX.X, ALU.max).then_inc(top_ready, 1)
                        dve.wait_ge(top_ready, 2 * t + half + 1)
                        nc.vector.tensor_tensor(P[:, u, BLK * half:BLK * (half + 1)].rearrange("p (h k) -> p h k", k=S),
                                                scores, heads.unsqueeze(2).to_broadcast([128, H // 2, S]),
                                                ALU.subtract).then_inc(s_used, 1)
                if has(t, 2, PAIRS + 2):
                    dve.wait_ge(y_ready, t - 1)
                    nc.vector.tensor_tensor(x[:, t - 2, :], psY[0:PT, 0:128], x[:, t - 2, :],
                                            ALU.add).then_inc(y_used, 1)
                if has(t, 1, PAIRS + 1):
                    dve.wait_ge(o_ready, t)
                    sums = psO[:, 0:144].rearrange("p (h d) -> p h d", h=H)
                    nc.vector.reciprocal(rden[:, v, :], sums[:, :, DK]).then_inc(rden_ready, 1)
                    dve.wait_ge(rden_ready, t)
                    wait_pos(dve, ot_ready, t - 2)
                    nc.vector.tensor_tensor(O[:, v, :].rearrange("p (h d) -> p h d", h=H), sums[:, :, 0:DK],
                                            rden[:, v, :].unsqueeze(2).to_broadcast([128, H, DK]),
                                            ALU.mult).then_inc(o_moved, 1)
                if has(t, -1, PAIRS - 1):
                    dve.wait_ge(v_ready, t + 2)
                    wait_pos(dve, o_ready, t)
                    for b in range(2):
                        vbd = nc.vector.tensor_tensor(Vbd[:, v, b, :, 0:DK],
                                                     psV[0:PT, b * 128:(b + 1) * 128].rearrange("p (h d) -> p h d", h=H),
                                                     vmask[:].rearrange("p (h d) -> p h d", h=H), ALU.mult)
                    vbd.then_inc(vbd_ready, 1)

            in_steps(dve, *steps, step)

        @block.scalar
        def _(act):
            act.wait_ge(loaded, 16 * LOADS)
            nc.scalar.copy(ident_bf16[:], core.ident[:]).then_inc(parts_made, 1)
            nc.scalar.copy(bias_parts[:], bias[:]).then_inc(parts_made, 1)
            act.wait_ge(padded, 1)
            act.wait_ge(proj_used, 2 * NBLK)

            def step(t, u, i):
                v = 1 - u
                if has(t, 2, PAIRS + 2):
                    act.wait_ge(ot_ready, t - 1)
                    wait_pos(act, y_ready, t - 2)
                    dst = OT[:, u, :].rearrange("p (b s) -> p b s", b=2)
                    src = psOT[:, 0:128].rearrange("p (b s) -> p b s", b=2)[:, :, 0:S]
                    if rope:
                        nc.scalar.activation(dst, src, ACT.Identity, bias=cols[:, 4:5]).then_inc(ot_moved, 1)
                    else:
                        nc.scalar.copy(dst, src).then_inc(ot_moved, 1)
                if has(t, 1, PAIRS + 1):
                    for half in range(2):
                        act.wait_ge(t_ready, 2 * t - 1 + half)
                        wait_pos(act, o_ready, t - 1)
                        nc.scalar.copy(PTr[:, 4 * half:4 * half + 4, :],
                                       psT[0:PT, half, :].rearrange("p (h c) -> p h c", c=128)).then_inc(t_moved, 1)
                if has(t, -1, PAIRS - 1):
                    wait_pos(act, s_ready, 2 * t)
                    wait_pos(act, v_ready, t)
                    nc.scalar.copy(q_pair[:, v, :, :], Q[:, bass.ds(2 * (t + 1), 2), :])
                    nc.scalar.copy(x_twice[:, v, :, :, :],
                                   xT[:, bass.ds(PT * (t + 1), PT)].rearrange("p (b s) -> p b s", b=2).unsqueeze(2)
                                   .to_broadcast([128, 2, 2, S])).then_inc(xs_ready, 1)
                if has(t, 0, PAIRS):
                    for half in range(2):
                        act.wait_ge(s_used, 2 * t + half + 1)
                        part = P[:, u, BLK * half:BLK * (half + 1)]
                        nc.scalar.activation(part, part, ACT.Exp, scale=HEAD_SCALE).then_inc(p_ready, 1)

            in_steps(act, *steps, step)


def units_by_chunk(plan, h):
    chunks = []
    for c in range(CHUNKS):
        others = [(kind, k) for kind, k in plan.get(c, []) if h == 0 or kind not in ("den", "y")]
        before = [unit for unit in others if unit[0] in ("den", "shift")]
        chunks.append(before + [("max", 2 * c)] + [unit for unit in others if unit not in before]
                      + [("max", 2 * c + 1)])
    return chunks


class Units:

    RING = 3
    PER_STEP = {"V": 3, "K": 3, "max": 2 * CHUNKS, "shift": 2, "den": 1, "y": 1}
    PLAN = {0: [("K", 0)], 1: [("K", 1)], 2: [("shift", 0), ("shift", 1)], 3: [("K", 2)], 4: [("den", 0)],
            5: [("V", 0)], 7: [("V", 1)], 9: [("V", 2)], 10: [("y", 0)]}
    CHUNK_UNITS = [units_by_chunk(PLAN, 0), units_by_chunk(PLAN, 1)]
    ORDER = [[unit for chunk in chunks for unit in chunk] for chunks in CHUNK_UNITS]
    PAIR = ORDER[0] + ORDER[1]
    assert len(PAIR) % RING == 0

    def __init__(self, ready, read):
        self.ready, self.read = ready, read

    @staticmethod
    def has(kind, s):
        low, high = {"V": (-1, B - 1), "K": (-3, B - 3), "max": (-2, B - 2), "shift": (-1, B - 1),
                     "den": (2, B + 1), "y": (2, B + 1)}[kind]
        return has(s, low, high)

    def bank(self, h, unit):
        return (h * len(self.ORDER[0]) + self.ORDER[h].index(unit)) % self.RING

    def count(self, kind, k, s, i):
        turn = {"V": s + 1, "K": s + 3, "max": s + 2, "shift": s + 1, "den": i - 1, "y": i - 1}[kind]
        return self.PER_STEP[kind] * turn + k + 1

    def wait_free(self, eng, s, h, i, unit):
        at = h * len(self.ORDER[0]) + self.ORDER[h].index(unit)
        back = 0
        while True:
            at -= self.RING
            if at < 0:
                at += len(self.PAIR)
                back += 1
                if isinstance(s, int) and i - back < -2:
                    return
            kind, k = self.PAIR[at]
            v = int(at >= len(self.ORDER[0]))
            before = s - h - 2 * back + v
            if self.has(kind, before):
                return wait_pos(eng, self.read[kind], self.count(kind, k, before, i - back))

    def wait_ready(self, eng, s, i, unit):
        eng.wait_ge(self.ready[unit[0]], self.count(*unit, s, i))

    def wait_read(self, eng, s, i, unit):
        eng.wait_ge(self.read[unit[0]], self.count(*unit, s, i))


def context_attention(core):
    nc, dram, x, xT = core.nc, core.dram, core.x, core.xT
    R = 32
    SLOTS = 4
    with ExitStack() as ctx:
        sb, ps, sem = tools(nc, ctx)
        wq, wk, wv, bo = (sb(f"c0_{n}", [128, 128]) for n in ("wq", "wk", "wv", "bo"))
        wo = sb("c0_wo", [128, HG, 128])
        sum_row = sb("c0_sum_row", [128, 128])
        head_in_group = sb("c0_head_in_group", [128, HG])
        q_hi, q_lo = sb("c0_q_hi", [128, B, HG, S], F16), sb("c0_q_lo", [128, B, HG, S], F16)
        ctxT = sb("c0_ctxT", [128, SLOTS, SK])
        k_hi, k_lo = sb("c0_k_hi", [128, 2, SK], F16), sb("c0_k_lo", [128, 2, SK], F16)
        Kst = [sb(f"c0_Kst{v}", [97, GROUPS, SK], F16) for v in range(SLOTS)]
        Qst = [sb(f"c0_Qst{v}", [97, GROUPS, HG, S], F16) for v in range(SLOTS)]
        V3 = sb("c0_V3", [CHUNK, 2, CHUNKS, GROUPS, R])
        V1 = sb("c0_V1", [CHUNK, 2, CHUNKS, GROUPS, R])
        P = sb("c0_P", [CHUNK, 3, GROUPS, GC])
        thirds = sb("c0_thirds", [PT, 8, 3])
        top = sb("c0_top", [PT, 8])
        sums = sb("c0_sums", [128, HG, 2, S])
        den = sb("c0_den", [128, HG, 2, S])
        rden = sb("c0_rden", [128, HG, 2, S])
        heads = sb("c0_heads", [128, HG, 2, S])

        psE = ps("c0_psE", [128, 2, 2, 512])
        psO = ps("c0_psO", [128, HG, S + 8])
        ring = [ps(f"c0_ring{k}", [128, 512]) for k in range(Units.RING)]

        first_loaded, loaded, filled = sem("c0_first_loaded"), sem("c0_loaded"), sem("c0_filled")
        q_ready, q_hi_made, q_lo_made = sem("c0_q_ready"), sem("c0_q_hi_made"), sem("c0_q_lo_made")
        ctx_loaded = [sem(f"c0_ctx_loaded{v}") for v in range(SLOTS)]
        stacked = [sem(f"c0_stacked{v}") for v in range(2)]
        rden_made = sem("c0_rden_made")
        k_hi_made, thirds_made, top_made = sem("c0_k_hi_made"), sem("c0_thirds_made"), sem("c0_top_made")
        e_ready, p_ready, av_done, o_moved, heads_made = (sem(f"c0_{n}") for n in (
            "e_ready", "p_ready", "av_done", "o_moved", "heads_made"))
        ready = {k: sem(f"c0_{k}_ready") for k in Units.PER_STEP}
        read = {k: sem(f"c0_{k}_read") for k in Units.PER_STEP}
        units = Units(ready, read)
        block = ctx.enter_context(nc.Block())
        FIRST_LOADS, LOADS = 3, 4
        STACK_DMAS = 6 * GROUPS
        FILLS = SLOTS + 4
        steps = (-3, B + 1, 4, B - 4, 4)

        def wait_stacked(eng, s, h, n):
            eng.wait_ge(stacked[(h + n) % 2], 8 * STACK_DMAS * (s + n - (h + n) % 2) + 16 * STACK_DMAS)

        @block.sync
        def _(sp):
            sp.dma_start(wk[:], dram["c0_wk"]).then_inc(first_loaded, 16)
            sp.dma_start(ctxT[:, 0, :], dram["ctxT"][0]).then_inc(ctx_loaded[0], 16)
            sp.dma_start(wq[:], dram["c0_wq"]).then_inc(first_loaded, 16)
            sp.dma_start(head_in_group[:], dram["head_in_group"]).then_inc(first_loaded, 16)
            for v in range(1, SLOTS):
                sp.dma_start(ctxT[:, v, :], dram["ctxT"][v]).then_inc(ctx_loaded[v], 16)
            for dst, name in ((wv, "c0_wv"), (bo, "c0_bo"), (wo, "c0_wo"), (sum_row, "c0_sum_row")):
                sp.dma_start(dst[:], dram[name]).then_inc(loaded, 16)

            def step(s, u, i):
                h = u % 2
                v, first = (u + 3) % SLOTS, isinstance(s, int) and s == -3

                def stack_keys():
                    units.wait_read(sp, s, i, ("K", 2))
                    for g in range(GROUPS):
                        for part, half in enumerate((k_hi, k_hi, k_lo)):
                            sp.dma_start(Kst[v][R * part:R * part + R, g, :],
                                         half[R * g:R * g + R, 1 - h, :]).then_inc(stacked[1 - h], 16)

                if first:
                    stack_keys()
                if units.has("K", s):
                    wait_pos(sp, e_ready, CHUNKS * s)
                    sp.wait_ge(q_lo_made, HG if first else NBLK * HG)
                    for g in range(GROUPS):
                        for part, half in enumerate((q_hi, q_lo, q_hi)):
                            sp.dma_start(Qst[v][R * part:R * part + R, g, :, :],
                                         half[R * g:R * g + R, s + 3, :, :]).then_inc(stacked[1 - h], 16)
                    if not first:
                        stack_keys()
                if has(s, 0, B - SLOTS):
                    sp.dma_start(ctxT[:, u, :], dram["ctxT"][s + SLOTS]).then_inc(ctx_loaded[u], 16)

            in_steps(sp, *steps, step)

        @block.gpsimd
        def _(pool):
            fills = (*((Kst[v][96:97, :, :], 1.0) for v in range(SLOTS)), (V3[:, :, :, :, 24:R], 0.0),
                     (V1[:, :, :, :, 8:R], 0.0), (V3[:, :, :, :, 24:25], 1.0), (V1[:, :, :, :, 24:25], 1.0))
            for n, (where, value) in enumerate(fills):
                wait_pos(pool, filled, n)
                nc.gpsimd.memset(where, value).then_inc(filled, 1)

        @block.tensor
        def _(pe):
            pe.wait_ge(first_loaded, 16 * FIRST_LOADS)

            def queries():
                for k in range(NBLK):
                    wait_pos(pe, q_lo_made, HG * (k - 1))
                    nc.tensor.matmul(psE[:, 0, k % 2, 0:BLK], wq[:], xT[:, k * BLK:(k + 1) * BLK],
                                     start=True, stop=True).then_inc(q_ready, 1)
                pe.wait_ge(q_lo_made, NBLK * HG)
                pe.wait_ge(filled, FILLS)
                pe.wait_ge(loaded, 16 * LOADS)

            def values(s, u, i, k):
                h, v, unit = u % 2, (u + 1) % SLOTS, ("V", k)
                units.wait_free(pe, s, h, i, unit)
                for c in range(4):
                    at = CHUNK * (4 * k + c)
                    mm = nc.tensor.matmul(ring[units.bank(h, unit)][0:CHUNK, 128 * c:128 * c + 128],
                                          ctxT[:, v, at:at + CHUNK], wv[:], start=True, stop=True)
                mm.then_inc(ready["V"], 1)

            def keys(s, u, i, k):
                h, v, unit = u % 2, (u + 3) % SLOTS, ("K", k)
                if k == 0:
                    pe.wait_ge(ctx_loaded[v], 4 * (s + 3 - v) + 16)
                units.wait_free(pe, s, h, i, unit)
                nc.tensor.matmul(ring[units.bank(h, unit)][:, 0:THIRD], wk[:], ctxT[:, v, THIRD * k:THIRD * (k + 1)],
                                 start=True, stop=True).then_inc(ready["K"], 1)

            def maxima(s, u, i, k):
                h, v, unit = u % 2, (u + 2) % SLOTS, ("max", k)
                tile, third = k // 3, k % 3
                g, half = tile // 2, tile % 2
                if k == 0:
                    wait_stacked(pe, s, h, 2)
                units.wait_free(pe, s, h, i, unit)
                nc.tensor.matmul(ring[units.bank(h, unit)][0:PT, 0:THIRD], Qst[v][0:96, g, 2 * half:2 * half + 2, :],
                                 Kst[v][0:96, g, THIRD * third:THIRD * (third + 1)],
                                 start=True, stop=True).then_inc(ready["max"], 1)

            def shift(s, u, i, k):
                h, unit = u % 2, ("shift", k)
                if k == 0:
                    pe.wait_ge(top_made, s + 2)
                units.wait_free(pe, s, h, i, unit)
                for t in range(4):
                    mm = nc.tensor.matmul(ring[units.bank(h, unit)][96:128, PT * t:PT * (t + 1)],
                                          top[:, 4 * k + t:4 * k + t + 1].to_broadcast([PT, 32]),
                                          core.ident[0:PT, 0:PT], start=True, stop=True)
                mm.then_inc(ready["shift"], 1)

            def denominators(s, u, i, k):
                h = u % 2
                units.wait_free(pe, s, h, i, ("den", 0))
                pe.wait_ge(o_moved, s)
                nc.tensor.matmul(ring[units.bank(h, ("den", 0))][:, 0:BLK], sum_row[:], sums[:],
                                 start=True, stop=True).then_inc(ready["den"], 1)

            def output(s, u, i, k):
                h = u % 2
                units.wait_free(pe, s, h, i, ("y", 0))
                pe.wait_ge(heads_made, i)
                bank = ring[units.bank(h, ("y", 0))]
                for j in range(HG):
                    nc.tensor.matmul(bank[0:PT, 0:128], heads[:, j, :, :], wo[:, j, :], start=(j == 0), stop=False)
                nc.tensor.matmul(bank[0:PT, 0:128], core.first_row[:, 0:PT], bo[:],
                                 start=False, stop=True).then_inc(ready["y"], 1)

            def scores(s, u, i, c):
                n = CHUNKS * s + c
                if c == 0:
                    units.wait_read(pe, s - 1, i, ("shift", 1))
                wait_pos(pe, p_ready, n - 1)
                for g in range(GROUPS):
                    mm = nc.tensor.matmul(psE[0:CHUNK, c % 2, g // 2, (g % 2) * GC:(g % 2 + 1) * GC],
                                          Kst[u][:, g, CHUNK * c:CHUNK * (c + 1)], Qst[u][:, g, :, :],
                                          start=True, stop=True)
                mm.then_inc(e_ready, 1)

            def weighted_values(s, u, i, c):
                n, h = CHUNKS * s + c, u % 2
                if c == 0:
                    units.wait_read(pe, s - 1, i, ("V", 2))
                    wait_pos(pe, o_moved, s)
                pe.wait_ge(p_ready, n + 1)
                for g in range(GROUPS):
                    nc.tensor.matmul(psO[R * g:R * g + R, 0:3, 0:S], V3[:, h, c, g, :], P[:, c % 3, g, 0:3 * S],
                                     start=(c == 0), stop=(c == CHUNKS - 1), skip_group_check=True)
                for g in range(GROUPS):
                    mm = nc.tensor.matmul(psO[R * g:R * g + R, 3, 0:S], V1[:, h, c, g, :], P[:, c % 3, g, 3 * S:4 * S],
                                          start=False, stop=(c == CHUNKS - 1), skip_group_check=True)
                mm.then_inc(av_done, 1)

            make = {"V": values, "K": keys, "max": maxima, "shift": shift, "den": denominators, "y": output}

            def step(s, u, i):
                for c in range(CHUNKS):
                    if has(s, 0, B):
                        scores(s, u, i, c)
                        if c > 0:
                            weighted_values(s, u, i, c - 1)
                    for kind, k in Units.CHUNK_UNITS[u % 2][c]:
                        if units.has(kind, s):
                            make[kind](s, u, i, k)
                if has(s, 0, B):
                    weighted_values(s, u, i, CHUNKS - 1)
                if isinstance(s, int) and s == -3:
                    queries()

            in_steps(pe, *steps, step)

        @block.vector
        def _(dve):
            dve.wait_ge(first_loaded, 16 * FIRST_LOADS)

            def queries():
                for k in range(NBLK):
                    src = psE[:, 0, k % 2, 0:BLK].rearrange("p (b q) -> p b q", q=S)
                    dve.wait_ge(q_hi_made, HG * (k + 1))
                    for j in range(HG):
                        nc.vector.scalar_tensor_tensor(q_lo[:, 8 * k:8 * k + 8, j, :], src, head_in_group[:, j:j + 1],
                                                       q_hi[:, 8 * k:8 * k + 8, j, :], ALU.mult,
                                                       ALU.subtract).then_inc(q_lo_made, 1)

            def step(s, u, i):
                h = u % 2
                if has(s, 1, B + 1):
                    dve.wait_ge(av_done, CHUNKS * s)
                    if h == 1:
                        wait_pos(dve, heads_made, i)
                    nc.vector.tensor_copy(sums[:, :, 1 - h, :], psO[:, :, 0:S]).then_inc(o_moved, 1)
                for c in range(CHUNKS):
                    for kind, k in Units.CHUNK_UNITS[h][c]:
                        if not units.has(kind, s):
                            continue
                        unit = (kind, k)
                        bank = ring[units.bank(h, unit)]
                        if kind == "K":
                            dve.wait_ge(k_hi_made, units.count("K", k, s, i))
                            at = slice(THIRD * k, THIRD * (k + 1))
                            nc.vector.tensor_tensor(k_lo[:, 1 - h, at], bank[:, 0:THIRD], k_hi[:, 1 - h, at],
                                                    ALU.subtract).then_inc(read["K"], 1)
                        elif kind == "max":
                            units.wait_ready(dve, s, i, unit)
                            if k == 0:
                                wait_pos(dve, top_made, s + 2)
                            nc.vector.tensor_reduce(thirds[:, k // 3, k % 3:k % 3 + 1], bank[0:PT, 0:THIRD], AX.X,
                                                    ALU.max).then_inc(read["max"], 1)
                        elif kind == "y":
                            units.wait_ready(dve, s, i, unit)
                            nc.vector.tensor_tensor(x[:, i - 1, :], bank[0:PT, 0:128], x[:, i - 1, :],
                                                    ALU.add).then_inc(read["y"], 1)
                    if h == 0 and units.has("den", s) and 5 <= c < 5 + HG:
                        j = c - 5
                        if j == 0:
                            units.wait_read(dve, s, i, ("den", 0))
                            wait_pos(dve, heads_made, i - 1)
                        nc.vector.reciprocal(rden[:, j, :, :], den[:, j, :, :]).then_inc(rden_made, 1)
                        if j == HG - 1:
                            dve.wait_ge(rden_made, HG * i)
                            dve.wait_ge(o_moved, s)
                            wait_pos(dve, ready["y"], i - 1)
                            nc.vector.tensor_tensor(heads[:], sums[:], rden[:], ALU.mult).then_inc(heads_made, 1)
                if units.has("max", s):
                    units.wait_read(dve, s, i, ("max", 2 * CHUNKS - 1))
                    wait_pos(dve, ready["shift"], 2 * (s + 2))
                    nc.vector.tensor_reduce(top[:], thirds[:], AX.X, ALU.max).then_inc(top_made, 1)
                if isinstance(s, int) and s == -3:
                    queries()

            in_steps(dve, *steps, step)

        @block.scalar
        def _(act):
            act.wait_ge(first_loaded, 16 * FIRST_LOADS)

            def queries():
                for k in range(NBLK):
                    src = psE[:, 0, k % 2, 0:BLK].rearrange("p (b q) -> p b q", q=S)
                    act.wait_ge(q_ready, k + 1)
                    for j in range(HG):
                        nc.scalar.activation(q_hi[:, 8 * k:8 * k + 8, j, :], src, ACT.Copy,
                                             scale=head_in_group[:, j:j + 1]).then_inc(q_hi_made, 1)
                act.wait_ge(filled, FILLS)

            def move_values(s, u, i, k):
                h, unit = u % 2, ("V", k)
                units.wait_ready(act, s, i, unit)
                wait_pos(act, av_done, CHUNKS * s)
                src = ring[units.bank(h, unit)][0:CHUNK, :].rearrange("p (c g r) -> p c g r", c=4, g=GROUPS)
                nc.scalar.copy(V3[:, 1 - h, 4 * k:4 * k + 4, :, 0:24], src[:, :, :, 0:24])
                nc.scalar.copy(V1[:, 1 - h, 4 * k:4 * k + 4, :, 0:8], src[:, :, :, 24:32]).then_inc(read["V"], 1)

            def move_keys(s, u, i, k):
                h, unit = u % 2, ("K", k)
                units.wait_ready(act, s, i, unit)
                if k == 0 and has(s, -1, B):
                    wait_stacked(act, s, h, 1)
                nc.scalar.copy(k_hi[:, 1 - h, THIRD * k:THIRD * (k + 1)],
                               ring[units.bank(h, unit)][:, 0:THIRD]).then_inc(k_hi_made, 1)

            def move_shift(s, u, i, k):
                h, unit = u % 2, ("shift", k)
                units.wait_ready(act, s, i, unit)
                nc.scalar.activation(Qst[(u + 1) % SLOTS][96:97, 2 * k:2 * k + 2, :, :].rearrange("p a b c -> p (a b c)"),
                                     ring[units.bank(h, unit)][96:97, 0:BLK], ACT.Copy,
                                     scale=-1.0).then_inc(read["shift"], 1)

            def move_denominators(s, u, i, k):
                units.wait_ready(act, s, i, ("den", 0))
                wait_pos(act, heads_made, i - 1)
                nc.scalar.copy(den[:].rearrange("p a b c -> p (a b c)"),
                               ring[units.bank(u % 2, ("den", 0))][:, 0:BLK]).then_inc(read["den"], 1)

            move = {"V": move_values, "K": move_keys, "shift": move_shift, "den": move_denominators}

            def step(s, u, i):
                for c in range(CHUNKS):
                    if has(s, 0, B):
                        n = CHUNKS * s + c
                        act.wait_ge(e_ready, n + 1)
                        wait_pos(act, av_done, n - 2)
                        nc.scalar.activation(P[:, c % 3, :, :].rearrange("p (a g) n -> p a (g n)", a=2),
                                             psE[0:CHUNK, c % 2, :, 0:2 * GC], ACT.Exp,
                                             scale=HEAD_SCALE).then_inc(p_ready, 1)
                    for kind, k in Units.CHUNK_UNITS[u % 2][c]:
                        if kind in move and units.has(kind, s):
                            move[kind](s, u, i, k)
                if isinstance(s, int) and s == -3:
                    queries()

            in_steps(act, *steps, step)


E = 8
TOP2_CAPACITY = -(-2 * TOK * 5 // (E * 4))
CHOICE = TOK // E
W_SCALE = 256.0


def chain(nc, sem):
    made = [0]

    def link(instruction):
        made[0] += 1
        instruction.then_inc(sem, 1)

    def wait():
        nc.vector.wait_ge(sem, made[0])

    return link, wait


def router_logits(core, pe, w, bank, bias_row, ready):
    nc = core.nc
    for t in range(PAIRS):
        mm = nc.tensor.matmul(bank[0:PT, E * t:E * t + E], core.xT[:, PT * t:PT * (t + 1)], w[:],
                              start=True, stop=bias_row is None)
        if bias_row is not None:
            mm = nc.tensor.matmul(bank[0:PT, E * t:E * t + E], core.first_row[:, 0:PT], bias_row[:],
                                  start=False, stop=True)
    mm.then_inc(ready, 1)


def over_experts(tile):
    return tile[:].unsqueeze(2).to_broadcast([PT, PAIRS, E])


def top2_experts(core):
    nc, dram, x, xT = core.nc, core.dram, core.x, core.xT
    F = 256
    with ExitStack() as ctx:
        sb, ps, sem = tools(nc, ctx)
        wg = sb("m0_wg", [128, E])
        w_in = sb("m0_w_in", [128, E, 2 * F])
        w_hi, w_lo = (sb(f"m0_w_{n}", [128, E, 2 * F], F16) for n in ("hi", "lo"))
        x_hi, x_lo = (sb(f"m0_x_{n}", [128, TOK], F16) for n in ("hi", "lo"))
        w_out = sb("m0_w_out", [128, E, 2, D])
        tri = sb("m0_tri", [128, 128])
        rank = sb("m0_rank", [PT, E])
        ones = sb("m0_ones", [PT, PT])
        small = [PT, PAIRS, E]
        prob, work, first, second, kept = (sb(f"m0_{n}", small) for n in ("prob", "work", "first", "second", "kept"))
        gates = sb("m0_gates", small)
        col = sb("m0_col", [PT, PAIRS])
        first_count = sb("m0_first_count", [PT, E])
        act_out = sb("m0_act_out", [128, 2, BLK])
        hidden = sb("m0_hidden", [128, 2, 2, BLK])

        psR = ps("m0_psR", [128, 512])
        psC = ps("m0_psC", [128, 512])
        psH = [ps(f"m0_psH{k}", [128, 2, 512]) for k in range(2)]
        psY = [ps(f"m0_psY{k}", [128, 512]) for k in range(2)]

        loaded, logits_ready, chained, shifted, exp_made, first_made, second_made, counted = (sem(f"m0_{n}") for n in (
            "loaded", "logits_ready", "chained", "shifted", "exp_made", "first_made", "second_made", "counted"))
        h_ready, gelu_made, hidden_made, y_ready, y_added, gates_made = (sem(f"m0_{n}") for n in (
            "h_ready", "gelu_made", "hidden_made", "y_ready", "y_added", "gates_made"))
        w_in_loaded = [sem(f"m0_w_in_loaded{k}") for k in range(2)]
        w_in_scaled = sem("m0_w_in_scaled")
        w_out_loaded, x_hi_made, x_lo_made, w_hi_made, w_lo_made = (sem(f"m0_{n}") for n in (
            "w_out_loaded", "x_hi_made", "x_lo_made", "w_hi_made", "w_lo_made"))
        block = ctx.enter_context(nc.Block())
        N_LOADS = 4

        @block.sync
        def _(sp):
            for dst, name in ((wg, "m0_wg"), (tri, "tri"), (rank, "rank"), (ones, "ones")):
                sp.dma_start(dst[:], dram[name]).then_inc(loaded, 16)
            for k in range(2):
                half = slice(E // 2 * k, E // 2 * (k + 1))
                sp.dma_start(w_in[:, half], dram["m0_w_in"][:, half]).then_inc(w_in_loaded[k], 16)
            sp.dma_start(w_out[:], dram["m0_w_out"]).then_inc(w_out_loaded, 16)

        @block.gpsimd
        def _(pool):
            pool.wait_ge(x_hi_made, 1)
            nc.gpsimd.tensor_tensor(x_lo[:], xT[:], x_hi[:], ALU.subtract).then_inc(x_lo_made, 1)
            for e in range(E):
                pool.wait_ge(w_hi_made, e + 1)
                nc.gpsimd.tensor_tensor(w_lo[:, e], w_in[:, e], w_hi[:, e], ALU.subtract).then_inc(w_lo_made, 1)

        def outputs(pe, n, e):
            pe.wait_ge(hidden_made, 16 * n + 2 * e + 2)
            if e >= 2:
                pe.wait_ge(y_added, 8 * n + e - 1)
            else:
                wait_pos(pe, y_added, 8 * n)
            for t in range(4):
                for c in range(2):
                    mm = nc.tensor.matmul(psY[e % 2][0:PT, 128 * t:128 * t + 128],
                                          hidden[:, e % 2, c, PT * t:PT * (t + 1)], w_out[:, e, c, :],
                                          start=(c == 0), stop=(c == 1))
            mm.then_inc(y_ready, 1)

        @block.tensor
        def _(pe):
            pe.wait_ge(loaded, 16 * N_LOADS)
            router_logits(core, pe, wg, psR, None, logits_ready)
            for n, (chosen, made) in enumerate(((first, first_made), (second, second_made))):
                pe.wait_ge(made, 1)
                if n == 1:
                    pe.wait_ge(first_made, 3)
                nc.tensor.matmul(psC[0:PT, 0:128], tri[0:PT, 0:PT], chosen[:], start=True, stop=False,
                                 skip_group_check=True)
                for t in range(PAIRS - 1):
                    mm = nc.tensor.matmul(psC[0:PT, E * (t + 1):128], ones[:],
                                          chosen[:, t, :].unsqueeze(1).to_broadcast([PT, PAIRS - 1 - t, E]),
                                          start=False, stop=t == PAIRS - 2, skip_group_check=True)
                if n == 1:
                    mm = nc.tensor.matmul(psC[0:PT, 0:128], ones[:],
                                          first_count[:].unsqueeze(1).to_broadcast([PT, PAIRS, E]),
                                          start=False, stop=True, skip_group_check=True)
                mm.then_inc(counted, 1)

            pe.wait_ge(x_lo_made, 1)
            pe.wait_ge(w_lo_made, E)
            pe.wait_ge(w_out_loaded, 16)

            def block_of_tokens(n):
                for e in range(E):
                    for c in range(2):
                        at = 2 * e + c
                        if at >= 2:
                            pe.wait_ge(hidden_made, 16 * n + at - 1)
                        else:
                            wait_pos(pe, hidden_made, 16 * n)
                        for g in range(2):
                            for part, (w, tokens) in enumerate(((w_hi, x_hi), (w_hi, x_lo), (w_lo, x_hi))):
                                mm = nc.tensor.matmul(psH[c][:, g, 0:BLK],
                                                      w[:, e, F * g + 128 * c:F * g + 128 * (c + 1)],
                                                      tokens[:, bass.ds(BLK * n, BLK)],
                                                      start=(part == 0), stop=(part == 2))
                        mm.then_inc(h_ready, 1)
                        if c == 1 and e >= 1:
                            outputs(pe, n, e - 1)
                outputs(pe, n, E - 1)

            in_blocks(pe, NBLK, block_of_tokens)

        @block.scalar
        def _(act):
            nc.scalar.copy(x_hi[:], xT[:]).then_inc(x_hi_made, 1)
            act.wait_ge(shifted, 1)
            nc.scalar.activation(prob[:], prob[:], ACT.Exp).then_inc(exp_made, 1)
            for e in range(E):
                if e % (E // 2) == 0:
                    act.wait_ge(w_in_loaded[e // (E // 2)], 16)
                nc.scalar.activation(w_in[:, e], w_in[:, e], ACT.Copy, scale=W_SCALE).then_inc(w_in_scaled, 1)
                act.wait_ge(w_in_scaled, e + 1)
                nc.scalar.copy(w_hi[:, e], w_in[:, e]).then_inc(w_hi_made, 1)

            def block_of_tokens(n):
                for e in range(E):
                    for c in range(2):
                        at = 2 * e + c
                        act.wait_ge(h_ready, 16 * n + at + 1)
                        if at >= 2:
                            act.wait_ge(hidden_made, 16 * n + at - 1)
                        else:
                            wait_pos(act, hidden_made, 16 * n)
                        nc.scalar.activation(act_out[:, c, :], psH[c][:, 0, 0:BLK], ACT.Gelu,
                                             scale=1.0 / W_SCALE).then_inc(gelu_made, 1)

            in_blocks(act, NBLK, block_of_tokens)

        @block.vector
        def _(dve):
            link, wait = chain(nc, chained)
            vec = nc.vector
            logits = psR[0:PT, 0:128].rearrange("p (t e) -> p t e", e=E)
            counts = psC[0:PT, 0:128].rearrange("p (t e) -> p t e", e=E)
            ranks = rank[:].unsqueeze(1).to_broadcast([PT, PAIRS, E])
            dve.wait_ge(logits_ready, 1)
            link(vec.tensor_reduce(col[:], logits, AX.X, ALU.max))
            wait()
            vec.tensor_tensor(prob[:], logits, over_experts(col), ALU.subtract).then_inc(shifted, 1)
            dve.wait_ge(exp_made, 1)
            link(vec.tensor_reduce(col[:], prob[:], AX.X, ALU.add))
            wait()
            link(vec.reciprocal(col[:], col[:]))
            wait()
            link(vec.tensor_tensor(prob[:], prob[:], over_experts(col), ALU.mult))
            wait()
            for n, (chosen, made) in enumerate(((first, first_made), (second, second_made))):
                source = prob if n == 0 else work
                link(vec.tensor_reduce(col[:], source[:], AX.X, ALU.max))
                wait()
                link(vec.tensor_tensor(kept[:], source[:], over_experts(col), ALU.is_equal))
                wait()
                link(vec.tensor_tensor(kept[:], kept[:], ranks, ALU.mult))
                wait()
                link(vec.tensor_reduce(col[:], kept[:], AX.X, ALU.max))
                wait()
                vec.tensor_tensor(chosen[:], kept[:], over_experts(col), ALU.is_equal).then_inc(made, 1)
                dve.wait_ge(made, 1)
                if n == 0:
                    link(vec.scalar_tensor_tensor(work[:].rearrange("p t e -> p (t e)"),
                                                  first[:].rearrange("p t e -> p (t e)"), -2.0,
                                                  prob[:].rearrange("p t e -> p (t e)"), ALU.mult, ALU.add))
                    wait()
            vec.tensor_reduce(first_count[:], first[:].rearrange("p t e -> p e t"), AX.X, ALU.add).then_inc(first_made, 1)
            dve.wait_ge(counted, 1)
            link(vec.scalar_tensor_tensor(work[:], counts, float(TOP2_CAPACITY), first[:], ALU.is_le, ALU.mult))
            wait()
            dve.wait_ge(first_made, 2)
            vec.tensor_copy(kept[:], work[:]).then_inc(first_made, 1)
            dve.wait_ge(counted, 2)
            link(vec.scalar_tensor_tensor(work[:], counts, float(TOP2_CAPACITY), second[:], ALU.is_le, ALU.mult))
            wait()
            dve.wait_ge(first_made, 3)
            link(vec.tensor_tensor(kept[:], kept[:], work[:], ALU.add))
            wait()
            link(vec.tensor_tensor(gates[:], prob[:], kept[:], ALU.mult))
            wait()
            link(vec.tensor_reduce(col[:], gates[:], AX.X, ALU.add))
            wait()
            link(vec.tensor_scalar(col[:], col[:], 1e-9, None, ALU.max))
            wait()
            link(vec.reciprocal(col[:], col[:]))
            wait()
            vec.tensor_tensor(gates[:], gates[:], over_experts(col), ALU.mult).then_inc(gates_made, 1)
            dve.wait_ge(gates_made, 1)

            def add_outputs(n, e):
                dve.wait_ge(y_ready, 8 * n + e + 1)
                if e >= 1:
                    dve.wait_ge(y_added, 8 * n + e)
                for t in range(4):
                    add = vec.scalar_tensor_tensor(x[:, 4 * n + t, :], psY[e % 2][0:PT, 128 * t:128 * t + 128],
                                                   gates[:, 4 * n + t, e:e + 1], x[:, 4 * n + t, :],
                                                   ALU.mult, ALU.add)
                add.then_inc(y_added, 1)

            def block_of_tokens(n):
                for e in range(E):
                    for c in range(2):
                        dve.wait_ge(gelu_made, 16 * n + 2 * e + c + 1)
                        if e >= 2:
                            dve.wait_ge(y_ready, 8 * n + e - 1)
                        else:
                            wait_pos(dve, y_ready, 8 * n)
                        vec.scalar_tensor_tensor(hidden[:, e % 2, c, :], psH[c][:, 1, 0:BLK], 1.0 / W_SCALE,
                                                 act_out[:, c, :], ALU.mult, ALU.mult).then_inc(hidden_made, 1)
                    if e >= 1:
                        add_outputs(n, e - 1)
                add_outputs(n, E - 1)

            in_blocks(dve, NBLK, block_of_tokens)

def masked_attention(core):
    nc, dram, x, xT = core.nc, core.dram, core.x, core.xT
    scale = float(D) ** -0.5
    with ExitStack() as ctx:
        sb, ps, sem = tools(nc, ctx)
        wq, wk, wv, bv = (sb(f"c1_{n}", [128, 128]) for n in ("wq", "wk", "wv", "bv"))
        cols = sb("c1_cols", [128, 2])
        Q = sb("c1_Q", [128, B, QP])
        QK = sb("c1_QK", [128, B, QP])
        q_bk = sb("c1_q_bk", [128, PAIRS])
        qk_pair = sb("c1_qk_pair", [128, 2, 2, QP])
        ctxT = sb("c1_ctxT", [128, 2, 2, SK])
        rows = sb("c1_rows", [CHUNK, 2, 2, CHUNKS, D])
        mask_words = sb("c1_mask", [128, 2, SK // 4], I32)
        mask = mask_words[:].rearrange("p u w -> p (u w)").bitcast(U8).rearrange("p (u n) -> p u n", u=2)
        masked = sb("c1_masked", [128, SK])
        P = sb("c1_P", [128, 2, SK])
        PTr = sb("c1_PTr", [CHUNK, CHUNKS, 128])
        top, down, total, rden = (sb(f"c1_{n}", [128, 2]) for n in ("top", "down", "total", "rden"))
        OT = sb("c1_OT", [128, 2, S])

        psS = ps("c1_psS", [128, 3, 512])
        psT = ps("c1_psT", [128, 3, 512])
        psO = ps("c1_psO", [128, 512])
        psY = ps("c1_psY", [128, 512])

        loaded, filled, q_ready, q_made, qk_ready, qk_made, b_ready, b_made = (sem(f"c1_{n}") for n in (
            "loaded", "filled", "q_ready", "q_made", "qk_ready", "qk_made", "b_ready", "b_made"))
        ctx_loaded, rows_loaded, mask_loaded = ([sem(f"c1_{n}_loaded{v}") for v in range(2)]
                                                for n in ("ctx", "rows", "mask"))
        pair_ready, down_cleared, s_ready, s_moved, s_masked, top_made, down_made, p_made, rden_made, p_ready = (sem(f"c1_{n}") for n in (
            "pair_ready", "down_cleared", "s_ready", "s_moved", "s_masked", "top_made", "down_made", "p_made", "rden_made", "p_ready"))
        t_ready, t_moved, o_ready, o_moved, y_ready, y_added = (sem(f"c1_{n}") for n in (
            "t_ready", "t_moved", "o_ready", "o_moved", "y_ready", "y_added"))
        block = ctx.enter_context(nc.Block())
        N_LOADS = 5

        @block.sync
        def _(sp):
            for dst, name in ((wq, "c1_wq"), (wk, "c1_wk"), (wv, "c1_wv"), (bv, "c1_bv"), (cols, "c1_cols")):
                sp.dma_start(dst[:], dram[name]).then_inc(loaded, 16)
            sp.wait_ge(filled, 2)

            def step(t, u, i):
                if not has(t, 0, PAIRS):
                    return
                wait_pos(sp, s_ready, t - 1)
                for b in range(2):
                    sp.dma_start(ctxT[:, u, b, :], dram["ctxT"][2 * t + b]).then_inc(ctx_loaded[u], 16)
                wait_pos(sp, s_masked, t - 1)
                for b in range(2):
                    sp.dma_start(mask_words[QP * b:QP * b + S, u, :], dram["mask"][2 * t + b]).then_inc(mask_loaded[u], 16)
                wait_pos(sp, o_ready, t - 1)
                for b in range(2):
                    sp.dma_start(rows[:, u, b, :, :],
                                 dram["ctx"][2 * t + b].rearrange("(p c) d -> p c d", c=CHUNKS)).then_inc(rows_loaded[u], 16)

            in_steps(sp, 0, PAIRS, 4, PAIRS, 2, step)

        @block.gpsimd
        def _(pool):
            nc.gpsimd.memset(mask_words[:], 0).then_inc(filled, 1)
            pool.wait_ge(filled, 1)
            nc.gpsimd.memset(Q[:, :, S:QP], 0.0).then_inc(filled, 1)
            pool.wait_ge(filled, 2)
            nc.gpsimd.memset(masked[:], NEG / scale).then_inc(filled, 1)

        @block.tensor
        def _(pe):
            pe.wait_ge(loaded, 16 * N_LOADS)
            pe.wait_ge(filled, 3)
            for k in range(NBLK):
                nc.tensor.matmul(psS[:, k, 0:BLK] if k < 3 else psO[:, 0:BLK], wq[:], xT[:, k * BLK:(k + 1) * BLK],
                                 start=True, stop=True).then_inc(q_ready, 1)
            for k in range(NBLK):
                pe.wait_ge(q_made, k + 1)
                nc.tensor.matmul(psT[:, k, :] if k < 3 else psY[:, :], wk[:], Q[:, 8 * k:8 * k + 8, :],
                                 start=True, stop=True).then_inc(qk_ready, 1)
            for t in range(PAIRS):
                mm = nc.tensor.matmul(psO[:, t:t + 1], Q[:, 2 * t:2 * t + 2, :], cols[:, 1:2], start=True, stop=True)
            mm.then_inc(b_ready, 1)
            pe.wait_ge(qk_made, NBLK)
            pe.wait_ge(b_made, 1)

            def step(t, u, i):
                v = 1 - u
                if has(t, 0, PAIRS):
                    pe.wait_ge(ctx_loaded[u], 32 * i + 32)
                    pe.wait_ge(pair_ready, t + 1)
                    wait_pos(pe, s_moved, t)
                    for b in range(2):
                        for k in range(3):
                            mm = nc.tensor.matmul(psS[QP * b:QP * (b + 1), k, 0:THIRD], qk_pair[:, u, b, :],
                                                  ctxT[:, u, b, THIRD * k:THIRD * (k + 1)], start=True, stop=True)
                    mm.then_inc(s_ready, 1)
                if has(t, 1, PAIRS + 1):
                    pe.wait_ge(p_ready, t)
                    for k in range(3):
                        wait_pos(pe, t_moved, 3 * (t - 2) + k + 1)
                        for c in range(4 * k, 4 * k + 4):
                            mm = nc.tensor.transpose(psT[0:CHUNK, k, (c % 4) * 128:(c % 4 + 1) * 128],
                                                     P[:, v, c:SK:CHUNKS], core.ident[:])
                        mm.then_inc(t_ready, 1)
                if has(t, 2, PAIRS + 2):
                    pe.wait_ge(o_moved, t - 1)
                    wait_pos(pe, y_added, t - 2)
                    nc.tensor.matmul(psY[0:PT, 0:128], OT[:], wv[:], start=True, stop=False)
                    nc.tensor.matmul(psY[0:PT, 0:128], core.first_row[:, 0:PT], bv[:],
                                     start=False, stop=True).then_inc(y_ready, 1)
                if has(t, 1, PAIRS + 1):
                    pe.wait_ge(rows_loaded[v], 32 * (i - (u == 0)) + 32)
                    wait_pos(pe, o_moved, t - 1)
                    for c in range(CHUNKS):
                        if c % 4 == 0:
                            pe.wait_ge(t_moved, 3 * (t - 1) + c // 4 + 1)
                        for b in range(2):
                            mm = nc.tensor.matmul(psO[:, S * b:S * (b + 1)], rows[:, v, b, c, :],
                                                  PTr[:, c, QP * b:QP * b + S], start=(c == 0 and b == 0),
                                                  stop=(c == CHUNKS - 1), skip_group_check=True)
                    mm.then_inc(o_ready, 1)

            in_steps(pe, 0, PAIRS + 2, 4, PAIRS, 2, step)

        @block.vector
        def _(dve):
            dve.wait_ge(filled, 2)
            dve.wait_ge(loaded, 16 * N_LOADS)
            for k in range(NBLK):
                dve.wait_ge(q_ready, k + 1)
                src = psS[:, k, 0:BLK] if k < 3 else psO[:, 0:BLK]
                nc.vector.tensor_scalar(Q[:, 8 * k:8 * k + 8, 0:S], src.rearrange("p (b s) -> p b s", s=S),
                                        cols[:, 0:1], None, ALU.add).then_inc(q_made, 1)
            for k in range(NBLK):
                dve.wait_ge(qk_ready, k + 1)
                nc.vector.tensor_copy(QK[:, 8 * k:8 * k + 8, :].rearrange("p b s -> p (b s)"),
                                      psT[:, k, :] if k < 3 else psY[:, :]).then_inc(qk_made, 1)
            dve.wait_ge(b_ready, 1)
            nc.vector.tensor_copy(q_bk[:], psO[:, 0:PAIRS]).then_inc(b_made, 1)
            dve.wait_ge(filled, 3)

            def step(t, u, i):
                v = 1 - u
                if has(t, 1, PAIRS + 1):
                    dve.wait_ge(p_made, t)
                    nc.vector.reciprocal(rden[:, v:v + 1], total[:, v:v + 1]).then_inc(rden_made, 1)
                    dve.wait_ge(rden_made, t)
                    nc.vector.tensor_scalar(P[:, v, :], P[:, v, :], rden[:, v:v + 1], None, ALU.mult).then_inc(p_ready, 1)
                if has(t, 0, PAIRS):
                    dve.wait_ge(mask_loaded[u], 32 * i + 32)
                    dve.wait_ge(s_moved, t + 1)
                    wait_pos(dve, p_made, t - 1)
                    nc.vector.memset(down[:, u:u + 1], 0.0).then_inc(down_cleared, 1)
                    nc.vector.copy_predicated(P[:, u, :], mask[:, u, :], masked[:]).then_inc(s_masked, 1)
                    dve.wait_ge(s_masked, t + 1)
                    wait_pos(dve, down_made, t - 1)
                    nc.vector.tensor_reduce(top[:, u:u + 1], P[:, u, :], AX.X, ALU.max).then_inc(top_made, 1)
                    dve.wait_ge(top_made, t + 1)
                    dve.wait_ge(down_cleared, t + 1)
                    nc.vector.tensor_scalar(down[:, u:u + 1], top[:, u:u + 1], -scale, None, ALU.mult).then_inc(down_made, 1)
                if has(t, 2, PAIRS + 2):
                    dve.wait_ge(y_ready, t - 1)
                    nc.vector.tensor_tensor(x[:, t - 2, :], psY[0:PT, 0:128], x[:, t - 2, :], ALU.add).then_inc(y_added, 1)

            in_steps(dve, 0, PAIRS + 2, 4, PAIRS, 2, step)

        @block.scalar
        def _(act):
            act.wait_ge(qk_made, NBLK)
            act.wait_ge(b_made, 1)

            def step(t, u, i):
                v = 1 - u
                if has(t, 0, PAIRS):
                    wait_pos(act, s_ready, t - 1)
                    nc.scalar.copy(qk_pair[:, u, :, :], QK[:, bass.ds(2 * t, 2), :]).then_inc(pair_ready, 1)
                    act.wait_ge(s_ready, t + 1)
                    wait_pos(act, t_ready, t - 1)
                    nc.scalar.activation(P[:, u, :].rearrange("p (a n) -> p a n", a=3), psS[:, :, 0:THIRD], ACT.Identity,
                                         bias=q_bk[:, bass.ds(t, 1)]).then_inc(s_moved, 1)
                if has(t, 1, PAIRS + 1):
                    wait_pos(act, o_ready, t - 1)
                    for k in range(3):
                        act.wait_ge(t_ready, 3 * (t - 1) + k + 1)
                        nc.scalar.copy(PTr[:, 4 * k:4 * k + 4, :].rearrange("p c q -> p (c q)"),
                                       psT[0:CHUNK, k, :]).then_inc(t_moved, 1)
                if has(t, 0, PAIRS):
                    act.wait_ge(down_made, t + 1)
                    wait_pos(act, rden_made, t - 1)
                    nc.scalar.activation(P[:, u, :], P[:, u, :], ACT.Exp, bias=down[:, u:u + 1], scale=scale,
                                         accum_out=total[:, u:u + 1]).then_inc(p_made, 1)
                if has(t, 1, PAIRS + 1):
                    act.wait_ge(o_ready, t)
                    wait_pos(act, y_ready, t - 1)
                    nc.scalar.copy(OT[:].rearrange("p b s -> p (b s)"), psO[:, 0:PT]).then_inc(o_moved, 1)

            in_steps(act, 0, PAIRS + 1, 4, PAIRS, 2, step)


def choosing_experts(core):
    nc, dram, x, xT = core.nc, core.dram, core.x, core.xT
    FC = 4
    BITS, AT_ONCE = 30, 3
    ROUNDS, TRIALS = BITS // AT_ONCE, 2 ** AT_ONCE - 1
    with ExitStack() as ctx:
        sb, ps, sem = tools(nc, ctx)
        ws = sb("m1_ws", [128, E])
        bs = sb("m1_bs", [128, E])
        b1 = sb("m1_b1", [128, E, FC])
        w1 = sb("m1_w1", [128, E, FC, 128])
        w1_hi, w1_lo = (sb(f"m1_w1_{n}", [128, E, FC, 128], F16) for n in ("hi", "lo"))
        x_hi, x_lo = (sb(f"m1_x_{n}", [128, TOK], F16) for n in ("hi", "lo"))
        w2 = sb("m1_w2", [128, E, FC, D])
        b2 = sb("m1_b2", [128, PAIRS, D])
        same = sb("m1_same", [128, 128])
        before = sb("m1_before", [128, 128])
        prob = sb("m1_prob", [PT, PAIRS, E])
        col = sb("m1_col", [PT, PAIRS])
        pT = sb("m1_pT", [128, PT])
        marks = sb("m1_marks", [128, TRIALS, PT])
        equal = sb("m1_equal", [128, PT])
        count = sb("m1_count", [128, TRIALS])
        equals = sb("m1_equals", [128, 1])
        room = sb("m1_room", [128, 1])
        earlier = sb("m1_earlier", [128, 1])
        prefix, most = (sb(f"m1_{n}", [128, 1], I32) for n in ("prefix", "most"))
        trial, tried, taken = (sb(f"m1_{n}", [128, TRIALS], I32) for n in ("trial", "tried", "taken"))
        gatesT = sb("m1_gatesT", [128, PT])
        gates = sb("m1_gates", [PT, PAIRS, E])
        hidden = sb("m1_hidden", [128, E, FC, BLK])

        psR = ps("m1_psR", [128, 512])
        psH = [ps(f"m1_psH{k}", [128, 512]) for k in range(4)]
        psY = [ps(f"m1_psY{k}", [128, 512]) for k in range(2)]

        loaded, logits_ready, chained, shifted, exp_made, prob_made, pT_ready, pT_made = (sem(f"m1_{n}") for n in (
            "loaded", "logits_ready", "chained", "shifted", "exp_made", "prob_made", "pT_ready", "pT_made"))
        w1_loaded = [sem(f"m1_w1_loaded{k}") for k in range(2)]
        w1_scaled = sem("m1_w1_scaled")
        w2_loaded, b2_loaded, x_hi_made, x_lo_made, w1_hi_made, w1_lo_made = (sem(f"m1_{n}") for n in (
            "w2_loaded", "b2_loaded", "x_hi_made", "x_lo_made", "w1_hi_made", "w1_lo_made"))
        tried_made, counted, count_ready, taken_made, most_made, prefix_made, trial_made = (sem(f"m1_{n}") for n in (
            "tried_made", "counted", "count_ready", "taken_made", "most_made", "prefix_made", "trial_made"))
        asked, answered, gatesT_made, gates_ready, gates_made, b2_ready, b2_added = (sem(f"m1_{n}") for n in (
            "asked", "answered", "gatesT_made", "gates_ready", "gates_made", "b2_ready", "b2_added"))
        h_ready, gelu_made, y_ready, y_added = (sem(f"m1_{n}") for n in ("h_ready", "gelu_made", "y_ready", "y_added"))
        block = ctx.enter_context(nc.Block())
        loads = ((ws, "m1_ws"), (bs, "m1_bs"), (b1, "m1_b1"), (same, "same"), (before, "before"),
                 (trial, "m1_trial"))

        @block.sync
        def _(sp):
            for dst, name in loads:
                sp.dma_start(dst[:], dram[name]).then_inc(loaded, 16)
            for k in range(2):
                half = slice(E // 2 * k, E // 2 * (k + 1))
                sp.dma_start(w1[:, half], dram["m1_w1"][:, half]).then_inc(w1_loaded[k], 16)
            sp.dma_start(b2[:], dram["m1_b2"]).then_inc(b2_loaded, 16)
            sp.dma_start(w2[:], dram["m1_w2"]).then_inc(w2_loaded, 16)

        @block.gpsimd
        def _(pool):
            pool.wait_ge(x_hi_made, 1)
            nc.gpsimd.tensor_tensor(x_lo[:], xT[:], x_hi[:], ALU.subtract).then_inc(x_lo_made, 1)
            for e in range(E):
                pool.wait_ge(w1_hi_made, e + 1)
                nc.gpsimd.tensor_tensor(w1_lo[:, e], w1[:, e], w1_hi[:, e], ALU.subtract).then_inc(w1_lo_made, 1)

        @block.tensor
        def _(pe):
            def hidden_of(n, e):
                for c in range(FC):
                    unit = FC * (E * n + e) + c
                    wait_pos(pe, gelu_made, unit - FC + 1)
                    for part, (w, tokens) in enumerate(((w1_hi, x_hi), (w1_hi, x_lo), (w1_lo, x_hi))):
                        mm = nc.tensor.matmul(psH[c][:, 0:BLK], w[:, e, c, :], tokens[:, bass.ds(BLK * n, BLK)],
                                              start=(part == 0), stop=(part == 2))
                    mm.then_inc(h_ready, 1)

            def outputs(n, e):
                pe.wait_ge(gelu_made, FC * (E * n + e + 1))
                wait_pos(pe, y_added, E * n + e - 1)
                for t in range(4):
                    for c in range(FC):
                        mm = nc.tensor.matmul(psY[e % 2][0:PT, 128 * t:128 * t + 128],
                                              hidden[:, e, c, PT * t:PT * (t + 1)], w2[:, e, c, :],
                                              start=(c == 0), stop=(c == FC - 1))
                mm.then_inc(y_ready, 1)

            pe.wait_ge(loaded, 16 * len(loads))
            router_logits(core, pe, ws, psR, bs, logits_ready)
            pe.wait_ge(prob_made, 1)
            nc.tensor.transpose(psR[:, 128:128 + PT], prob[:].rearrange("p t e -> p (t e)"),
                                core.ident[0:PT, 0:PT]).then_inc(pT_ready, 1)
            pe.wait_ge(x_lo_made, 1)
            for n in range(ROUNDS):
                pe.wait_ge(counted, n + 1)
                nc.tensor.matmul(psR[:, 256:256 + TRIALS], same[:], count[:], start=True, stop=True).then_inc(count_ready, 1)
                if 1 <= n <= E:
                    pe.wait_ge(w1_lo_made, n)
                    hidden_of(0, n - 1)
            pe.wait_ge(asked, 1)
            nc.tensor.matmul(psR[:, 264:265], same[:], count[:, 0:1], start=True, stop=True)
            nc.tensor.matmul(psR[:, 265:266], before[:], equals[:], start=True, stop=True).then_inc(answered, 1)
            pe.wait_ge(gatesT_made, 1)
            nc.tensor.transpose(psR[0:PT, 384:512], gatesT[:], core.ident[:]).then_inc(gates_ready, 1)
            pe.wait_ge(b2_loaded, 16)
            for k in range(4):
                wait_pos(pe, b2_added, k - 1)
                for t in range(4):
                    mm = nc.tensor.matmul(psY[k % 2][0:PT, 128 * t:128 * t + 128], gatesT[:], b2[:, 4 * k + t, :],
                                          start=True, stop=True)
                mm.then_inc(b2_ready, 1)
            pe.wait_ge(w2_loaded, 16)
            pe.wait_ge(b2_added, 4)

            def block_of_tokens(n):
                for e in range(E):
                    outputs(n, e)
                    hidden_of(n + 1, e)

            in_blocks(pe, NBLK - 1, block_of_tokens)
            for e in range(E):
                outputs(NBLK - 1, e)

        @block.scalar
        def _(act):
            nc.scalar.copy(x_hi[:], xT[:]).then_inc(x_hi_made, 1)
            act.wait_ge(shifted, 1)
            nc.scalar.activation(prob[:], prob[:], ACT.Exp).then_inc(exp_made, 1)
            for e in range(E):
                if e % (E // 2) == 0:
                    act.wait_ge(w1_loaded[e // (E // 2)], 16)
                nc.scalar.activation(w1[:, e], w1[:, e], ACT.Copy, scale=W_SCALE).then_inc(w1_scaled, 1)
                act.wait_ge(w1_scaled, e + 1)
                nc.scalar.copy(w1_hi[:, e], w1[:, e]).then_inc(w1_hi_made, 1)

            def block_of_tokens(n):
                for e in range(E):
                    wait_pos(act, y_ready, E * (n - 1) + e + 1)
                    for c in range(FC):
                        act.wait_ge(h_ready, FC * (E * n + e) + c + 1)
                        nc.scalar.activation(hidden[:, e, c, :], psH[c][:, 0:BLK], ACT.Gelu_apprx_tanh,
                                             bias=b1[:, e, c:c + 1], scale=1.0 / W_SCALE).then_inc(gelu_made, 1)

            in_blocks(act, NBLK, block_of_tokens)

        @block.vector
        def _(dve):
            link, wait = chain(nc, chained)
            vec = nc.vector
            logits = psR[0:PT, 0:128].rearrange("p (t e) -> p t e", e=E)
            link(vec.memset(prefix[:], 0))
            dve.wait_ge(logits_ready, 1)
            link(vec.tensor_reduce(col[:], logits, AX.X, ALU.max))
            wait()
            vec.tensor_tensor(prob[:], logits, over_experts(col), ALU.subtract).then_inc(shifted, 1)
            dve.wait_ge(exp_made, 1)
            link(vec.tensor_reduce(col[:], prob[:], AX.X, ALU.add))
            wait()
            link(vec.reciprocal(col[:], col[:]))
            wait()
            vec.tensor_tensor(prob[:], prob[:], over_experts(col), ALU.mult).then_inc(prob_made, 1)
            dve.wait_ge(pT_ready, 1)
            link(vec.tensor_copy(pT[:], psR[:, 128:128 + PT]))
            wait()
            def test_bits(n):
                wait_pos(dve, prefix_made, n)
                wait_pos(dve, trial_made, n)
                vec.tensor_tensor(tried[:], trial[:], prefix[:].to_broadcast([128, TRIALS]),
                                  ALU.bitwise_or).then_inc(tried_made, 1)
                dve.wait_ge(tried_made, n + 1)
                for k in range(TRIALS):
                    mark = vec.tensor_scalar(marks[:, k, :], pT[:], tried[:, k:k + 1].bitcast(F32), 0.0,
                                             ALU.is_ge, ALU.add, accum_out=count[:, k:k + 1])
                mark.then_inc(counted, 1)
                dve.wait_ge(count_ready, n + 1)
                vec.scalar_tensor_tensor(taken[:], psR[:, 256:256 + TRIALS], float(CHOICE), trial[:], ALU.is_ge,
                                         ALU.mult).then_inc(taken_made, 1)
                dve.wait_ge(taken_made, n + 1)
                vec.tensor_reduce(most[:], taken[:], AX.X, ALU.max).then_inc(most_made, 1)
                vec.tensor_scalar(trial[:], trial[:], AT_ONCE, None, ALU.logical_shift_right).then_inc(trial_made, 1)
                dve.wait_ge(most_made, n + 1)
                vec.tensor_tensor(prefix[:], prefix[:], most[:], ALU.bitwise_or).then_inc(prefix_made, 1)

            in_blocks(dve, ROUNDS, test_bits)
            dve.wait_ge(prefix_made, ROUNDS)
            threshold = prefix[:].bitcast(F32)
            chosen, order = marks[:, 0, :], marks[:, 1, :]
            link(vec.tensor_scalar(chosen, pT[:], threshold, 0.0, ALU.is_gt, ALU.add, accum_out=count[:, 0:1]))
            wait()
            vec.tensor_scalar(equal[:], pT[:], threshold, 0.0, ALU.is_equal, ALU.add,
                              accum_out=equals[:]).then_inc(asked, 1)
            dve.wait_ge(asked, 1)
            link(vec.tensor_tensor_scan(order, equal[:], equal[:], 0.0, ALU.add, ALU.max))
            dve.wait_ge(answered, 1)
            link(vec.tensor_scalar(room[:], psR[:, 264:265], -1.0, float(CHOICE), ALU.mult, ALU.add))
            wait()
            link(vec.tensor_scalar(order, order, psR[:, 265:266], None, ALU.add))
            wait()
            link(vec.scalar_tensor_tensor(order, order, room[:], equal[:], ALU.is_le, ALU.mult))
            wait()
            link(vec.tensor_tensor(chosen, chosen, order, ALU.add))
            wait()
            vec.tensor_tensor(gatesT[:], chosen, pT[:], ALU.mult).then_inc(gatesT_made, 1)
            dve.wait_ge(gates_ready, 1)
            vec.tensor_copy(gates[:].rearrange("p t e -> p (t e)"), psR[0:PT, 384:512]).then_inc(gates_made, 1)
            for k in range(4):
                dve.wait_ge(b2_ready, k + 1)
                rows = x[:, 4 * k:4 * k + 4, :].rearrange("p t d -> p (t d)")
                vec.tensor_tensor(rows, psY[k % 2][0:PT, :], rows, ALU.add).then_inc(b2_added, 1)
            dve.wait_ge(b2_added, 4)
            dve.wait_ge(gates_made, 1)

            def block_of_tokens(n):
                for e in range(E):
                    dve.wait_ge(y_ready, 8 * n + e + 1)
                    if e >= 1:
                        dve.wait_ge(y_added, 8 * n + e)
                    for t in range(4):
                        add = vec.scalar_tensor_tensor(x[:, 4 * n + t, :], psY[e % 2][0:PT, 128 * t:128 * t + 128],
                                                       gates[:, 4 * n + t, e:e + 1], x[:, 4 * n + t, :],
                                                       ALU.mult, ALU.add)
                    add.then_inc(y_added, 1)

            in_blocks(dve, NBLK, block_of_tokens)

def program(nc, dram, out, stages=6):
    with ExitStack() as ctx:
        sb, ps, sem = tools(nc, ctx)
        core = Core(nc, dram)
        core.x = sb("x", [PT, PAIRS, D])
        core.xT = sb("xT", [128, TOK])
        core.ident = sb("ident", [128, 128])
        core.first_row = sb("first_row", [128, 128])
        load_inputs(core)
        self_attention(core, 0)
        layer_norm(core, "n0")
        context_attention(core)
        layer_norm(core, "n1")
        top2_experts(core)
        layer_norm(core, "n2")
        self_attention(core, 1)
        layer_norm(core, "n3")
        masked_attention(core)
        layer_norm(core, "n4")
        choosing_experts(core)
        layer_norm(core, "n5", out)




def shape_tables():
    f = np.float32
    p = np.arange(128)
    t = {"ident": np.eye(128, dtype=f), "first_row": np.zeros((128, 128), f)}
    t["first_row"][0] = 1.0
    t["head_of_row"] = (p[:, None] // DK == np.arange(H)[None]).astype(f)
    two = np.arange(PT)[:, None] // S
    t["vmask"] = ((p[None] // DK) % 2 == two).astype(f)
    ones = np.zeros((PT, 2, H, DK + 1), f)
    ones[:, :, :, DK] = (np.arange(H)[None, None] % 2 == two[:, :, None])
    t["vbd_ones"] = ones
    inv = (f(1.0) / f(10000.0) ** (np.arange(0, DK, 2, dtype=f) / f(DK))).astype(f)
    ang = np.arange(S, dtype=f)[:, None] * inv
    at = (p % DK) // 2
    t["rope_cos"] = np.cos(ang).astype(f).T[at]
    t["rope_sin"] = np.sin(ang).astype(f).T[at] * np.where(p % 2 == 0, -1, 1).astype(f)[:, None]
    causal = np.where(np.tril(np.ones((S, S), bool)), f(0), f(NEG))
    phi = (1.0 + np.sqrt(5.0)) / 2.0
    pos = (np.arange(S, dtype=f) * f(phi)) % f(1.0)
    dist = np.abs(pos[:, None] - pos[None, :])
    table = np.log(np.exp(-dist) + f(1e-8)) / f(HEAD_SCALE)
    for n, a in (("s0_bias", causal), ("s1_bias", table)):
        padded = np.zeros((2, QP, S), f)
        padded[:, :S] = a
        parts = []
        for _ in range(1 if n == "s0_bias" else 3):
            parts.append((padded.view(np.uint32) & np.uint32(0xffff0000)).view(f))
            padded = padded - parts[-1]
        t[n] = np.stack(parts, axis=2).reshape(128, len(parts), S)
    t["head_in_group"] = ((p[:, None] // DK) % HG == np.arange(HG)[None]).astype(f)
    t["tri"] = np.triu(np.ones((128, 128), f))
    t["ones"] = np.ones((PT, PT), f)
    t["rank"] = np.broadcast_to(E - np.arange(E, dtype=f), (PT, E))
    expert, pair = p % E, p // E
    t["same"] = (expert[:, None] == expert[None]).astype(f)
    t["before"] = t["same"] * (pair[:, None] < pair[None])
    t["m1_trial"] = np.broadcast_to(np.arange(1, 8, dtype=np.int32) << 27, (128, 7))
    t["c0_sum_row"] = (p[:, None] == (p // 32 * 32 + 24)[None]).astype(f)
    return t


def laid_out(i):
    f = np.float32
    swap = np.arange(128) ^ 1

    def row(v):
        out = np.zeros((128, 128), f)
        out[0] = v
        return out

    a = {"x": i["x"].reshape(TOK, D), "xT": i["x"].reshape(TOK, D).T}
    a["s0_wq"], a["s0_wk"], a["s0_wv"], a["s0_wo"] = (i[f"L0_attn_W{n}"].T for n in "qkvo")
    a["s0_wqs"], a["s0_wks"] = a["s0_wq"][:, swap], a["s0_wk"][:, swap]
    a["s0_bo"] = row(i["L0_attn_bo"])
    a["s0_cols"] = np.stack([i["L0_attn_bq"], i["L0_attn_bq"][swap], i["L0_attn_bk"], i["L0_attn_bk"][swap],
                             i["L0_attn_bv"]], axis=1)
    a["ctxT"] = i["ctx_1024"].transpose(0, 2, 1)
    a["c0_wq"], a["c0_wk"], a["c0_wv"] = (i[f"L0_xattn_W_{n}"].transpose(1, 0, 2).reshape(128, 128) for n in "qkv")
    wo = i["L0_xattn_W_o"].T.reshape(GROUPS, HG, DK, 128)
    padded = np.zeros((GROUPS, 32, HG, 128), f)
    for j in range(HG):
        at = DK * j if j < 3 else 0
        padded[:, at:at + DK, j, :] = wo[:, j]
    a["c0_wo"] = padded.reshape(128, HG, 128)
    a["c0_bo"] = row(i["L0_xattn_b_o"])
    a["m0_wg"] = i["L0_ffn_Wg"]
    a["m0_w_in"] = i["L0_ffn_W_in"].transpose(1, 0, 2)
    a["m0_w_out"] = i["L0_ffn_W_out"].reshape(E, 2, 128, D).transpose(2, 0, 1, 3)
    a["s1_wq"], a["s1_wk"], a["s1_wv"] = (i["L1_attn_w_qkv"][:, 128 * n:128 * n + 128] for n in range(3))
    a["s1_wo"], a["s1_bo"] = i["L1_attn_w_proj"], row(i["L1_attn_b_proj"])
    a["ctx"] = i["ctx_1024"]
    a["mask"] = i["mask_BxSxS2_bk1"].view(np.int32)
    a["c1_wq"], a["c1_wk"], a["c1_wv"] = i["L1_xattn_Wq"].T, i["L1_xattn_Wk"], i["L1_xattn_Wv"].T
    a["c1_bv"] = row(i["L1_xattn_bv"])
    a["c1_cols"] = np.stack([i["L1_xattn_bq"], i["L1_xattn_bk"]], axis=1)
    a["m1_ws"] = i["L1_ffn_Ws"]
    a["m1_bs"] = row8 = np.zeros((128, E), f)
    row8[0] = i["L1_ffn_bs"]
    a["m1_b1"] = i["L1_ffn_b1"].reshape(E, 4, 128).transpose(2, 0, 1)
    a["m1_w1"] = i["L1_ffn_W1"].reshape(E, D, 4, 128).transpose(1, 0, 2, 3)
    a["m1_w2"] = i["L1_ffn_W2"].reshape(E, 4, 128, D).transpose(2, 0, 1, 3)
    b2 = np.zeros((PAIRS, E, PAIRS, D), f)
    for t in range(PAIRS):
        b2[t, :, t] = i["L1_ffn_b2"]
    a["m1_b2"] = b2.reshape(128, PAIRS, D)
    return a


def kernel(**inputs):
    import concourse.bacc as bacc
    from concourse.bass_utils import run_bass_kernel_spmd

    inputs = {k: np.asarray(v) for k, v in inputs.items()}
    arrays = {f"in_{k}": np.ascontiguousarray(v) for k, v in {**laid_out(inputs), **shape_tables()}.items()}
    nc = bacc.Bacc("TRN2", target_bir_lowering=False, num_devices=1)
    dram = {k[3:]: nc.dram_tensor(k, v.shape, mybir.dt.from_np(v.dtype), kind="ExternalInput").ap()
            for k, v in arrays.items()}
    out = nc.dram_tensor("out", (TOK, D), F32, kind="ExternalOutput").ap()
    program(nc, dram, out)
    result = run_bass_kernel_spmd(nc, [arrays], core_ids=[0])
    return result.results[0]["out"].reshape(B, S, D)
```

```python
from contextlib import ExitStack

import numpy as np

import concourse.bass as bass
from concourse import mybir

F32 = mybir.dt.float32
F16 = mybir.dt.float16
BF16 = mybir.dt.bfloat16
I32 = mybir.dt.int32
U8 = mybir.dt.uint8
ALU = mybir.AluOpType
ACT = mybir.ActivationFunctionType
AX = mybir.AxisListType

B, S, D = 32, 56, 128
SK = 1500
H, DK = 16, 8
PAIRS = B // 2
PT = 2 * S
TOK = B * S
QP = 64
CHUNK = 125
CHUNKS = SK // CHUNK
GROUPS, HG = 4, 4
GC = HG * S
THIRD = SK // 3
HEAD_SCALE = float(DK) ** -0.5
LN_EPS = 1e-5
NEG = -1e9
BLK = 448
NBLK = TOK // BLK


def wait_pos(eng, sem, value):
    if isinstance(value, int) and value <= 0:
        return
    eng.wait_ge(sem, value)


def in_steps(eng, first, last, loop_from, loop_to, period, body):
    for s in range(first, loop_from):
        body(s, s % period, s // 2)
    with eng.Fori(loop_from // period, loop_to // period) as n:
        for u in range(period):
            body(period * n + u, u, period // 2 * n + u // 2)
    for s in range(loop_to, last):
        body(s, s % period, s // 2)


def in_blocks(eng, count, body):
    body(0)
    with eng.Fori(1, count) as n:
        body(n)


def has(s, low, high):
    return not isinstance(s, int) or low <= s < high


SMALL = {
    "s0": ("s0_wq", "s0_wqs", "rope_cos", "rope_sin", "s0_cols", "s0_wk", "s0_wks", "s0_wv", "s0_wo", "s0_bo", "s0_bias",
           "head_of_row", "vmask"),
    "c0": ("c0_wk", "c0_wq", "head_in_group", "c0_wv", "c0_bo", "c0_wo", "c0_sum_row"),
    "m0": ("m0_wg", "tri", "rank", "ones"),
    "s1": ("s1_wq", "s1_wk", "s1_wv", "s1_wo", "s1_bo", "s1_bias"),
    "c1": ("c1_wq", "c1_wk", "c1_wv", "c1_bv", "c1_cols"),
    "m1": ("m1_ws", "m1_bs", "m1_b1", "same", "before", "m1_trial"),
}


class Core:

    def __init__(self, nc, dram):
        self.nc, self.dram = nc, dram
        self.small, self.small_loaded = {}, {}

    def load_small(self, eng, stage):
        for name in SMALL[stage]:
            eng.dma_start(self.small[name][:], self.dram[name]).then_inc(self.small_loaded[stage], 16)

    def wait_small(self, eng, stage):
        eng.wait_ge(self.small_loaded[stage], 16 * len(SMALL[stage]))


def tools(nc, ctx):
    stage_sems = []

    @ctx.callback
    def _():
        nc.clear_and_free_semaphores(stage_sems)
        nc.all_engine_barrier()

    def sb(name, shape, dt=F32):
        return ctx.enter_context(nc.sbuf_tensor(name, shape, dt))

    def ps(name, shape, dt=F32):
        return ctx.enter_context(nc.psum_tensor(name, shape, dt))

    def sem(name):
        stage_sems.append(nc.alloc_semaphore(name))
        return stage_sems[-1]

    return sb, ps, sem


def load_inputs(core):
    nc, dram = core.nc, core.dram
    with ExitStack() as ctx:
        sb, ps, sem = tools(nc, ctx)
        loaded = sem("in_loaded")
        block = ctx.enter_context(nc.Block())

        @block.sync
        def _(sp):
            sp.dma_start(core.xT[:], dram["xT"]).then_inc(loaded, 16)
            sp.dma_start(core.x[:], dram["x"].rearrange("(t p) d -> p t d", p=PT)).then_inc(loaded, 16)
            sp.dma_start(core.ident[:], dram["ident"]).then_inc(loaded, 16)
            sp.dma_start(core.first_row[:], dram["first_row"]).then_inc(loaded, 16)
            core.load_small(sp, "s0")
            sp.wait_ge(loaded, 64)


def layer_norm(core, tag, out=None):
    nc, x, xT = core.nc, core.x, core.xT
    stats, measured = core.stats, core.measured
    ON_DVE = 10
    with ExitStack() as ctx:
        sb, ps, sem = tools(nc, ctx)
        mv = sb(f"{tag}_mv", [PT, PAIRS, 2])
        std = sb(f"{tag}_std", [PT, PAIRS])
        rstd = sb(f"{tag}_rstd", [PT, PAIRS])
        offset = sb(f"{tag}_offset", [PT, PAIRS])
        unused = sb(f"{tag}_unused", [PT, 1])
        turned = [ps(f"{tag}_turned{k}", [128, 512]) for k in range(4)]
        stats_made, mv_made, var_made, std_made, rstd_made, offset_made = (sem(f"{tag}_{n}") for n in (
            "stats_made", "mv_made", "var_made", "std_made", "rstd_made", "offset_made"))
        dve_normed, act_normed, transposed, stored = (sem(f"{tag}_{n}") for n in (
            "dve_normed", "act_normed", "transposed", "stored"))
        block = ctx.enter_context(nc.Block())

        def wait_normed(eng, k):
            eng.wait_ge(dve_normed, min(4 * k + 4, ON_DVE))
            wait_pos(eng, act_normed, 4 * k + 4 - ON_DVE)

        def move(copy, k):
            copy(xT[:, k * BLK:(k + 1) * BLK], turned[k][:, 0:BLK])

        @block.vector
        def _(dve):
            for t in range(measured, PAIRS):
                nc.vector.bn_stats(stats[:, t, :], x[:, t, :]).then_inc(stats_made, 1)
            for t in range(PAIRS):
                wait_pos(dve, stats_made, t - measured + 1)
                nc.vector.bn_aggr(mv[:, t, :], stats[:, t, :]).then_inc(mv_made, 1)
            dve.wait_ge(mv_made, PAIRS)
            nc.vector.tensor_scalar(std[:], mv[:, :, 1], LN_EPS, None, ALU.add).then_inc(var_made, 1)
            dve.wait_ge(std_made, 1)
            nc.vector.reciprocal(rstd[:], std[:]).then_inc(rstd_made, 1)
            dve.wait_ge(rstd_made, 1)
            nc.vector.scalar_tensor_tensor(offset[:], mv[:, :, 0], -1.0, rstd[:], ALU.mult, ALU.mult).then_inc(offset_made, 1)
            for t in range(ON_DVE):
                nc.vector.tensor_scalar(x[:, t, :], x[:, t, :], mv[:, t, 0:1], rstd[:, t:t + 1],
                                        ALU.subtract, ALU.mult).then_inc(dve_normed, 1)
            if out is None:
                for k in range(2):
                    dve.wait_ge(transposed, k + 1)
                    move(nc.vector.tensor_copy, k)

        @block.scalar
        def _(act):
            nc.scalar.activation(unused[:], core.ident[0:PT, 0:1], ACT.Sqrt)
            act.wait_ge(var_made, 1)
            nc.scalar.activation(std[:], std[:], ACT.Sqrt).then_inc(std_made, 1)
            act.wait_ge(rstd_made, 1)
            act.wait_ge(offset_made, 1)
            for t in range(ON_DVE, PAIRS):
                nc.scalar.activation(x[:, t, :], x[:, t, :], ACT.Identity, bias=offset[:, t:t + 1],
                                     scale=rstd[:, t:t + 1]).then_inc(act_normed, 1)
            if out is None:
                for k in range(2, 4):
                    act.wait_ge(transposed, k + 1)
                    move(nc.scalar.copy, k)

        @block.tensor
        def _(pe):
            if out is None:
                for k in range(4):
                    wait_normed(pe, k)
                    for t in range(4):
                        mm = nc.tensor.transpose(turned[k][:, t * PT:(t + 1) * PT], x[:, 4 * k + t, :],
                                                 core.ident[0:PT, 0:PT])
                    mm.then_inc(transposed, 1)

        @block.sync
        def _(sp):
            if out is not None:
                for k in range(4):
                    wait_normed(sp, k)
                    sp.dma_start(out[4 * k * PT:4 * (k + 1) * PT, :].rearrange("(t p) d -> p t d", p=PT),
                                 x[:, 4 * k:4 * k + 4, :]).then_inc(stored, 16)
                sp.wait_ge(stored, 64)


def self_attention(core, layer):
    nc, dram, x, xT = core.nc, core.dram, core.x, core.xT
    rope = layer == 0
    L = f"s{layer}_"
    names = ["wq", "wqs", "wk", "wks", "wv", "wo", "bo"] if rope else ["wq", "wk", "wv", "wo", "bo"]
    core.measured = PAIRS - 1
    with ExitStack() as ctx:
        sb, ps, sem = tools(nc, ctx)
        W = {n: core.small[L + n] for n in names}
        PARTS = 1 if rope else 3
        bias = core.small[L + "bias"]
        bias_parts = sb(L + "bias_parts", [128, PARTS, S], BF16)
        ident_bf16 = sb(L + "ident_bf16", [128, 128], BF16)
        head_of_row, vmask = core.small["head_of_row"], core.small["vmask"]
        if rope:
            cos, sin = core.small["rope_cos"], core.small["rope_sin"]
            cols = core.small["s0_cols"]
            part_a, part_b = sb(L + "part_a", [128, 2, BLK]), sb(L + "part_b", [128, 2, BLK])
        Q = sb(L + "Q", [128, B, QP])
        K = sb(L + "K", [128, B, S])
        q_pair = sb(L + "q_pair", [128, 2, 2, QP])
        x_twice = sb(L + "x_twice", [128, 2, 2, 2, S])
        Kbd = sb(L + "Kbd", [128, 2, 2, H * S])
        Vbd = sb(L + "Vbd", [PT, 2, 2, H, DK + 1])
        P = sb(L + "P", [128, 2, H * S])
        PTr = sb(L + "PTr", [PT, H // 2, 128])
        top = sb(L + "top", [128, 2, H])
        rden = sb(L + "rden", [128, 2, H])
        O = sb(L + "O", [128, 2, 128])
        OT = sb(L + "OT", [128, 2, PT])

        psS = ps(L + "psS", [128, 2, 512])
        psT = ps(L + "psT", [128, 2, 512])
        psV = ps(L + "psV", [128, 512])
        psO = ps(L + "psO", [128, 512])
        psOT = ps(L + "psOT", [128, 512])
        psY = ps(L + "psY", [128, 512])

        loaded, padded, parts_made = (sem(L + n) for n in ("loaded", "padded", "parts_made"))
        proj_ready, proj_used, rope_parts = (sem(L + n) for n in ("proj_ready", "proj_used", "rope_parts"))
        xs_ready, kbd_ready, v_ready, vbd_ready, s_ready, top_ready, s_used, p_ready = (sem(L + n) for n in (
            "xs_ready", "kbd_ready", "v_ready", "vbd_ready", "s_ready", "top_ready", "s_used", "p_ready"))
        t_ready, t_moved, o_ready, rden_ready, o_moved, ot_ready, ot_moved, y_ready, y_used = (sem(L + n) for n in (
            "t_ready", "t_moved", "o_ready", "rden_ready", "o_moved", "ot_ready", "ot_moved", "y_ready", "y_used"))
        block = ctx.enter_context(nc.Block())
        steps = (-1, PAIRS + 2, 4, PAIRS - 2, 2)
        projections = [("wq", "wqs", 0, Q), ("wk", "wks", 2, K)]
        banks = [psS[:, 0, :], psS[:, 1, :], psT[:, 0, :], psT[:, 1, :]]

        @block.sync
        def _(sp):
            for u in range(2):
                sp.dma_start(Vbd[:, u, :, :, :], dram["vbd_ones"]).then_inc(loaded, 16)
            if layer == 0:
                for stage in ("c0", "m0", "s1", "c1", "m1"):
                    core.load_small(sp, stage)

        @block.gpsimd
        def _(pool):
            nc.gpsimd.memset(Q[:, :, S:QP], 0.0).then_inc(padded, 1)
            if rope:
                pool.wait_ge(padded, 1)
                for n, (_, _, _, dest) in enumerate(projections):
                    for k in range(NBLK):
                        m = n * NBLK + k
                        pool.wait_ge(rope_parts, 2 * m + 2)
                        nc.gpsimd.tensor_tensor(dest[:, 8 * k:8 * k + 8, 0:S],
                                                part_a[:, m % 2, :].rearrange("p (b s) -> p b s", b=8),
                                                part_b[:, m % 2, :].rearrange("p (b s) -> p b s", b=8),
                                                ALU.add).then_inc(proj_used, 1)
            core.wait_small(pool, L[:2])
            pool.wait_ge(proj_used, 2 * NBLK)

            def step(t, u, i):
                if has(t, 0, PAIRS):
                    wait_pos(pool, s_ready, 2 * (t - 1))
                    for b in range(2):
                        nc.gpsimd.tensor_tensor(
                            Kbd[:, u, b, :].rearrange("p (h k) -> p h k", h=H),
                            K[:, 2 * t + b, :].unsqueeze(1).to_broadcast([128, H, S]),
                            head_of_row[:].unsqueeze(2).to_broadcast([128, H, S]), ALU.mult).then_inc(kbd_ready, 1)

            in_steps(pool, 0, PAIRS, 2, PAIRS, 2, step)

        @block.tensor
        def _(pe):
            core.wait_small(pe, L[:2])
            for n, (w, ws, _, _) in enumerate(projections):
                for k in range(NBLK):
                    m = n * NBLK + k
                    if rope:
                        wait_pos(pe, rope_parts, 2 * (m - 1))
                        nc.tensor.matmul(banks[2 * (m % 2)][:, 0:BLK], W[w][:], xT[:, k * BLK:(k + 1) * BLK],
                                         start=True, stop=True)
                        nc.tensor.matmul(banks[2 * (m % 2) + 1][:, 0:BLK], W[ws][:], xT[:, k * BLK:(k + 1) * BLK],
                                         start=True, stop=True).then_inc(proj_ready, 1)
                    else:
                        wait_pos(pe, proj_used, m - 3)
                        nc.tensor.matmul(banks[m % 4][:, 0:BLK], W[w][:], xT[:, k * BLK:(k + 1) * BLK],
                                         start=True, stop=True).then_inc(proj_ready, 1)
            pe.wait_ge(proj_used, 2 * NBLK)
            pe.wait_ge(loaded, 32)
            pe.wait_ge(parts_made, 2)

            def step(t, u, i):
                v = 1 - u
                if has(t, 2, PAIRS + 2):
                    pe.wait_ge(o_moved, t - 1)
                    wait_pos(pe, ot_moved, t - 2)
                    nc.tensor.transpose(psOT[:, 0:128], O[:, u, :], core.ident[:]).then_inc(ot_ready, 1)
                if has(t, 1, PAIRS + 1):
                    for half in range(2):
                        pe.wait_ge(p_ready, 2 * t - 1 + half)
                        wait_pos(pe, t_moved, 2 * t - 3 + half)
                        for hp in range(4):
                            at = half * BLK + hp * PT
                            mm = nc.tensor.transpose(psT[0:PT, half, hp * 128:(hp + 1) * 128], P[:, v, at:at + PT],
                                                     core.ident[:])
                        mm.then_inc(t_ready, 1)
                if has(t, 0, PAIRS):
                    pe.wait_ge(xs_ready, t + 1)
                    pe.wait_ge(kbd_ready, 2 * t + 2)
                    for half in range(2):
                        wait_pos(pe, s_used, 2 * t - 1 + half)
                        for part in range(PARTS):
                            nc.tensor.matmul(psS[:, half, 0:BLK], ident_bf16[:],
                                             bias_parts[:, part, :].unsqueeze(1).to_broadcast([128, H // 2, S]),
                                             start=(part == 0), stop=False, skip_group_check=True)
                        for b in range(2):
                            mm = nc.tensor.matmul(psS[QP * b:QP * (b + 1), half, 0:BLK], q_pair[:, u, b, :],
                                                  Kbd[:, u, b, half * BLK:(half + 1) * BLK],
                                                  start=False, stop=True, skip_group_check=True)
                        mm.then_inc(s_ready, 1)
                if has(t, 2, PAIRS + 2):
                    pe.wait_ge(ot_moved, t - 1)
                    wait_pos(pe, y_used, t - 2)
                    nc.tensor.matmul(psY[0:PT, 0:128], OT[:, u, :], W["wo"][:], start=True, stop=False)
                    nc.tensor.matmul(psY[0:PT, 0:128], core.first_row[:, 0:PT], W["bo"][:],
                                     start=False, stop=True).then_inc(y_ready, 1)
                if has(t, 1, PAIRS + 1):
                    pe.wait_ge(t_moved, 2 * t)
                    pe.wait_ge(vbd_ready, t)
                    wait_pos(pe, o_moved, t - 1)
                    for b in range(2):
                        for hp in range(H // 2):
                            mm = nc.tensor.matmul(
                                psO[QP * b:QP * (b + 1), hp * 18:(hp + 1) * 18], PTr[:, hp, QP * b:QP * (b + 1)],
                                Vbd[:, v, b, 2 * hp:2 * hp + 2, :], start=True, stop=True)
                    mm.then_inc(o_ready, 1)
                if has(t, -1, PAIRS - 1):
                    pe.wait_ge(xs_ready, t + 2)
                    wait_pos(pe, vbd_ready, t + 1)
                    for b in range(2):
                        mm = nc.tensor.matmul(psV[0:PT, b * 128:(b + 1) * 128], x_twice[:, v, b, :, :], W["wv"][:],
                                              start=True, stop=True)
                    mm.then_inc(v_ready, 1)

            in_steps(pe, *steps, step)

        @block.vector
        def _(dve):
            core.wait_small(dve, L[:2])
            dve.wait_ge(loaded, 32)
            for n, (_, _, col, dest) in enumerate(projections):
                for k in range(NBLK):
                    m = n * NBLK + k
                    dve.wait_ge(proj_ready, m + 1)
                    if not rope:
                        nc.vector.tensor_copy(dest[:, 8 * k:8 * k + 8, 0:S],
                                              banks[m % 4][:, 0:BLK].rearrange("p (b s) -> p b s", b=8)).then_inc(proj_used, 1)
                        continue
                    wait_pos(dve, proj_used, m - 1)
                    for w, part, table in ((0, part_a, cos), (1, part_b, sin)):
                        nc.vector.scalar_tensor_tensor(
                            part[:, m % 2, :].rearrange("p (b s) -> p b s", b=8),
                            banks[2 * (m % 2) + w][:, 0:BLK].rearrange("p (b s) -> p b s", b=8),
                            cols[:, col + w:col + w + 1], table[:].unsqueeze(1).to_broadcast([128, 8, S]),
                            ALU.add, ALU.mult).then_inc(rope_parts, 1)

            def step(t, u, i):
                v = 1 - u
                if has(t, 0, PAIRS):
                    for half in range(2):
                        dve.wait_ge(s_ready, 2 * t + half + 1)
                        scores = psS[:, half, 0:BLK].rearrange("p (h k) -> p h k", k=S)
                        heads = top[:, u, H // 2 * half:H // 2 * (half + 1)]
                        nc.vector.tensor_reduce(heads, scores, AX.X, ALU.max).then_inc(top_ready, 1)
                        dve.wait_ge(top_ready, 2 * t + half + 1)
                        nc.vector.tensor_tensor(P[:, u, BLK * half:BLK * (half + 1)].rearrange("p (h k) -> p h k", k=S),
                                                scores, heads.unsqueeze(2).to_broadcast([128, H // 2, S]),
                                                ALU.subtract).then_inc(s_used, 1)
                if has(t, 2, PAIRS + 2):
                    dve.wait_ge(y_ready, t - 1)
                    nc.vector.tensor_tensor(x[:, t - 2, :], psY[0:PT, 0:128], x[:, t - 2, :],
                                            ALU.add).then_inc(y_used, 1)
                if has(t, 3, PAIRS + 2):
                    dve.wait_ge(y_used, t - 2)
                    nc.vector.bn_stats(core.stats[:, t - 3, :], x[:, t - 3, :])
                if has(t, 1, PAIRS + 1):
                    dve.wait_ge(o_ready, t)
                    sums = psO[:, 0:144].rearrange("p (h d) -> p h d", h=H)
                    nc.vector.reciprocal(rden[:, v, :], sums[:, :, DK]).then_inc(rden_ready, 1)
                    dve.wait_ge(rden_ready, t)
                    wait_pos(dve, ot_ready, t - 2)
                    nc.vector.tensor_tensor(O[:, v, :].rearrange("p (h d) -> p h d", h=H), sums[:, :, 0:DK],
                                            rden[:, v, :].unsqueeze(2).to_broadcast([128, H, DK]),
                                            ALU.mult).then_inc(o_moved, 1)
                if has(t, -1, PAIRS - 1):
                    dve.wait_ge(v_ready, t + 2)
                    wait_pos(dve, o_ready, t)
                    for b in range(2):
                        vbd = nc.vector.tensor_tensor(Vbd[:, v, b, :, 0:DK],
                                                     psV[0:PT, b * 128:(b + 1) * 128].rearrange("p (h d) -> p h d", h=H),
                                                     vmask[:].rearrange("p (h d) -> p h d", h=H), ALU.mult)
                    vbd.then_inc(vbd_ready, 1)

            in_steps(dve, *steps, step)

        @block.scalar
        def _(act):
            core.wait_small(act, L[:2])
            nc.scalar.copy(ident_bf16[:], core.ident[:]).then_inc(parts_made, 1)
            nc.scalar.copy(bias_parts[:], bias[:]).then_inc(parts_made, 1)
            act.wait_ge(padded, 1)
            act.wait_ge(proj_used, 2 * NBLK)

            def step(t, u, i):
                v = 1 - u
                if has(t, 2, PAIRS + 2):
                    act.wait_ge(ot_ready, t - 1)
                    wait_pos(act, y_ready, t - 2)
                    dst = OT[:, u, :].rearrange("p (b s) -> p b s", b=2)
                    src = psOT[:, 0:128].rearrange("p (b s) -> p b s", b=2)[:, :, 0:S]
                    if rope:
                        nc.scalar.activation(dst, src, ACT.Identity, bias=cols[:, 4:5]).then_inc(ot_moved, 1)
                    else:
                        nc.scalar.copy(dst, src).then_inc(ot_moved, 1)
                if has(t, 1, PAIRS + 1):
                    for half in range(2):
                        act.wait_ge(t_ready, 2 * t - 1 + half)
                        wait_pos(act, o_ready, t - 1)
                        nc.scalar.copy(PTr[:, 4 * half:4 * half + 4, :],
                                       psT[0:PT, half, :].rearrange("p (h c) -> p h c", c=128)).then_inc(t_moved, 1)
                if has(t, -1, PAIRS - 1):
                    wait_pos(act, s_ready, 2 * t)
                    wait_pos(act, v_ready, t)
                    nc.scalar.copy(q_pair[:, v, :, :], Q[:, bass.ds(2 * (t + 1), 2), :])
                    nc.scalar.copy(x_twice[:, v, :, :, :],
                                   xT[:, bass.ds(PT * (t + 1), PT)].rearrange("p (b s) -> p b s", b=2).unsqueeze(2)
                                   .to_broadcast([128, 2, 2, S])).then_inc(xs_ready, 1)
                if has(t, 0, PAIRS):
                    for half in range(2):
                        act.wait_ge(s_used, 2 * t + half + 1)
                        part = P[:, u, BLK * half:BLK * (half + 1)]
                        nc.scalar.activation(part, part, ACT.Exp, scale=HEAD_SCALE).then_inc(p_ready, 1)

            in_steps(act, *steps, step)


def units_by_chunk(plan, h):
    chunks = []
    for c in range(CHUNKS):
        others = [(kind, k) for kind, k in plan.get(c, []) if h == 0 or kind not in ("den", "y")]
        before = [unit for unit in others if unit[0] in ("den", "shift")]
        chunks.append(before + [("max", 2 * c)] + [unit for unit in others if unit not in before]
                      + [("max", 2 * c + 1)])
    return chunks


class Units:

    RING = 3
    PER_STEP = {"V": 3, "K": 3, "max": 2 * CHUNKS, "shift": 2, "den": 1, "y": 1}
    PLAN = {0: [("K", 0)], 2: [("K", 1)], 3: [("shift", 0), ("shift", 1)], 4: [("K", 2)], 5: [("den", 0)],
            6: [("V", 0)], 8: [("V", 1)], 9: [("V", 2)], 11: [("y", 0)]}
    CHUNK_UNITS = [units_by_chunk(PLAN, 0), units_by_chunk(PLAN, 1)]
    ORDER = [[unit for chunk in chunks for unit in chunk] for chunks in CHUNK_UNITS]
    PAIR = ORDER[0] + ORDER[1]
    assert len(PAIR) % RING == 0

    def __init__(self, ready, read):
        self.ready, self.read = ready, read

    @staticmethod
    def has(kind, s):
        low, high = {"V": (-1, B - 1), "K": (-3, B - 3), "max": (-2, B - 2), "shift": (-1, B - 1),
                     "den": (2, B + 1), "y": (2, B + 1)}[kind]
        return has(s, low, high)

    def bank(self, h, unit):
        return (h * len(self.ORDER[0]) + self.ORDER[h].index(unit)) % self.RING

    def count(self, kind, k, s, i):
        turn = {"V": s + 1, "K": s + 3, "max": s + 2, "shift": s + 1, "den": i - 1, "y": i - 1}[kind]
        return self.PER_STEP[kind] * turn + k + 1

    def wait_free(self, eng, s, h, i, unit):
        at = h * len(self.ORDER[0]) + self.ORDER[h].index(unit)
        back = 0
        while True:
            at -= self.RING
            if at < 0:
                at += len(self.PAIR)
                back += 1
                if isinstance(s, int) and i - back < -2:
                    return
            kind, k = self.PAIR[at]
            v = int(at >= len(self.ORDER[0]))
            before = s - h - 2 * back + v
            if self.has(kind, before):
                return wait_pos(eng, self.read[kind], self.count(kind, k, before, i - back))

    def wait_ready(self, eng, s, i, unit):
        eng.wait_ge(self.ready[unit[0]], self.count(*unit, s, i))

    def wait_read(self, eng, s, i, unit):
        eng.wait_ge(self.read[unit[0]], self.count(*unit, s, i))


def context_attention(core):
    nc, dram, x, xT = core.nc, core.dram, core.x, core.xT
    R = 32
    SLOTS = 4
    core.measured = PAIRS - 1
    with ExitStack() as ctx:
        sb, ps, sem = tools(nc, ctx)
        wq, wk, wv, bo, wo, sum_row = (core.small[f"c0_{n}"] for n in ("wq", "wk", "wv", "bo", "wo", "sum_row"))
        head_in_group = core.small["head_in_group"]
        q_hi, q_lo = sb("c0_q_hi", [128, B, HG, S], F16), sb("c0_q_lo", [128, B, HG, S], F16)
        ctxT = sb("c0_ctxT", [128, SLOTS, SK])
        k_hi, k_lo = sb("c0_k_hi", [128, 2, SK], F16), sb("c0_k_lo", [128, 2, SK], F16)
        Kst = [sb(f"c0_Kst{v}", [97, GROUPS, SK], F16) for v in range(SLOTS)]
        Qst = [sb(f"c0_Qst{v}", [97, GROUPS, HG, S], F16) for v in range(SLOTS)]
        V3 = sb("c0_V3", [CHUNK, 2, CHUNKS, GROUPS, R])
        V1 = sb("c0_V1", [CHUNK, 2, CHUNKS, GROUPS, R])
        P = sb("c0_P", [CHUNK, 3, GROUPS, GC])
        thirds = sb("c0_thirds", [PT, 8, 3])
        top = sb("c0_top", [PT, 8])
        sums = sb("c0_sums", [128, HG, 2, S])
        den = sb("c0_den", [128, HG, 2, S])
        rden = sb("c0_rden", [128, HG, 2, S])
        heads = sb("c0_heads", [128, HG, 2, S])

        psE = ps("c0_psE", [128, 2, 2, 512])
        psO = ps("c0_psO", [128, HG, S + 8])
        ring = [ps(f"c0_ring{k}", [128, 512]) for k in range(Units.RING)]

        filled = sem("c0_filled")
        q_ready, q_hi_made, q_lo_made = sem("c0_q_ready"), sem("c0_q_hi_made"), sem("c0_q_lo_made")
        ctx_loaded = [sem(f"c0_ctx_loaded{v}") for v in range(SLOTS)]
        stacked = [sem(f"c0_stacked{v}") for v in range(2)]
        rden_made = sem("c0_rden_made")
        k_hi_made, top_made = sem("c0_k_hi_made"), sem("c0_top_made")
        e_ready, p_ready, av_done, o_moved, heads_made = (sem(f"c0_{n}") for n in (
            "e_ready", "p_ready", "av_done", "o_moved", "heads_made"))
        ready = {k: sem(f"c0_{k}_ready") for k in Units.PER_STEP}
        read = {k: sem(f"c0_{k}_read") for k in Units.PER_STEP}
        units = Units(ready, read)
        block = ctx.enter_context(nc.Block())
        STACK_DMAS = 6 * GROUPS
        FILLS = SLOTS + 4
        steps = (-3, B + 1, 4, B - 4, 4)

        def wait_stacked(eng, s, h, n):
            eng.wait_ge(stacked[(h + n) % 2], 8 * STACK_DMAS * (s + n - (h + n) % 2) + 16 * STACK_DMAS)

        @block.sync
        def _(sp):
            for v in range(SLOTS):
                sp.dma_start(ctxT[:, v, :], dram["ctxT"][v]).then_inc(ctx_loaded[v], 16)

            def step(s, u, i):
                h = u % 2
                v, first = (u + 3) % SLOTS, isinstance(s, int) and s == -3

                def stack_keys():
                    units.wait_read(sp, s, i, ("K", 2))
                    for g in range(GROUPS):
                        for part, half in enumerate((k_hi, k_hi, k_lo)):
                            sp.dma_start(Kst[v][R * part:R * part + R, g, :],
                                         half[R * g:R * g + R, 1 - h, :]).then_inc(stacked[1 - h], 16)

                if first:
                    stack_keys()
                if units.has("K", s):
                    wait_pos(sp, e_ready, CHUNKS * s)
                    sp.wait_ge(q_lo_made, HG if first else NBLK * HG)
                    for g in range(GROUPS):
                        for part, half in enumerate((q_hi, q_lo, q_hi)):
                            sp.dma_start(Qst[v][R * part:R * part + R, g, :, :],
                                         half[R * g:R * g + R, s + 3, :, :]).then_inc(stacked[1 - h], 16)
                    if not first:
                        stack_keys()
                if has(s, 0, B - SLOTS):
                    sp.dma_start(ctxT[:, u, :], dram["ctxT"][s + SLOTS]).then_inc(ctx_loaded[u], 16)

            in_steps(sp, *steps, step)

        @block.gpsimd
        def _(pool):
            fills = (*((Kst[v][96:97, :, :], 1.0) for v in range(SLOTS)), (V3[:, :, :, :, 24:R], 0.0),
                     (V1[:, :, :, :, 8:R], 0.0), (V3[:, :, :, :, 24:25], 1.0), (V1[:, :, :, :, 24:25], 1.0))
            for n, (where, value) in enumerate(fills):
                wait_pos(pool, filled, n)
                nc.gpsimd.memset(where, value).then_inc(filled, 1)

        @block.tensor
        def _(pe):
            core.wait_small(pe, "c0")

            def queries():
                for k in range(NBLK):
                    wait_pos(pe, q_lo_made, HG * (k - 1))
                    nc.tensor.matmul(psE[:, 0, k % 2, 0:BLK], wq[:], xT[:, k * BLK:(k + 1) * BLK],
                                     start=True, stop=True).then_inc(q_ready, 1)
                pe.wait_ge(q_lo_made, NBLK * HG)
                pe.wait_ge(filled, FILLS)

            def values(s, u, i, k):
                h, v, unit = u % 2, (u + 1) % SLOTS, ("V", k)
                units.wait_free(pe, s, h, i, unit)
                for c in range(4):
                    at = CHUNK * (4 * k + c)
                    mm = nc.tensor.matmul(ring[units.bank(h, unit)][0:CHUNK, 128 * c:128 * c + 128],
                                          ctxT[:, v, at:at + CHUNK], wv[:], start=True, stop=True)
                mm.then_inc(ready["V"], 1)

            def keys(s, u, i, k):
                h, v, unit = u % 2, (u + 3) % SLOTS, ("K", k)
                if k == 0:
                    pe.wait_ge(ctx_loaded[v], 4 * (s + 3 - v) + 16)
                units.wait_free(pe, s, h, i, unit)
                nc.tensor.matmul(ring[units.bank(h, unit)][:, 0:THIRD], wk[:], ctxT[:, v, THIRD * k:THIRD * (k + 1)],
                                 start=True, stop=True).then_inc(ready["K"], 1)

            def maxima(s, u, i, k):
                h, v, unit = u % 2, (u + 2) % SLOTS, ("max", k)
                tile, third = k // 3, k % 3
                g, half = tile // 2, tile % 2
                if k == 0:
                    wait_stacked(pe, s, h, 2)
                units.wait_free(pe, s, h, i, unit)
                nc.tensor.matmul(ring[units.bank(h, unit)][0:PT, 0:THIRD], Qst[v][0:96, g, 2 * half:2 * half + 2, :],
                                 Kst[v][0:96, g, THIRD * third:THIRD * (third + 1)],
                                 start=True, stop=True).then_inc(ready["max"], 1)

            def shift(s, u, i, k):
                h, unit = u % 2, ("shift", k)
                if k == 0:
                    pe.wait_ge(top_made, s + 2)
                units.wait_free(pe, s, h, i, unit)
                for t in range(4):
                    mm = nc.tensor.matmul(ring[units.bank(h, unit)][96:128, PT * t:PT * (t + 1)],
                                          top[:, 4 * k + t:4 * k + t + 1].to_broadcast([PT, 32]),
                                          core.ident[0:PT, 0:PT], start=True, stop=True)
                mm.then_inc(ready["shift"], 1)

            def denominators(s, u, i, k):
                h = u % 2
                units.wait_free(pe, s, h, i, ("den", 0))
                pe.wait_ge(o_moved, s)
                nc.tensor.matmul(ring[units.bank(h, ("den", 0))][:, 0:BLK], sum_row[:], sums[:],
                                 start=True, stop=True).then_inc(ready["den"], 1)

            def output(s, u, i, k):
                h = u % 2
                units.wait_free(pe, s, h, i, ("y", 0))
                pe.wait_ge(heads_made, i)
                bank = ring[units.bank(h, ("y", 0))]
                for j in range(HG):
                    nc.tensor.matmul(bank[0:PT, 0:128], heads[:, j, :, :], wo[:, j, :], start=(j == 0), stop=False)
                nc.tensor.matmul(bank[0:PT, 0:128], core.first_row[:, 0:PT], bo[:],
                                 start=False, stop=True).then_inc(ready["y"], 1)

            def scores(s, u, i, c):
                n = CHUNKS * s + c
                if c == 0:
                    units.wait_read(pe, s - 1, i, ("shift", 1))
                wait_pos(pe, p_ready, n - 1)
                for g in range(GROUPS):
                    mm = nc.tensor.matmul(psE[0:CHUNK, c % 2, g // 2, (g % 2) * GC:(g % 2 + 1) * GC],
                                          Kst[u][:, g, CHUNK * c:CHUNK * (c + 1)], Qst[u][:, g, :, :],
                                          start=True, stop=True)
                mm.then_inc(e_ready, 1)

            def weighted_values(s, u, i, c):
                n, h = CHUNKS * s + c, u % 2
                if c == 0:
                    units.wait_read(pe, s - 1, i, ("V", 2))
                    wait_pos(pe, o_moved, s)
                pe.wait_ge(p_ready, n + 1)
                for g in range(GROUPS):
                    nc.tensor.matmul(psO[R * g:R * g + R, 0:3, 0:S], V3[:, h, c, g, :], P[:, c % 3, g, 0:3 * S],
                                     start=(c == 0), stop=(c == CHUNKS - 1), skip_group_check=True)
                for g in range(GROUPS):
                    mm = nc.tensor.matmul(psO[R * g:R * g + R, 3, 0:S], V1[:, h, c, g, :], P[:, c % 3, g, 3 * S:4 * S],
                                          start=False, stop=(c == CHUNKS - 1), skip_group_check=True)
                mm.then_inc(av_done, 1)

            make = {"V": values, "K": keys, "max": maxima, "shift": shift, "den": denominators, "y": output}

            def step(s, u, i):
                for c in range(CHUNKS):
                    if has(s, 0, B):
                        scores(s, u, i, c)
                        if c > 0:
                            weighted_values(s, u, i, c - 1)
                    for kind, k in Units.CHUNK_UNITS[u % 2][c]:
                        if units.has(kind, s):
                            make[kind](s, u, i, k)
                if has(s, 0, B):
                    weighted_values(s, u, i, CHUNKS - 1)
                if isinstance(s, int) and s == -3:
                    queries()

            in_steps(pe, *steps, step)

        @block.vector
        def _(dve):
            core.wait_small(dve, "c0")

            def queries():
                for k in range(NBLK):
                    src = psE[:, 0, k % 2, 0:BLK].rearrange("p (b q) -> p b q", q=S)
                    dve.wait_ge(q_hi_made, HG * (k + 1))
                    for j in range(HG):
                        nc.vector.scalar_tensor_tensor(q_lo[:, 8 * k:8 * k + 8, j, :], src, head_in_group[:, j:j + 1],
                                                       q_hi[:, 8 * k:8 * k + 8, j, :], ALU.mult,
                                                       ALU.subtract).then_inc(q_lo_made, 1)

            def step(s, u, i):
                h = u % 2
                if has(s, 1, B + 1):
                    dve.wait_ge(av_done, CHUNKS * s)
                    if h == 1:
                        wait_pos(dve, heads_made, i)
                    nc.vector.tensor_copy(sums[:, :, 1 - h, :], psO[:, :, 0:S]).then_inc(o_moved, 1)
                for c in range(CHUNKS):
                    for kind, k in Units.CHUNK_UNITS[h][c]:
                        if not units.has(kind, s):
                            continue
                        unit = (kind, k)
                        bank = ring[units.bank(h, unit)]
                        if kind == "K":
                            dve.wait_ge(k_hi_made, units.count("K", k, s, i))
                            at = slice(THIRD * k, THIRD * (k + 1))
                            nc.vector.tensor_tensor(k_lo[:, 1 - h, at], bank[:, 0:THIRD], k_hi[:, 1 - h, at],
                                                    ALU.subtract).then_inc(read["K"], 1)
                        elif kind == "max":
                            units.wait_ready(dve, s, i, unit)
                            if k == 0:
                                wait_pos(dve, top_made, s + 2)
                            nc.vector.tensor_reduce(thirds[:, k // 3, k % 3:k % 3 + 1], bank[0:PT, 0:THIRD], AX.X,
                                                    ALU.max).then_inc(read["max"], 1)
                        elif kind == "y":
                            units.wait_ready(dve, s, i, unit)
                            nc.vector.tensor_tensor(x[:, i - 1, :], bank[0:PT, 0:128], x[:, i - 1, :],
                                                    ALU.add).then_inc(read["y"], 1)
                            if has(s, 4, B + 1):
                                dve.wait_ge(read["y"], i - 1)
                                nc.vector.bn_stats(core.stats[:, i - 2, :], x[:, i - 2, :])
                    if h == 0 and units.has("den", s) and 5 <= c < 5 + HG:
                        j = c - 5
                        if j == 0:
                            units.wait_read(dve, s, i, ("den", 0))
                            wait_pos(dve, heads_made, i - 1)
                        nc.vector.reciprocal(rden[:, j, :, :], den[:, j, :, :]).then_inc(rden_made, 1)
                        if j == HG - 1:
                            dve.wait_ge(rden_made, HG * i)
                            dve.wait_ge(o_moved, s)
                            wait_pos(dve, ready["y"], i - 1)
                            nc.vector.tensor_tensor(heads[:], sums[:], rden[:], ALU.mult).then_inc(heads_made, 1)
                if units.has("max", s):
                    units.wait_read(dve, s, i, ("max", 2 * CHUNKS - 1))
                    wait_pos(dve, ready["shift"], 2 * (s + 2))
                    nc.vector.tensor_reduce(top[:], thirds[:], AX.X, ALU.max).then_inc(top_made, 1)
                if isinstance(s, int) and s == -3:
                    queries()

            in_steps(dve, *steps, step)

        @block.scalar
        def _(act):
            core.wait_small(act, "c0")

            def queries():
                for k in range(NBLK):
                    src = psE[:, 0, k % 2, 0:BLK].rearrange("p (b q) -> p b q", q=S)
                    act.wait_ge(q_ready, k + 1)
                    for j in range(HG):
                        nc.scalar.activation(q_hi[:, 8 * k:8 * k + 8, j, :], src, ACT.Copy,
                                             scale=head_in_group[:, j:j + 1]).then_inc(q_hi_made, 1)
                act.wait_ge(filled, FILLS)

            def move_values(s, u, i, k):
                h, unit = u % 2, ("V", k)
                units.wait_ready(act, s, i, unit)
                wait_pos(act, av_done, CHUNKS * s)
                src = ring[units.bank(h, unit)][0:CHUNK, :].rearrange("p (c g r) -> p c g r", c=4, g=GROUPS)
                nc.scalar.copy(V3[:, 1 - h, 4 * k:4 * k + 4, :, 0:24], src[:, :, :, 0:24])
                nc.scalar.copy(V1[:, 1 - h, 4 * k:4 * k + 4, :, 0:8], src[:, :, :, 24:32]).then_inc(read["V"], 1)

            def move_keys(s, u, i, k):
                h, unit = u % 2, ("K", k)
                units.wait_ready(act, s, i, unit)
                if k == 0 and has(s, -1, B):
                    wait_stacked(act, s, h, 1)
                nc.scalar.copy(k_hi[:, 1 - h, THIRD * k:THIRD * (k + 1)],
                               ring[units.bank(h, unit)][:, 0:THIRD]).then_inc(k_hi_made, 1)

            def move_shift(s, u, i, k):
                h, unit = u % 2, ("shift", k)
                units.wait_ready(act, s, i, unit)
                nc.scalar.activation(Qst[(u + 1) % SLOTS][96:97, 2 * k:2 * k + 2, :, :].rearrange("p a b c -> p (a b c)"),
                                     ring[units.bank(h, unit)][96:97, 0:BLK], ACT.Copy,
                                     scale=-1.0).then_inc(read["shift"], 1)

            def move_denominators(s, u, i, k):
                units.wait_ready(act, s, i, ("den", 0))
                wait_pos(act, heads_made, i - 1)
                nc.scalar.copy(den[:].rearrange("p a b c -> p (a b c)"),
                               ring[units.bank(u % 2, ("den", 0))][:, 0:BLK]).then_inc(read["den"], 1)

            move = {"V": move_values, "K": move_keys, "shift": move_shift, "den": move_denominators}

            def step(s, u, i):
                for c in range(CHUNKS):
                    if has(s, 0, B):
                        n = CHUNKS * s + c
                        act.wait_ge(e_ready, n + 1)
                        wait_pos(act, av_done, n - 2)
                        nc.scalar.activation(P[:, c % 3, :, :].rearrange("p (a g) n -> p a (g n)", a=2),
                                             psE[0:CHUNK, c % 2, :, 0:2 * GC], ACT.Exp,
                                             scale=HEAD_SCALE).then_inc(p_ready, 1)
                    for kind, k in Units.CHUNK_UNITS[u % 2][c]:
                        if kind in move and units.has(kind, s):
                            move[kind](s, u, i, k)
                if isinstance(s, int) and s == -3:
                    queries()

            in_steps(act, *steps, step)


E = 8
TOP2_CAPACITY = -(-2 * TOK * 5 // (E * 4))
CHOICE = TOK // E
W_SCALE = 256.0


def chain(nc, sem):
    made = [0]

    def link(instruction):
        made[0] += 1
        instruction.then_inc(sem, 1)

    def wait():
        nc.vector.wait_ge(sem, made[0])

    return link, wait


def router_logits(core, pe, w, bank, bias_row, ready):
    nc = core.nc
    for t in range(PAIRS):
        mm = nc.tensor.matmul(bank[0:PT, E * t:E * t + E], core.xT[:, PT * t:PT * (t + 1)], w[:],
                              start=True, stop=bias_row is None)
        if bias_row is not None:
            mm = nc.tensor.matmul(bank[0:PT, E * t:E * t + E], core.first_row[:, 0:PT], bias_row[:],
                                  start=False, stop=True)
    mm.then_inc(ready, 1)


def over_experts(tile):
    return tile[:].unsqueeze(2).to_broadcast([PT, PAIRS, E])


def top2_experts(core):
    nc, dram, x, xT = core.nc, core.dram, core.x, core.xT
    F = 256
    core.measured = PAIRS - 4
    with ExitStack() as ctx:
        sb, ps, sem = tools(nc, ctx)
        wg, tri, rank, ones = (core.small[n] for n in ("m0_wg", "tri", "rank", "ones"))
        w_in = sb("m0_w_in", [128, E, 2 * F])
        w_hi, w_lo = (sb(f"m0_w_{n}", [128, E, 2 * F], F16) for n in ("hi", "lo"))
        x_hi, x_lo = (sb(f"m0_x_{n}", [128, TOK], F16) for n in ("hi", "lo"))
        w_out = sb("m0_w_out", [128, E, 2, D])
        small = [PT, PAIRS, E]
        prob, work, first, second, kept = (sb(f"m0_{n}", small) for n in ("prob", "work", "first", "second", "kept"))
        gates = sb("m0_gates", small)
        col = sb("m0_col", [PT, PAIRS])
        running = [sb(f"m0_running{k}", [PT, 2 * PAIRS, E]) for k in range(2)]
        act_out = sb("m0_act_out", [128, 2, BLK])
        hidden = sb("m0_hidden", [128, 2, 2, BLK])

        psR = ps("m0_psR", [128, 512])
        psC = ps("m0_psC", [128, 512])
        psH = [ps(f"m0_psH{k}", [128, 2, 512]) for k in range(2)]
        psY = [ps(f"m0_psY{k}", [128, 512]) for k in range(2)]

        logits_ready, chained, shifted, exp_made, first_made, second_made, counted = (sem(f"m0_{n}") for n in (
            "logits_ready", "chained", "shifted", "exp_made", "first_made", "second_made", "counted"))
        h_ready, gelu_made, hidden_made, y_ready, y_added, gates_made = (sem(f"m0_{n}") for n in (
            "h_ready", "gelu_made", "hidden_made", "y_ready", "y_added", "gates_made"))
        w_in_loaded = [sem(f"m0_w_in_loaded{k}") for k in range(2)]
        w_in_scaled = sem("m0_w_in_scaled")
        w_out_loaded, x_hi_made, x_lo_made, w_hi_made, w_lo_made = (sem(f"m0_{n}") for n in (
            "w_out_loaded", "x_hi_made", "x_lo_made", "w_hi_made", "w_lo_made"))
        block = ctx.enter_context(nc.Block())

        @block.sync
        def _(sp):
            for k in range(2):
                half = slice(E // 2 * k, E // 2 * (k + 1))
                sp.dma_start(w_in[:, half], dram["m0_w_in"][:, half]).then_inc(w_in_loaded[k], 16)
            sp.dma_start(w_out[:], dram["m0_w_out"]).then_inc(w_out_loaded, 16)

        @block.gpsimd
        def _(pool):
            pool.wait_ge(x_hi_made, 1)
            nc.gpsimd.tensor_tensor(x_lo[:], xT[:], x_hi[:], ALU.subtract).then_inc(x_lo_made, 1)
            for e in range(E):
                pool.wait_ge(w_hi_made, e + 1)
                nc.gpsimd.tensor_tensor(w_lo[:, e], w_in[:, e], w_hi[:, e], ALU.subtract).then_inc(w_lo_made, 1)

        def outputs(pe, n, e):
            pe.wait_ge(hidden_made, 16 * n + 2 * e + 2)
            if e >= 2:
                pe.wait_ge(y_added, 8 * n + e - 1)
            else:
                wait_pos(pe, y_added, 8 * n)
            for t in range(4):
                for c in range(2):
                    mm = nc.tensor.matmul(psY[e % 2][0:PT, 128 * t:128 * t + 128],
                                          hidden[:, e % 2, c, PT * t:PT * (t + 1)], w_out[:, e, c, :],
                                          start=(c == 0), stop=(c == 1))
            mm.then_inc(y_ready, 1)

        @block.tensor
        def _(pe):
            core.wait_small(pe, "m0")
            router_logits(core, pe, wg, psR, None, logits_ready)
            for n, (chosen, made) in enumerate(((first, first_made), (second, second_made))):
                pe.wait_ge(made, 1)
                nc.tensor.matmul(psC[0:PT, 128 * n:128 * n + 128], tri[0:PT, 0:PT], chosen[:], start=True, stop=True)
                nc.tensor.matmul(psC[0:PT, 256 + 128 * n:384 + 128 * n], ones[:], chosen[:],
                                 start=True, stop=True).then_inc(counted, 1)
            pe.wait_ge(x_lo_made, 1)
            pe.wait_ge(w_lo_made, E)
            pe.wait_ge(w_out_loaded, 16)

            def block_of_tokens(n):
                for e in range(E):
                    for c in range(2):
                        at = 2 * e + c
                        if at >= 2:
                            pe.wait_ge(hidden_made, 16 * n + at - 1)
                        else:
                            wait_pos(pe, hidden_made, 16 * n)
                        for g in range(2):
                            for part, (w, tokens) in enumerate(((w_hi, x_hi), (w_hi, x_lo), (w_lo, x_hi))):
                                mm = nc.tensor.matmul(psH[c][:, g, 0:BLK],
                                                      w[:, e, F * g + 128 * c:F * g + 128 * (c + 1)],
                                                      tokens[:, bass.ds(BLK * n, BLK)],
                                                      start=(part == 0), stop=(part == 2))
                        mm.then_inc(h_ready, 1)
                        if c == 1 and e >= 1:
                            outputs(pe, n, e - 1)
                outputs(pe, n, E - 1)

            in_blocks(pe, NBLK, block_of_tokens)

        @block.scalar
        def _(act):
            nc.scalar.copy(x_hi[:], xT[:]).then_inc(x_hi_made, 1)
            act.wait_ge(shifted, 1)
            nc.scalar.activation(prob[:], prob[:], ACT.Exp).then_inc(exp_made, 1)
            for e in range(E):
                if e % (E // 2) == 0:
                    act.wait_ge(w_in_loaded[e // (E // 2)], 16)
                nc.scalar.activation(w_in[:, e], w_in[:, e], ACT.Copy, scale=W_SCALE).then_inc(w_in_scaled, 1)
                act.wait_ge(w_in_scaled, e + 1)
                nc.scalar.copy(w_hi[:, e], w_in[:, e]).then_inc(w_hi_made, 1)

            def block_of_tokens(n):
                for e in range(E):
                    for c in range(2):
                        at = 2 * e + c
                        act.wait_ge(h_ready, 16 * n + at + 1)
                        if at >= 2:
                            act.wait_ge(hidden_made, 16 * n + at - 1)
                        else:
                            wait_pos(act, hidden_made, 16 * n)
                        nc.scalar.activation(act_out[:, c, :], psH[c][:, 0, 0:BLK], ACT.Gelu,
                                             scale=1.0 / W_SCALE).then_inc(gelu_made, 1)

            in_blocks(act, NBLK, block_of_tokens)

        @block.vector
        def _(dve):
            link, wait = chain(nc, chained)
            vec = nc.vector
            logits = psR[0:PT, 0:128].rearrange("p (t e) -> p t e", e=E)
            counts = psC[0:PT, 0:256].rearrange("p (t e) -> p t e", e=E)
            totals = psC[0:PT, 256:512].rearrange("p (t e) -> p t e", e=E)
            ranks = rank[:].unsqueeze(1).to_broadcast([PT, PAIRS, E])
            dve.wait_ge(logits_ready, 1)
            link(vec.tensor_reduce(col[:], logits, AX.X, ALU.max))
            wait()
            vec.tensor_tensor(prob[:], logits, over_experts(col), ALU.subtract).then_inc(shifted, 1)
            dve.wait_ge(exp_made, 1)
            link(vec.tensor_reduce(col[:], prob[:], AX.X, ALU.add))
            wait()
            link(vec.reciprocal(col[:], col[:]))
            wait()
            link(vec.tensor_tensor(prob[:], prob[:], over_experts(col), ALU.mult))
            wait()
            for n, (chosen, made) in enumerate(((first, first_made), (second, second_made))):
                source = prob if n == 0 else work
                link(vec.tensor_reduce(col[:], source[:], AX.X, ALU.max))
                wait()
                link(vec.tensor_tensor(kept[:], source[:], over_experts(col), ALU.is_equal))
                wait()
                link(vec.tensor_tensor(kept[:], kept[:], ranks, ALU.mult))
                wait()
                link(vec.tensor_reduce(col[:], kept[:], AX.X, ALU.max))
                wait()
                vec.tensor_tensor(chosen[:], kept[:], over_experts(col), ALU.is_equal).then_inc(made, 1)
                dve.wait_ge(made, 1)
                if n == 0:
                    link(vec.scalar_tensor_tensor(work[:].rearrange("p t e -> p (t e)"),
                                                  first[:].rearrange("p t e -> p (t e)"), -2.0,
                                                  prob[:].rearrange("p t e -> p (t e)"), ALU.mult, ALU.add))
                    wait()
            dve.wait_ge(counted, 2)
            link(vec.memset(running[0][:, 0:1, :], 0.0))
            link(vec.tensor_copy(running[0][:, 1:, :], totals[:, 0:2 * PAIRS - 1, :]))
            wait()
            before, step = 0, 1
            while step < 2 * PAIRS:
                a, b = running[before], running[1 - before]
                link(vec.tensor_copy(b[:, 0:step, :], a[:, 0:step, :]))
                link(vec.tensor_tensor(b[:, step:, :], a[:, step:, :], a[:, 0:2 * PAIRS - step, :], ALU.add))
                wait()
                before, step = 1 - before, 2 * step
            place = running[1 - before]
            link(vec.tensor_tensor(place[:], counts, running[before][:], ALU.add))
            wait()
            link(vec.scalar_tensor_tensor(kept[:], place[:, 0:PAIRS, :], float(TOP2_CAPACITY), first[:], ALU.is_le, ALU.mult))
            link(vec.scalar_tensor_tensor(work[:], place[:, PAIRS:, :], float(TOP2_CAPACITY), second[:], ALU.is_le, ALU.mult))
            wait()
            link(vec.tensor_tensor(kept[:], kept[:], work[:], ALU.add))
            wait()
            link(vec.tensor_tensor(gates[:], prob[:], kept[:], ALU.mult))
            wait()
            link(vec.tensor_reduce(col[:], gates[:], AX.X, ALU.add))
            wait()
            link(vec.tensor_scalar(col[:], col[:], 1e-9, None, ALU.max))
            wait()
            link(vec.reciprocal(col[:], col[:]))
            wait()
            vec.tensor_tensor(gates[:], gates[:], over_experts(col), ALU.mult).then_inc(gates_made, 1)
            dve.wait_ge(gates_made, 1)

            def add_outputs(n, e):
                dve.wait_ge(y_ready, 8 * n + e + 1)
                if e >= 1:
                    dve.wait_ge(y_added, 8 * n + e)
                for t in range(4):
                    add = vec.scalar_tensor_tensor(x[:, 4 * n + t, :], psY[e % 2][0:PT, 128 * t:128 * t + 128],
                                                   gates[:, 4 * n + t, e:e + 1], x[:, 4 * n + t, :],
                                                   ALU.mult, ALU.add)
                add.then_inc(y_added, 1)

            def block_of_tokens(n):
                for e in range(E):
                    if e == 1 and has(n, 1, NBLK):
                        dve.wait_ge(y_added, 8 * n)
                        for t in range(4):
                            vec.bn_stats(core.stats[:, 4 * n - 4 + t, :], x[:, 4 * n - 4 + t, :])
                    for c in range(2):
                        dve.wait_ge(gelu_made, 16 * n + 2 * e + c + 1)
                        if e >= 2:
                            dve.wait_ge(y_ready, 8 * n + e - 1)
                        else:
                            wait_pos(dve, y_ready, 8 * n)
                        vec.scalar_tensor_tensor(hidden[:, e % 2, c, :], psH[c][:, 1, 0:BLK], 1.0 / W_SCALE,
                                                 act_out[:, c, :], ALU.mult, ALU.mult).then_inc(hidden_made, 1)
                    if e >= 1:
                        add_outputs(n, e - 1)
                add_outputs(n, E - 1)

            in_blocks(dve, NBLK, block_of_tokens)

def masked_attention(core):
    nc, dram, x, xT = core.nc, core.dram, core.x, core.xT
    scale = float(D) ** -0.5
    SLOTS = 4
    core.measured = PAIRS - 1
    with ExitStack() as ctx:
        sb, ps, sem = tools(nc, ctx)
        wq, wk, wv, bv, cols = (core.small[f"c1_{n}"] for n in ("wq", "wk", "wv", "bv", "cols"))
        Q = sb("c1_Q", [128, B, QP])
        QK = sb("c1_QK", [128, B, QP])
        q_bk = sb("c1_q_bk", [128, PAIRS])
        qk_pair = sb("c1_qk_pair", [128, 2, 2, QP])
        ctxT = sb("c1_ctxT", [128, SLOTS, 2, SK])
        rows = sb("c1_rows", [CHUNK, SLOTS, 2, CHUNKS, D])
        mask_words = sb("c1_mask", [128, SLOTS, SK // 4], I32)
        mask = mask_words[:].rearrange("p u w -> p (u w)").bitcast(U8).rearrange("p (u n) -> p u n", u=SLOTS)
        masked = sb("c1_masked", [128, SK])
        P = sb("c1_P", [128, 2, SK])
        PTr = sb("c1_PTr", [CHUNK, CHUNKS, 128])
        top, down, total, rden = (sb(f"c1_{n}", [128, 2]) for n in ("top", "down", "total", "rden"))
        O = sb("c1_O", [128, D])
        OT = sb("c1_OT", [128, 2, S])

        psS = ps("c1_psS", [128, 3, 512])
        psT = ps("c1_psT", [128, 3, 512])
        psO = ps("c1_psO", [128, 512])
        psY = ps("c1_psY", [128, 512])

        filled, q_ready, q_made, qk_ready, qk_made, b_ready, b_made = (sem(f"c1_{n}") for n in (
            "filled", "q_ready", "q_made", "qk_ready", "qk_made", "b_ready", "b_made"))
        ctx_loaded, rows_loaded, mask_loaded = ([sem(f"c1_{n}_loaded{v}") for v in range(SLOTS)]
                                                for n in ("ctx", "rows", "mask"))
        pair_ready, down_cleared, s_ready, s_moved, s_masked, top_made, down_made, p_made, rden_made = (sem(f"c1_{n}") for n in (
            "pair_ready", "down_cleared", "s_ready", "s_moved", "s_masked", "top_made", "down_made", "p_made", "rden_made"))
        t_ready, t_moved, o_ready, o_moved, ot_ready, ot_moved, y_ready, y_added = (sem(f"c1_{n}") for n in (
            "t_ready", "t_moved", "o_ready", "o_moved", "ot_ready", "ot_moved", "y_ready", "y_added"))
        block = ctx.enter_context(nc.Block())
        loop = (4, PAIRS, SLOTS)

        @block.sync
        def _(sp):
            def step(t, u, i):
                wait_pos(sp, s_ready, t - 3)
                for b in range(2):
                    sp.dma_start(ctxT[:, u, b, :], dram["ctxT"][2 * t + b]).then_inc(ctx_loaded[u], 16)
                if isinstance(t, int) and t == 0:
                    sp.wait_ge(filled, 1)
                wait_pos(sp, s_masked, t - 3)
                for b in range(2):
                    sp.dma_start(mask_words[QP * b:QP * b + S, u, :], dram["mask"][2 * t + b]).then_inc(mask_loaded[u], 16)
                wait_pos(sp, o_ready, t - 3)
                for b in range(2):
                    sp.dma_start(rows[:, u, b, :, :],
                                 dram["ctx"][2 * t + b].rearrange("(p c) d -> p c d", c=CHUNKS)).then_inc(rows_loaded[u], 16)

            in_steps(sp, 0, PAIRS, *loop, step)

        @block.gpsimd
        def _(pool):
            nc.gpsimd.memset(mask_words[:], 0).then_inc(filled, 1)
            pool.wait_ge(filled, 1)
            nc.gpsimd.memset(Q[:, :, S:QP], 0.0).then_inc(filled, 1)
            pool.wait_ge(filled, 2)
            nc.gpsimd.memset(masked[:], NEG / scale).then_inc(filled, 1)
            pool.wait_ge(qk_made, NBLK)

            def step(t, u, i):
                wait_pos(pool, s_ready, t - 1)
                nc.gpsimd.tensor_copy(qk_pair[:, u % 2, :, :], QK[:, bass.ds(2 * t, 2), :]).then_inc(pair_ready, 1)

            in_steps(pool, 0, PAIRS, *loop, step)

        @block.tensor
        def _(pe):
            core.wait_small(pe, "c1")
            pe.wait_ge(filled, 3)
            for k in range(NBLK):
                nc.tensor.matmul(psS[:, k, 0:BLK] if k < 3 else psO[:, 0:BLK], wq[:], xT[:, k * BLK:(k + 1) * BLK],
                                 start=True, stop=True).then_inc(q_ready, 1)
            for k in range(NBLK):
                pe.wait_ge(q_made, k + 1)
                nc.tensor.matmul(psT[:, k, :] if k < 3 else psY[:, :], wk[:], Q[:, 8 * k:8 * k + 8, :],
                                 start=True, stop=True).then_inc(qk_ready, 1)
            for t in range(PAIRS):
                mm = nc.tensor.matmul(psO[:, t:t + 1], Q[:, 2 * t:2 * t + 2, :], cols[:, 1:2], start=True, stop=True)
            mm.then_inc(b_ready, 1)
            pe.wait_ge(qk_made, NBLK)
            pe.wait_ge(b_made, 1)

            def step(t, u, i):
                h, v = u % 2, (u - 1) % SLOTS
                if has(t, 0, PAIRS):
                    pe.wait_ge(ctx_loaded[u], 8 * (t - u) + 32)
                    pe.wait_ge(pair_ready, t + 1)
                    wait_pos(pe, s_moved, t)
                    for b in range(2):
                        for k in range(3):
                            mm = nc.tensor.matmul(psS[QP * b:QP * (b + 1), k, 0:THIRD], qk_pair[:, h, b, :],
                                                  ctxT[:, u, b, THIRD * k:THIRD * (k + 1)], start=True, stop=True)
                    mm.then_inc(s_ready, 1)
                if has(t, 2, PAIRS + 2):
                    pe.wait_ge(o_moved, t - 1)
                    wait_pos(pe, y_added, t - 2)
                    nc.tensor.transpose(psY[:, 128:256], O[:], core.ident[:]).then_inc(ot_ready, 1)
                if has(t, 1, PAIRS + 1):
                    pe.wait_ge(p_made, t)
                    for k in range(3):
                        wait_pos(pe, t_moved, 3 * (t - 2) + k + 1)
                        for c in range(4 * k, 4 * k + 4):
                            mm = nc.tensor.transpose(psT[0:CHUNK, k, (c % 4) * 128:(c % 4 + 1) * 128],
                                                     P[:, 1 - h, c:SK:CHUNKS], core.ident[:])
                        mm.then_inc(t_ready, 1)
                if has(t, 2, PAIRS + 2):
                    pe.wait_ge(ot_moved, t - 1)
                    nc.tensor.matmul(psY[0:PT, 0:128], OT[:], wv[:], start=True, stop=False)
                    nc.tensor.matmul(psY[0:PT, 0:128], core.first_row[:, 0:PT], bv[:],
                                     start=False, stop=True).then_inc(y_ready, 1)
                if has(t, 1, PAIRS + 1):
                    pe.wait_ge(rows_loaded[v], 8 * (t - 1 - v) + 32)
                    wait_pos(pe, o_moved, t - 1)
                    for c in range(CHUNKS):
                        if c % 4 == 0:
                            pe.wait_ge(t_moved, 3 * (t - 1) + c // 4 + 1)
                        for b in range(2):
                            mm = nc.tensor.matmul(psO[QP * b:QP * (b + 1), 0:D], PTr[:, c, QP * b:QP * (b + 1)],
                                                  rows[:, v, b, c, :], start=(c == 0),
                                                  stop=(c == CHUNKS - 1), skip_group_check=True)
                    mm.then_inc(o_ready, 1)

            in_steps(pe, 0, PAIRS + 2, *loop, step)

        @block.vector
        def _(dve):
            dve.wait_ge(filled, 2)
            core.wait_small(dve, "c1")
            for k in range(NBLK):
                dve.wait_ge(q_ready, k + 1)
                src = psS[:, k, 0:BLK] if k < 3 else psO[:, 0:BLK]
                nc.vector.tensor_scalar(Q[:, 8 * k:8 * k + 8, 0:S], src.rearrange("p (b s) -> p b s", s=S),
                                        cols[:, 0:1], None, ALU.add).then_inc(q_made, 1)
            for k in range(NBLK):
                dve.wait_ge(qk_ready, k + 1)
                nc.vector.tensor_copy(QK[:, 8 * k:8 * k + 8, :].rearrange("p b s -> p (b s)"),
                                      psT[:, k, :] if k < 3 else psY[:, :]).then_inc(qk_made, 1)
            dve.wait_ge(b_ready, 1)
            nc.vector.tensor_copy(q_bk[:], psO[:, 0:PAIRS]).then_inc(b_made, 1)
            dve.wait_ge(filled, 3)

            def step(t, u, i):
                h = u % 2
                if has(t, 0, PAIRS):
                    dve.wait_ge(mask_loaded[u], 8 * (t - u) + 32)
                    dve.wait_ge(s_moved, t + 1)
                    wait_pos(dve, p_made, t - 1)
                    nc.vector.memset(down[:, h:h + 1], 0.0).then_inc(down_cleared, 1)
                    nc.vector.copy_predicated(P[:, h, :], mask[:, u, :], masked[:]).then_inc(s_masked, 1)
                    dve.wait_ge(s_masked, t + 1)
                    wait_pos(dve, down_made, t - 1)
                    nc.vector.tensor_reduce(top[:, h:h + 1], P[:, h, :], AX.X, ALU.max).then_inc(top_made, 1)
                    dve.wait_ge(top_made, t + 1)
                    dve.wait_ge(down_cleared, t + 1)
                    nc.vector.tensor_scalar(down[:, h:h + 1], top[:, h:h + 1], -scale, None, ALU.mult).then_inc(down_made, 1)
                if has(t, 2, PAIRS + 2):
                    dve.wait_ge(y_ready, t - 1)
                    nc.vector.tensor_tensor(x[:, t - 2, :], psY[0:PT, 0:128], x[:, t - 2, :], ALU.add).then_inc(y_added, 1)
                if has(t, 3, PAIRS + 2):
                    dve.wait_ge(y_added, t - 2)
                    nc.vector.bn_stats(core.stats[:, t - 3, :], x[:, t - 3, :])
                if has(t, 1, PAIRS + 1):
                    dve.wait_ge(p_made, t)
                    nc.vector.reciprocal(rden[:, 1 - h:2 - h], total[:, 1 - h:2 - h]).then_inc(rden_made, 1)
                    dve.wait_ge(rden_made, t)
                    dve.wait_ge(o_ready, t)
                    wait_pos(dve, ot_ready, t - 1)
                    nc.vector.tensor_scalar(O[:], psO[:, 0:D], rden[:, 1 - h:2 - h], None, ALU.mult).then_inc(o_moved, 1)

            in_steps(dve, 0, PAIRS + 2, *loop, step)

        @block.scalar
        def _(act):
            act.wait_ge(b_made, 1)

            def step(t, u, i):
                h = u % 2
                if has(t, 0, PAIRS):
                    act.wait_ge(s_ready, t + 1)
                    wait_pos(act, t_ready, 3 * (t - 1))
                    nc.scalar.activation(P[:, h, :].rearrange("p (a n) -> p a n", a=3), psS[:, :, 0:THIRD], ACT.Identity,
                                         bias=q_bk[:, bass.ds(t, 1)]).then_inc(s_moved, 1)
                if has(t, 2, PAIRS + 2):
                    act.wait_ge(ot_ready, t - 1)
                    wait_pos(act, y_ready, t - 2)
                    nc.scalar.copy(OT[:], psY[:, 128:256].rearrange("p (b s) -> p b s", b=2)[:, :, 0:S]).then_inc(ot_moved, 1)
                if has(t, 1, PAIRS + 1):
                    wait_pos(act, o_ready, t - 1)
                    for k in range(3):
                        act.wait_ge(t_ready, 3 * (t - 1) + k + 1)
                        nc.scalar.copy(PTr[:, 4 * k:4 * k + 4, :].rearrange("p c q -> p (c q)"),
                                       psT[0:CHUNK, k, :]).then_inc(t_moved, 1)
                if has(t, 0, PAIRS):
                    act.wait_ge(down_made, t + 1)
                    wait_pos(act, rden_made, t - 1)
                    nc.scalar.activation(P[:, h, :], P[:, h, :], ACT.Exp, bias=down[:, h:h + 1], scale=scale,
                                         accum_out=total[:, h:h + 1]).then_inc(p_made, 1)

            in_steps(act, 0, PAIRS + 2, *loop, step)


def choosing_experts(core):
    nc, dram, x, xT = core.nc, core.dram, core.x, core.xT
    FC = 4
    BITS, AT_ONCE = 30, 3
    ROUNDS, TRIALS = BITS // AT_ONCE, 2 ** AT_ONCE - 1
    core.measured = PAIRS - 4
    with ExitStack() as ctx:
        sb, ps, sem = tools(nc, ctx)
        ws, bs, b1 = (core.small[f"m1_{n}"] for n in ("ws", "bs", "b1"))
        w1 = sb("m1_w1", [128, E, FC, 128])
        w1_hi, w1_lo = (sb(f"m1_w1_{n}", [128, E, FC, 128], F16) for n in ("hi", "lo"))
        x_hi, x_lo = (sb(f"m1_x_{n}", [128, TOK], F16) for n in ("hi", "lo"))
        w2 = sb("m1_w2", [128, E, FC, D])
        b2 = sb("m1_b2", [128, PAIRS, D])
        same, before = core.small["same"], core.small["before"]
        prob = sb("m1_prob", [PT, PAIRS, E])
        col = sb("m1_col", [PT, PAIRS])
        pT = sb("m1_pT", [128, PT])
        marks = sb("m1_marks", [128, TRIALS, PT])
        equal = sb("m1_equal", [128, PT])
        count = sb("m1_count", [128, TRIALS])
        equals = sb("m1_equals", [128, 1])
        room = sb("m1_room", [128, 1])
        prefix, most = (sb(f"m1_{n}", [128, 1], I32) for n in ("prefix", "most"))
        trial = core.small["m1_trial"]
        tried, taken = (sb(f"m1_{n}", [128, TRIALS], I32) for n in ("tried", "taken"))
        gatesT = sb("m1_gatesT", [128, PT])
        gates = sb("m1_gates", [PT, PAIRS, E])
        hidden = sb("m1_hidden", [128, E, FC, BLK])

        psR = ps("m1_psR", [128, 512])
        psH = [ps(f"m1_psH{k}", [128, 512]) for k in range(4)]
        psY = [ps(f"m1_psY{k}", [128, 512]) for k in range(2)]

        logits_ready, chained, shifted, exp_made, prob_made, pT_ready = (sem(f"m1_{n}") for n in (
            "logits_ready", "chained", "shifted", "exp_made", "prob_made", "pT_ready"))
        w1_loaded = [sem(f"m1_w1_loaded{k}") for k in range(2)]
        w1_scaled = sem("m1_w1_scaled")
        w2_loaded, b2_loaded, x_hi_made, x_lo_made, w1_hi_made, w1_lo_made = (sem(f"m1_{n}") for n in (
            "w2_loaded", "b2_loaded", "x_hi_made", "x_lo_made", "w1_hi_made", "w1_lo_made"))
        tried_made, counted, count_ready, taken_made, most_made, prefix_made, trial_made = (sem(f"m1_{n}") for n in (
            "tried_made", "counted", "count_ready", "taken_made", "most_made", "prefix_made", "trial_made"))
        asked, answered, gatesT_made, gates_ready, gates_made, b2_ready, b2_added = (sem(f"m1_{n}") for n in (
            "asked", "answered", "gatesT_made", "gates_ready", "gates_made", "b2_ready", "b2_added"))
        h_ready, gelu_made, y_ready, y_added = (sem(f"m1_{n}") for n in ("h_ready", "gelu_made", "y_ready", "y_added"))
        block = ctx.enter_context(nc.Block())
        @block.sync
        def _(sp):
            for k in range(2):
                half = slice(E // 2 * k, E // 2 * (k + 1))
                sp.dma_start(w1[:, half], dram["m1_w1"][:, half]).then_inc(w1_loaded[k], 16)
            sp.dma_start(b2[:], dram["m1_b2"]).then_inc(b2_loaded, 16)
            sp.dma_start(w2[:], dram["m1_w2"]).then_inc(w2_loaded, 16)

        @block.gpsimd
        def _(pool):
            pool.wait_ge(x_hi_made, 1)
            nc.gpsimd.tensor_tensor(x_lo[:], xT[:], x_hi[:], ALU.subtract).then_inc(x_lo_made, 1)
            for e in range(E):
                pool.wait_ge(w1_hi_made, e + 1)
                nc.gpsimd.tensor_tensor(w1_lo[:, e], w1[:, e], w1_hi[:, e], ALU.subtract).then_inc(w1_lo_made, 1)

        @block.tensor
        def _(pe):
            def hidden_of(n, e):
                for c in range(FC):
                    unit = FC * (E * n + e) + c
                    wait_pos(pe, gelu_made, unit - FC + 1)
                    for part, (w, tokens) in enumerate(((w1_hi, x_hi), (w1_hi, x_lo), (w1_lo, x_hi))):
                        mm = nc.tensor.matmul(psH[c][:, 0:BLK], w[:, e, c, :], tokens[:, bass.ds(BLK * n, BLK)],
                                              start=(part == 0), stop=(part == 2))
                    mm.then_inc(h_ready, 1)

            def outputs(n, e):
                pe.wait_ge(gelu_made, FC * (E * n + e + 1))
                wait_pos(pe, y_added, E * n + e - 1)
                for t in range(4):
                    for c in range(FC):
                        mm = nc.tensor.matmul(psY[e % 2][0:PT, 128 * t:128 * t + 128],
                                              hidden[:, e, c, PT * t:PT * (t + 1)], w2[:, e, c, :],
                                              start=(c == 0), stop=(c == FC - 1))
                mm.then_inc(y_ready, 1)

            core.wait_small(pe, "m1")
            router_logits(core, pe, ws, psR, bs, logits_ready)
            pe.wait_ge(prob_made, 1)
            nc.tensor.transpose(psR[:, 128:128 + PT], prob[:].rearrange("p t e -> p (t e)"),
                                core.ident[0:PT, 0:PT]).then_inc(pT_ready, 1)
            pe.wait_ge(x_lo_made, 1)
            for n in range(ROUNDS):
                pe.wait_ge(counted, n + 1)
                nc.tensor.matmul(psR[:, 256:256 + TRIALS], same[:], count[:], start=True, stop=True).then_inc(count_ready, 1)
                if 1 <= n <= E:
                    pe.wait_ge(w1_lo_made, n)
                    hidden_of(0, n - 1)
            pe.wait_ge(asked, 1)
            nc.tensor.matmul(psR[:, 264:265], same[:], count[:, 0:1], start=True, stop=True)
            nc.tensor.matmul(psR[:, 265:266], before[:], equals[:], start=True, stop=True).then_inc(answered, 1)
            pe.wait_ge(gatesT_made, 1)
            nc.tensor.transpose(psR[0:PT, 384:512], gatesT[:], core.ident[:]).then_inc(gates_ready, 1)
            pe.wait_ge(b2_loaded, 16)
            for k in range(4):
                wait_pos(pe, b2_added, k - 1)
                for t in range(4):
                    mm = nc.tensor.matmul(psY[k % 2][0:PT, 128 * t:128 * t + 128], gatesT[:], b2[:, 4 * k + t, :],
                                          start=True, stop=True)
                mm.then_inc(b2_ready, 1)
            pe.wait_ge(w2_loaded, 16)
            pe.wait_ge(b2_added, 4)

            def block_of_tokens(n):
                for e in range(E):
                    outputs(n, e)
                    hidden_of(n + 1, e)

            in_blocks(pe, NBLK - 1, block_of_tokens)
            for e in range(E):
                outputs(NBLK - 1, e)

        @block.scalar
        def _(act):
            nc.scalar.copy(x_hi[:], xT[:]).then_inc(x_hi_made, 1)
            act.wait_ge(shifted, 1)
            nc.scalar.activation(prob[:], prob[:], ACT.Exp).then_inc(exp_made, 1)
            for e in range(E):
                if e % (E // 2) == 0:
                    act.wait_ge(w1_loaded[e // (E // 2)], 16)
                nc.scalar.activation(w1[:, e], w1[:, e], ACT.Copy, scale=W_SCALE).then_inc(w1_scaled, 1)
                act.wait_ge(w1_scaled, e + 1)
                nc.scalar.copy(w1_hi[:, e], w1[:, e]).then_inc(w1_hi_made, 1)

            def block_of_tokens(n):
                for e in range(E):
                    wait_pos(act, y_ready, E * (n - 1) + e + 1)
                    for c in range(FC):
                        act.wait_ge(h_ready, FC * (E * n + e) + c + 1)
                        nc.scalar.activation(hidden[:, e, c, :], psH[c][:, 0:BLK], ACT.Gelu_apprx_tanh,
                                             bias=b1[:, e, c:c + 1], scale=1.0 / W_SCALE).then_inc(gelu_made, 1)

            in_blocks(act, NBLK, block_of_tokens)

        @block.vector
        def _(dve):
            link, wait = chain(nc, chained)
            vec = nc.vector
            logits = psR[0:PT, 0:128].rearrange("p (t e) -> p t e", e=E)
            link(vec.memset(prefix[:], 0))
            dve.wait_ge(logits_ready, 1)
            link(vec.tensor_reduce(col[:], logits, AX.X, ALU.max))
            wait()
            vec.tensor_tensor(prob[:], logits, over_experts(col), ALU.subtract).then_inc(shifted, 1)
            dve.wait_ge(exp_made, 1)
            link(vec.tensor_reduce(col[:], prob[:], AX.X, ALU.add))
            wait()
            link(vec.reciprocal(col[:], col[:]))
            wait()
            vec.tensor_tensor(prob[:], prob[:], over_experts(col), ALU.mult).then_inc(prob_made, 1)
            dve.wait_ge(pT_ready, 1)
            link(vec.tensor_copy(pT[:], psR[:, 128:128 + PT]))
            wait()
            def test_bits(n):
                wait_pos(dve, prefix_made, n)
                wait_pos(dve, trial_made, n)
                vec.tensor_tensor(tried[:], trial[:], prefix[:].to_broadcast([128, TRIALS]),
                                  ALU.bitwise_or).then_inc(tried_made, 1)
                dve.wait_ge(tried_made, n + 1)
                for k in range(TRIALS):
                    mark = vec.tensor_scalar(marks[:, k, :], pT[:], tried[:, k:k + 1].bitcast(F32), 0.0,
                                             ALU.is_ge, ALU.add, accum_out=count[:, k:k + 1])
                mark.then_inc(counted, 1)
                dve.wait_ge(count_ready, n + 1)
                vec.scalar_tensor_tensor(taken[:], psR[:, 256:256 + TRIALS], float(CHOICE), trial[:], ALU.is_ge,
                                         ALU.mult).then_inc(taken_made, 1)
                dve.wait_ge(taken_made, n + 1)
                vec.tensor_reduce(most[:], taken[:], AX.X, ALU.max).then_inc(most_made, 1)
                vec.tensor_scalar(trial[:], trial[:], AT_ONCE, None, ALU.logical_shift_right).then_inc(trial_made, 1)
                dve.wait_ge(most_made, n + 1)
                vec.tensor_tensor(prefix[:], prefix[:], most[:], ALU.bitwise_or).then_inc(prefix_made, 1)

            in_blocks(dve, ROUNDS, test_bits)
            dve.wait_ge(prefix_made, ROUNDS)
            threshold = prefix[:].bitcast(F32)
            chosen, order = marks[:, 0, :], marks[:, 1, :]
            link(vec.tensor_scalar(chosen, pT[:], threshold, 0.0, ALU.is_gt, ALU.add, accum_out=count[:, 0:1]))
            wait()
            vec.tensor_scalar(equal[:], pT[:], threshold, 0.0, ALU.is_equal, ALU.add,
                              accum_out=equals[:]).then_inc(asked, 1)
            dve.wait_ge(asked, 1)
            link(vec.tensor_tensor_scan(order, equal[:], equal[:], 0.0, ALU.add, ALU.max))
            dve.wait_ge(answered, 1)
            link(vec.tensor_scalar(room[:], psR[:, 264:265], -1.0, float(CHOICE), ALU.mult, ALU.add))
            wait()
            link(vec.tensor_scalar(order, order, psR[:, 265:266], None, ALU.add))
            wait()
            link(vec.scalar_tensor_tensor(order, order, room[:], equal[:], ALU.is_le, ALU.mult))
            wait()
            link(vec.tensor_tensor(chosen, chosen, order, ALU.add))
            wait()
            vec.tensor_tensor(gatesT[:], chosen, pT[:], ALU.mult).then_inc(gatesT_made, 1)
            dve.wait_ge(gates_ready, 1)
            vec.tensor_copy(gates[:].rearrange("p t e -> p (t e)"), psR[0:PT, 384:512]).then_inc(gates_made, 1)
            for k in range(4):
                dve.wait_ge(b2_ready, k + 1)
                rows = x[:, 4 * k:4 * k + 4, :].rearrange("p t d -> p (t d)")
                vec.tensor_tensor(rows, psY[k % 2][0:PT, :], rows, ALU.add).then_inc(b2_added, 1)
            dve.wait_ge(b2_added, 4)
            dve.wait_ge(gates_made, 1)

            def block_of_tokens(n):
                if has(n, 1, NBLK):
                    dve.wait_ge(y_added, 8 * n)
                    for t in range(4):
                        vec.bn_stats(core.stats[:, 4 * n - 4 + t, :], x[:, 4 * n - 4 + t, :])
                for e in range(E):
                    dve.wait_ge(y_ready, 8 * n + e + 1)
                    if e >= 1:
                        dve.wait_ge(y_added, 8 * n + e)
                    for t in range(4):
                        add = vec.scalar_tensor_tensor(x[:, 4 * n + t, :], psY[e % 2][0:PT, 128 * t:128 * t + 128],
                                                       gates[:, 4 * n + t, e:e + 1], x[:, 4 * n + t, :],
                                                       ALU.mult, ALU.add)
                    add.then_inc(y_added, 1)

            in_blocks(dve, NBLK, block_of_tokens)

def program(nc, dram, out):
    with ExitStack() as ctx:
        sb, ps, sem = tools(nc, ctx)
        core = Core(nc, dram)
        core.x = sb("x", [PT, PAIRS, D])
        core.xT = sb("xT", [128, TOK])
        core.stats = sb("stats", [PT, PAIRS, 6])
        core.ident = sb("ident", [128, 128])
        core.first_row = sb("first_row", [128, 128])
        for stage, names in SMALL.items():
            core.small_loaded[stage] = sem(f"{stage}_small_loaded")
            for name in names:
                if name not in core.small:
                    core.small[name] = sb(name, list(dram[name].shape), dram[name].dtype)
        load_inputs(core)
        self_attention(core, 0)
        layer_norm(core, "n0")
        context_attention(core)
        layer_norm(core, "n1")
        top2_experts(core)
        layer_norm(core, "n2")
        self_attention(core, 1)
        layer_norm(core, "n3")
        masked_attention(core)
        layer_norm(core, "n4")
        choosing_experts(core)
        layer_norm(core, "n5", out)




def shape_tables():
    f = np.float32
    p = np.arange(128)
    t = {"ident": np.eye(128, dtype=f), "first_row": np.zeros((128, 128), f)}
    t["first_row"][0] = 1.0
    t["head_of_row"] = (p[:, None] // DK == np.arange(H)[None]).astype(f)
    two = np.arange(PT)[:, None] // S
    t["vmask"] = ((p[None] // DK) % 2 == two).astype(f)
    ones = np.zeros((PT, 2, H, DK + 1), f)
    ones[:, :, :, DK] = (np.arange(H)[None, None] % 2 == two[:, :, None])
    t["vbd_ones"] = ones
    inv = (f(1.0) / f(10000.0) ** (np.arange(0, DK, 2, dtype=f) / f(DK))).astype(f)
    ang = np.arange(S, dtype=f)[:, None] * inv
    at = (p % DK) // 2
    t["rope_cos"] = np.cos(ang).astype(f).T[at]
    t["rope_sin"] = np.sin(ang).astype(f).T[at] * np.where(p % 2 == 0, -1, 1).astype(f)[:, None]
    causal = np.where(np.tril(np.ones((S, S), bool)), f(0), f(NEG))
    phi = (1.0 + np.sqrt(5.0)) / 2.0
    pos = (np.arange(S, dtype=f) * f(phi)) % f(1.0)
    dist = np.abs(pos[:, None] - pos[None, :])
    table = np.log(np.exp(-dist) + f(1e-8)) / f(HEAD_SCALE)
    for n, a in (("s0_bias", causal), ("s1_bias", table)):
        padded = np.zeros((2, QP, S), f)
        padded[:, :S] = a
        parts = []
        for _ in range(1 if n == "s0_bias" else 3):
            parts.append((padded.view(np.uint32) & np.uint32(0xffff0000)).view(f))
            padded = padded - parts[-1]
        t[n] = np.stack(parts, axis=2).reshape(128, len(parts), S)
    t["head_in_group"] = ((p[:, None] // DK) % HG == np.arange(HG)[None]).astype(f)
    t["tri"] = np.triu(np.ones((128, 128), f))
    t["ones"] = np.ones((PT, PT), f)
    t["rank"] = np.broadcast_to(E - np.arange(E, dtype=f), (PT, E))
    expert, pair = p % E, p // E
    t["same"] = (expert[:, None] == expert[None]).astype(f)
    t["before"] = t["same"] * (pair[:, None] < pair[None])
    t["m1_trial"] = np.broadcast_to(np.arange(1, 8, dtype=np.int32) << 27, (128, 7))
    t["c0_sum_row"] = (p[:, None] == (p // 32 * 32 + 24)[None]).astype(f)
    return t


def laid_out(i):
    f = np.float32
    swap = np.arange(128) ^ 1

    def row(v):
        out = np.zeros((128, 128), f)
        out[0] = v
        return out

    a = {"x": i["x"].reshape(TOK, D), "xT": i["x"].reshape(TOK, D).T}
    a["s0_wq"], a["s0_wk"], a["s0_wv"], a["s0_wo"] = (i[f"L0_attn_W{n}"].T for n in "qkvo")
    a["s0_wqs"], a["s0_wks"] = a["s0_wq"][:, swap], a["s0_wk"][:, swap]
    a["s0_bo"] = row(i["L0_attn_bo"])
    a["s0_cols"] = np.stack([i["L0_attn_bq"], i["L0_attn_bq"][swap], i["L0_attn_bk"], i["L0_attn_bk"][swap],
                             i["L0_attn_bv"]], axis=1)
    a["ctxT"] = i["ctx_1024"].transpose(0, 2, 1)
    a["c0_wq"], a["c0_wk"], a["c0_wv"] = (i[f"L0_xattn_W_{n}"].transpose(1, 0, 2).reshape(128, 128) for n in "qkv")
    wo = i["L0_xattn_W_o"].T.reshape(GROUPS, HG, DK, 128)
    padded = np.zeros((GROUPS, 32, HG, 128), f)
    for j in range(HG):
        at = DK * j if j < 3 else 0
        padded[:, at:at + DK, j, :] = wo[:, j]
    a["c0_wo"] = padded.reshape(128, HG, 128)
    a["c0_bo"] = row(i["L0_xattn_b_o"])
    a["m0_wg"] = i["L0_ffn_Wg"]
    a["m0_w_in"] = i["L0_ffn_W_in"].transpose(1, 0, 2)
    a["m0_w_out"] = i["L0_ffn_W_out"].reshape(E, 2, 128, D).transpose(2, 0, 1, 3)
    a["s1_wq"], a["s1_wk"], a["s1_wv"] = (i["L1_attn_w_qkv"][:, 128 * n:128 * n + 128] for n in range(3))
    a["s1_wo"], a["s1_bo"] = i["L1_attn_w_proj"], row(i["L1_attn_b_proj"])
    a["ctx"] = i["ctx_1024"]
    a["mask"] = i["mask_BxSxS2_bk1"].view(np.int32)
    a["c1_wq"], a["c1_wk"], a["c1_wv"] = i["L1_xattn_Wq"].T, i["L1_xattn_Wk"], i["L1_xattn_Wv"].T
    a["c1_bv"] = row(i["L1_xattn_bv"])
    a["c1_cols"] = np.stack([i["L1_xattn_bq"], i["L1_xattn_bk"]], axis=1)
    a["m1_ws"] = i["L1_ffn_Ws"]
    a["m1_bs"] = row8 = np.zeros((128, E), f)
    row8[0] = i["L1_ffn_bs"]
    a["m1_b1"] = i["L1_ffn_b1"].reshape(E, 4, 128).transpose(2, 0, 1)
    a["m1_w1"] = i["L1_ffn_W1"].reshape(E, D, 4, 128).transpose(1, 0, 2, 3)
    a["m1_w2"] = i["L1_ffn_W2"].reshape(E, 4, 128, D).transpose(2, 0, 1, 3)
    b2 = np.zeros((PAIRS, E, PAIRS, D), f)
    for t in range(PAIRS):
        b2[t, :, t] = i["L1_ffn_b2"]
    a["m1_b2"] = b2.reshape(128, PAIRS, D)
    return a


def kernel(**inputs):
    import concourse.bacc as bacc
    from concourse.bass_utils import run_bass_kernel_spmd

    inputs = {k: np.asarray(v) for k, v in inputs.items()}
    arrays = {f"in_{k}": np.ascontiguousarray(v) for k, v in {**laid_out(inputs), **shape_tables()}.items()}
    nc = bacc.Bacc("TRN2", target_bir_lowering=False, num_devices=1)
    dram = {k[3:]: nc.dram_tensor(k, v.shape, mybir.dt.from_np(v.dtype), kind="ExternalInput").ap()
            for k, v in arrays.items()}
    out = nc.dram_tensor("out", (TOK, D), F32, kind="ExternalOutput").ap()
    program(nc, dram, out)
    result = run_bass_kernel_spmd(nc, [arrays], core_ids=[0])
    return result.results[0]["out"].reshape(B, S, D)
```
